# Optimizing a Trainium2 kernel written in Bass

```python
import numpy as np
import jax
import jax.numpy as jnp

def _softmax(x, axis=-1):
    return jax.nn.softmax(x, axis=axis)

def _gelu(x):
    return jax.nn.gelu(x, approximate=True)

def _silu(x):
    return jax.nn.silu(x)

def _sigmoid(x):
    return jax.nn.sigmoid(x)

def _layernorm(x, axis=-1, eps=1e-05):
    m = jnp.mean(x, axis=axis, keepdims=True)
    v = jnp.var(x, axis=axis, keepdims=True)
    return (x - m) / jnp.sqrt(v + eps)

def _scatter_add(tgt, idx, src, axis=0):
    return tgt.at[idx].add(src)

def _segment_sum(src, seg, n):
    return jax.ops.segment_sum(src, seg, n)
kernel_name = 'mk_flamingo_gated_d1_seqx_r4_0ad9af'

def setup_inputs(seed: int=0):
    np.random.seed(seed)
    _w = jnp.asarray

    def _rec_inputs():
        import jax
        import jax.numpy as jnp
        _rk = jax.random.key(seed)
        x = 7.22e-05 + 1 * jax.random.normal(jax.random.fold_in(_rk, 1), (64, 128, 256), jnp.float32)
        _lenS = 128 - jax.random.randint(jax.random.fold_in(_rk, 7), (64,), 0, max(1, 128 // 4) + 1, jnp.int32)
        _lenS2 = 128 - jax.random.randint(jax.random.fold_in(_rk, 8), (64,), 0, max(1, 128 // 4) + 1, jnp.int32)
        _ctx_1024P = jax.random.normal(jax.random.fold_in(_rk, 11), (64, 16, 256), jnp.float32)
        _ctx_1024c = jax.random.dirichlet(jax.random.fold_in(_rk, 511), 0.3 * jnp.ones((16,), jnp.float32), (64, 128))
        _ctx_1024t = jnp.einsum('bsk,bkd->bsd', _ctx_1024c, _ctx_1024P)
        _ctx_1024t = _ctx_1024t * jax.lax.rsqrt(jnp.mean(jnp.square(_ctx_1024t)) + 1e-12) * 0.953939
        ctx_1024 = 4.13588e-05 + 0.999923 * (_ctx_1024t + 0.3 * jax.random.normal(jax.random.fold_in(_rk, 611), (64, 128, 256), jnp.float32))
        _g = jax.random.normal(jax.random.fold_in(_rk, 9001), (2, 1), jnp.float32)
        _g = jnp.sign(_g) * jnp.maximum(jnp.abs(_g), 1.0) + (_g == 0) * 1.0
        g_xattn = _g[0]
        g_ffn = _g[1]
        return (x, ctx_1024, g_xattn, g_ffn)
    x, ctx_1024, g_xattn, g_ffn = _rec_inputs()

    def _L0_xattn_setup():
        import jax, jax.numpy as jnp
        import numpy as np
        D_MODEL = 256
        NUM_HEADS = 16
        HEAD_DIM = D_MODEL // NUM_HEADS
        MAX_SEQ = 128

        def rope_tables(seq_len, dim):
            inv_freq = 1.0 / 10000.0 ** (jnp.arange(0, dim, 2, dtype=jnp.float32) / dim)
            t = jnp.arange(seq_len, dtype=jnp.float32)
            freqs = jnp.einsum('i,j->ij', t, inv_freq)
            emb = jnp.concatenate([freqs, freqs], axis=-1)
            return (jnp.cos(emb), jnp.sin(emb))

        def rotate_half(x):
            x1, x2 = jnp.split(x, 2, axis=-1)
            return jnp.concatenate([-x2, x1], axis=-1)
        key = jax.random.key(seed)
        ks = jax.random.split(key, 12)
        B, S, D = (16, 128, D_MODEL)
        s = 1.0 / np.sqrt(D)
        inp = {'query': jax.random.normal(ks[0], (B, S, D), jnp.float32), 'key': jax.random.normal(ks[1], (B, S, D), jnp.float32), 'value': jax.random.normal(ks[2], (B, S, D), jnp.float32), 'Wq': jax.random.normal(ks[3], (D, D), jnp.float32) * s, 'bq': jnp.zeros((D,), jnp.float32), 'Wk': jax.random.normal(ks[4], (D, D), jnp.float32) * s, 'bk': jnp.zeros((D,), jnp.float32), 'Wv': jax.random.normal(ks[5], (D, D), jnp.float32) * s, 'bv': jnp.zeros((D,), jnp.float32), 'Wo': jax.random.normal(ks[6], (D, D), jnp.float32) * s, 'bo': jnp.zeros((D,), jnp.float32)}
        return inp
    _L0_xattn_all = _L0_xattn_setup()
    _L0_xattn_in = {k: v for k, v in _L0_xattn_all.items() if k in ('Wq', 'bq', 'Wk', 'bk', 'Wv', 'bv', 'Wo', 'bo')}
    del _L0_xattn_all

    def _L0_ffn_setup():
        import jax, jax.numpy as jnp
        import numpy as np
        import math
        B, S, D = (4, 512, 256)
        E, DFF = (16, 512)
        CAP_FACTOR = 2.0
        ROUTER_HIDDEN = 128
        CAPACITY = int(math.ceil(S * CAP_FACTOR / E))
        key = jax.random.key(seed)
        ks = jax.random.split(key, 6)

        def uinit(k, shape, fan_in):
            bound = math.sqrt(3.0) * math.sqrt(1.0 / 3.0) / math.sqrt(fan_in)
            return jax.random.uniform(k, shape, jnp.float32, -bound, bound)
        return {'hidden_states': jax.random.normal(ks[0], (B, S, D), jnp.float32), 'router_w1': jax.random.normal(ks[1], (D, ROUTER_HIDDEN), jnp.float32) / math.sqrt(D), 'router_w2': jax.random.normal(ks[2], (ROUTER_HIDDEN, E), jnp.float32) / math.sqrt(ROUTER_HIDDEN), 'w1': uinit(ks[3], (E, D, DFF), D), 'w2': uinit(ks[4], (E, D, DFF), D), 'w3': uinit(ks[5], (E, DFF, D), DFF)}
    _L0_ffn_all = _L0_ffn_setup()
    _L0_ffn_in = {k: v for k, v in _L0_ffn_all.items() if k in ('router_w1', 'router_w2', 'w1', 'w2', 'w3')}
    del _L0_ffn_all
    return {'x': x, 'ctx_1024': ctx_1024, 'g_xattn': g_xattn, 'g_ffn': g_ffn, 'L0_xattn_Wq': _L0_xattn_in['Wq'], 'L0_xattn_bq': _L0_xattn_in['bq'], 'L0_xattn_Wk': _L0_xattn_in['Wk'], 'L0_xattn_bk': _L0_xattn_in['bk'], 'L0_xattn_Wv': _L0_xattn_in['Wv'], 'L0_xattn_bv': _L0_xattn_in['bv'], 'L0_xattn_Wo': _L0_xattn_in['Wo'], 'L0_xattn_bo': _L0_xattn_in['bo'], 'L0_ffn_router_w1': _L0_ffn_in['router_w1'], 'L0_ffn_router_w2': _L0_ffn_in['router_w2'], 'L0_ffn_w1': _L0_ffn_in['w1'], 'L0_ffn_w2': _L0_ffn_in['w2'], 'L0_ffn_w3': _L0_ffn_in['w3']}

def reference(x, ctx_1024, g_xattn, g_ffn, L0_xattn_Wq, L0_xattn_bq, L0_xattn_Wk, L0_xattn_bk, L0_xattn_Wv, L0_xattn_bv, L0_xattn_Wo, L0_xattn_bo, L0_ffn_router_w1, L0_ffn_router_w2, L0_ffn_w1, L0_ffn_w2, L0_ffn_w3):
    import jax
    import jax.numpy as jnp

    def _L0_xattn_ref(query, key, value, Wq, bq, Wk, bk, Wv, bv, Wo, bo):
        import jax, jax.numpy as jnp
        import numpy as np
        D_MODEL = 256
        NUM_HEADS = 16
        HEAD_DIM = D_MODEL // NUM_HEADS
        MAX_SEQ = 128

        def rope_tables(seq_len, dim):
            inv_freq = 1.0 / 10000.0 ** (jnp.arange(0, dim, 2, dtype=jnp.float32) / dim)
            t = jnp.arange(seq_len, dtype=jnp.float32)
            freqs = jnp.einsum('i,j->ij', t, inv_freq)
            emb = jnp.concatenate([freqs, freqs], axis=-1)
            return (jnp.cos(emb), jnp.sin(emb))

        def rotate_half(x):
            x1, x2 = jnp.split(x, 2, axis=-1)
            return jnp.concatenate([-x2, x1], axis=-1)
        B, S, D = query.shape
        H, Hd = (NUM_HEADS, HEAD_DIM)
        scale = Hd ** (-0.5)

        def proj(x, W, b):
            y = jnp.einsum('bsd,ed->bse', x, W) + b
            return y.reshape(B, S, H, Hd).transpose(0, 2, 1, 3)
        q = proj(query, Wq, bq)
        k = proj(key, Wk, bk)
        v = proj(value, Wv, bv)
        cos, sin = rope_tables(S, Hd)
        cos = cos[None, None]
        sin = sin[None, None]
        q = q * cos + rotate_half(q) * sin
        k = k * cos + rotate_half(k) * sin
        attn = jnp.einsum('bhqd,bhkd->bhqk', q, k) * scale
        attn_w = jax.nn.softmax(attn, axis=-1)
        out = jnp.einsum('bhqk,bhkd->bhqd', attn_w, v)
        out = out.transpose(0, 2, 1, 3).reshape(B, S, D)
        out = jnp.einsum('bsd,ed->bse', out, Wo) + bo
        return out

    def _L0_ffn_ref(hidden_states, router_w1, router_w2, w1, w2, w3):
        import jax, jax.numpy as jnp
        import numpy as np
        import math
        B, S, D = (4, 512, 256)
        E, DFF = (16, 512)
        CAP_FACTOR = 2.0
        ROUTER_HIDDEN = 128
        CAPACITY = int(math.ceil(S * CAP_FACTOR / E))
        b, s, d = hidden_states.shape
        e = w1.shape[0]
        cap = CAPACITY
        router_logits = jax.nn.silu(hidden_states @ router_w1) @ router_w2
        expert_probs = jax.nn.softmax(router_logits.transpose(0, 2, 1), axis=-1)
        expert_weights, token_indices = jax.lax.top_k(expert_probs, cap)
        expert_weights = expert_weights / (expert_weights.sum(-1, keepdims=True) + 1e-09)
        expert_inputs = jax.vmap(lambda h, i: h[i])(hidden_states, token_indices)
        gate = jax.nn.silu(jnp.einsum('becd,edf->becf', expert_inputs, w1))
        value = jnp.einsum('becd,edf->becf', expert_inputs, w2)
        expert_out = jnp.einsum('becf,efd->becd', gate * value, w3)
        weighted = expert_out * expert_weights[..., None]

        def combine(idx, vals):
            return jnp.zeros((s, d), vals.dtype).at[idx.reshape(-1)].add(vals.reshape(-1, d))
        output = jax.vmap(combine)(token_indices, weighted)
        return output
    x = x + jnp.tanh(g_xattn[0]) * _L0_xattn_ref(_layernorm(x, axis=-1), ctx_1024, ctx_1024, L0_xattn_Wq, L0_xattn_bq, L0_xattn_Wk, L0_xattn_bk, L0_xattn_Wv, L0_xattn_bv, L0_xattn_Wo, L0_xattn_bo)
    x = x + jnp.tanh(g_ffn[0]) * _L0_ffn_ref(_layernorm(x, axis=-1), L0_ffn_router_w1, L0_ffn_router_w2, L0_ffn_w1, L0_ffn_w2, L0_ffn_w3)
    return x

_drawn_inputs = setup_inputs


def setup_inputs(seed=0):
    import zlib

    import numpy as np

    out = dict(_drawn_inputs(seed))
    spreads = {'L0_xattn_bq': (0.0, 0.529),
     'L0_xattn_bk': (0.0, 0.8),
     'L0_xattn_bv': (0.0, 0.1),
     'L0_xattn_bo': (0.0, 0.1)}
    factors = {'L0_ffn_router_w1': 8.0,
     'L0_ffn_router_w2': 8.0,
     'L0_ffn_w1': 8.0,
     'L0_ffn_w2': 8.0,
     'L0_ffn_w3': 8.0}
    for name, (base, spread) in spreads.items():
        noise = np.random.default_rng([zlib.crc32(name.encode()), seed]).standard_normal(out[name].shape)
        drawn = base * np.exp(spread * noise) if base else spread * noise
        out[name] = jnp.asarray(drawn.astype(out[name].dtype))
    for name, factor in factors.items():
        out[name] = (out[name] * factor).astype(out[name].dtype)
    return out
```

```python
from contextlib import ExitStack

import concourse.bass as bass
from concourse import mybir

F32 = mybir.dt.float32
F16 = mybir.dt.float16
ALU = mybir.AluOpType
ACT = mybir.ActivationFunctionType
AX_X = mybir.AxisListType.X

P = 128
HEADS = 16
HD = 16
PAIRS = HEADS // 2
CHUNKS = 4
TOP = 64
GB = 8
QE = 4
LN_EPS = 1e-5
W_UP = 64.0
ATT_UP = 16.0
Y_DOWN = 1.0 / 64
HI, LO = 0, 1


def need(engine, semaphore, value):
    if isinstance(value, int) and value <= 0:
        return
    engine.wait_ge(semaphore, value)


def three_pass(eng, out, stationary, moving, ks, first=True, last=True):
    todo = [(k, a, b) for k in ks for a, b in ((HI, HI), (HI, LO), (LO, HI))]
    for n, (k, a, b) in enumerate(todo):
        mm = eng.matmul(out, stationary(a, k), moving(b, k), start=(first and n == 0),
                        stop=(last and n == len(todo) - 1), skip_group_check=True)
    return mm


def attention_phase(nc, io, keep, dims):
    NB, D, E, RH = dims["NB"], dims["D"], dims["E"], dims["RH"]
    K = D // P
    ctx = ExitStack()
    with ctx:
        def sb(name, shape, dt=F32):
            return ctx.enter_context(nc.sbuf_tensor(name, shape, dt))

        def bank(name):
            return ctx.enter_context(nc.psum_tensor(name, [P, 512], F32))

        def sem(name):
            return ctx.enter_context(nc.semaphore(name))

        ident = sb("ident", [P, P])
        ident16 = sb("ident16", [P, P], F16)
        rope = sb("rope", [P, 2, HD])
        w_raw = sb("w_raw", [P, 4, K, D])
        WT4 = sb("WT4", [P, 4, 2, K, D], F16)
        rw1_raw = sb("rw1_raw", [P, K, RH])
        rw1 = sb("rw1", [P, 2, K, RH], F16)
        rw2_raw = sb("rw2_raw", [P, E])
        rw2 = sb("rw2", [P, 2, E], F16)
        bqk = sb("bqk", [P, 2, D])
        bvo = sb("bvo", [P, 2, D])
        gates = sb("gates", [P, 2])
        tanh_g = sb("tanh_g", [P, 2])
        x_scale = sb("x_scale", [P, 1])
        w_scale = sb("w_scale", [P, 1])
        bo_g = sb("bo_g", [P, D])
        eps = sb("eps", [P, 1])
        minus_half = sb("minus_half", [P, 1])
        zeros = sb("zeros", [P, P])

        x_in = sb("x_in", [P, 2, D])
        c_in = sb("c_in", [P, 2, D])
        x_res = sb("x_res", [P, 2, D])
        ln_st = sb("ln_st", [P, 2, 6])
        ln_mv = sb("ln_mv", [P, 2, 2])
        ln_ve = sb("ln_ve", [P, 2])
        ln_rs = sb("ln_rs", [P, 2])
        xn = sb("xn", [P, D])
        xT = sb("xT", [P, 2, 2 * K, P], F16)
        qk = sb("qk", [P, 2 * D])
        rot_a = sb("rot_a", [P, 2 * D])
        rot_b = sb("rot_b", [P, 2 * D])
        qkr = sb("qkr", [P, 2 * D])
        QS = sb("QS", [P, PAIRS, 3, 32], F16)
        KS = sb("KS", [P, PAIRS, 2, 3, 2, HD], F16)
        QT = sb("QT", [96, PAIRS, P], F16)
        KT = sb("KT", [96, HEADS, P], F16)
        v32 = sb("v32", [P, D])
        V = sb("V", [P, 2, 2, HEADS, HD + 1], F16)
        mx = sb("mx", [P, 2, 4])
        nm = sb("nm", [P, 2, 4])
        Pr = sb("Pr", [P, 2, 4, P])
        PT = sb("PT", [P, 2, 2, 4, P], F16)
        den = sb("den", [P, HEADS])
        att = sb("att", [P, HEADS, HD])
        attT = sb("attT", [P, 2, K, P], F16)
        x1 = sb("x1", [P, 2, D])
        h32 = sb("h32", [P, D])
        hT = sb("hT", [P, 2, K, P], F16)
        r_e = sb("r_e", [P, P])
        r_d = sb("r_d", [P, P])
        r_r = sb("r_r", [P, P])
        r_a = sb("r_a", [P, P])
        aT = sb("aT", [P, 2, P], F16)
        L = sb("L", [P, NB, E])

        Lg = sb("Lg", [P, P])
        t_mx = sb("t_mx", [P, 1])
        t_nm = sb("t_nm", [P, 1])
        t_e = sb("t_e", [P, P])
        t_sum = sb("t_sum", [P, 1])
        t_rs = sb("t_rs", [P, 1])
        t_p = sb("t_p", [P, P])
        t_w = sb("t_w", [P, 2, P])
        t_m8 = sb("t_m8", [P, 8])
        t_msk = sb("t_msk", [P, P])
        t_pm = sb("t_pm", [P, P])
        t_ps = sb("t_ps", [P, 1])
        t_dn = sb("t_dn", [P, 1])
        t_rd = sb("t_rd", [P, 1])
        t_wr = sb("t_wr", [P, 1])
        t_wt = sb("t_wt", [P, P])
        t_cum = sb("t_cum", [P, P])
        t_pos = sb("t_pos", [P, P])
        spare = sb("spare", [P, 1])

        S_ps = [bank("S0_ps"), bank("S1_ps")]
        PT_ps = [bank("PT0_ps"), bank("PT1_ps")]
        qk_bank = bank("qk_bank")
        small = bank("small_ps")
        vo_bank = bank("vo_bank")
        T_ps = bank("T_ps")
        att_ps = small[:, 0:HEADS * (HD + 1)].rearrange("p (h d) -> p h d", d=HD + 1)
        r1_ps = small[:, 272:272 + P]
        r2_ps = small[:, 400:400 + E]
        v_ps = vo_bank[:, 0:D]
        o_ps = vo_bank[:, D:2 * D]
        fill_a = vo_bank[:, :].bitcast(F16).rearrange("p (h s) -> p h s", s=P)
        fill_b = qk_bank[:, :].bitcast(F16).rearrange("p (h s) -> p h s", s=P)

        s_const_in = sem("const_in")
        s_w_in = sem("w_in")
        s_zero_set = sem("zero_set")
        s_ident16_set = sem("ident16_set")
        s_v_ones = sem("v_ones")
        s_wT_ps = sem("wT_ps")
        s_wT_hi = sem("wT_hi")
        s_wT_lo = sem("wT_lo")
        s_rw_hi = sem("rw_hi")
        s_rw_lo = sem("rw_lo")
        s_tanh_done = sem("tanh_done")
        s_scales_set = sem("scales_set")
        s_x_in_done = sem("x_in_done")
        s_c_in_done = sem("c_in_done")
        s_xr_in = sem("xr_in")
        s_ln1_stat = sem("ln1_stat")
        s_ln1_mv = sem("ln1_mv")
        s_ln1_ve = sem("ln1_ve")
        s_ln1_rstd = sem("ln1_rstd")
        s_xn_ready = sem("xn_ready")
        s_xT_ps = sem("xT_ps")
        s_xT_hi = sem("xT_hi")
        s_xT_lo = sem("xT_lo")
        s_qk_ps = sem("qk_ps")
        s_v_done_ps = sem("v_done_ps")
        s_qk_sb = sem("qk_sb")
        s_v_sb = sem("v_sb")
        s_v_hi = sem("v_hi")
        s_v_lo = sem("v_lo")
        s_rot_cos = sem("rot_cos")
        s_rot_sin = sem("rot_sin")
        s_rot = sem("rot")
        s_qk_hi = sem("qk_hi")
        s_qk_lo = sem("qk_lo")
        s_qkT_ps = sem("qkT_ps")
        s_qkT_sb = sem("qkT_sb")
        s_scores = sem("scores")
        s_max_done = sem("max_done")
        s_neg_max = sem("neg_max")
        s_exp_done = sem("exp_done")
        s_p_T = sem("p_T")
        s_p_hi = sem("p_hi")
        s_p_lo = sem("p_lo")
        s_pv = sem("pv")
        s_recip_den = sem("recip_den")
        s_att_sb = sem("att_sb")
        s_att_T = sem("att_T")
        s_attT_hi = sem("attT_hi")
        s_attT_lo = sem("attT_lo")
        s_o_done = sem("o_done")
        s_xrb = sem("xrb")
        s_x1_done = sem("x1_done")
        s_x1_out = sem("x1_out")
        s_ln2_stat = sem("ln2_stat")
        s_ln2_mv = sem("ln2_mv")
        s_ln2_ve = sem("ln2_ve")
        s_ln2_rstd = sem("ln2_rstd")
        s_h_sb = sem("h_sb")
        s_h_hi = sem("h_hi")
        s_h_lo = sem("h_lo")
        s_hT_ps = sem("hT_ps")
        s_hT_hi = sem("hT_hi")
        s_hT_lo = sem("hT_lo")
        s_r1 = sem("r1")
        s_r_exp = sem("r_exp")
        s_r_one = sem("r_one")
        s_r_rec = sem("r_rec")
        s_r_act = sem("r_act")
        s_a_hi = sem("a_hi")
        s_a_lo = sem("a_lo")
        s_r2 = sem("r2")
        s_logit = sem("logit")
        s_tk_copy = sem("tk_copy")
        s_tk_T = sem("tk_T")
        s_tk_max = sem("tk_max")
        s_tk_neg = sem("tk_neg")
        s_tk_exp = sem("tk_exp")
        s_tk_rec = sem("tk_rec")
        s_tk_p = sem("tk_p")
        s_tk_top = sem("tk_top")
        s_tk_rest = sem("tk_rest")
        s_tk_msk = sem("tk_msk")
        s_tk_sum = sem("tk_sum")
        s_tk_den = sem("tk_den")
        s_tk_rden = sem("tk_rden")
        s_tk_wr = sem("tk_wr")
        s_tk_cum = sem("tk_cum")
        s_tk_res = sem("tk_res")
        s_tk_T2 = sem("tk_T2")
        s_tk_pos = sem("tk_pos")
        s_tk_wt = sem("tk_wt")
        CONST_IN = 16 * 3
        W_IN = 16 * 12

        FIRST, LAST = -3, NB + 2
        LOOP_FROM, LOOP_TO = 3, NB - 6

        def slots(eng, step):
            for t in range(FIRST, LOOP_FROM):
                step(t, t % 2)
            with eng.Fori(0, (LOOP_TO - LOOP_FROM + 1) // 2) as j:
                for k in range(2):
                    step(2 * j + (LOOP_FROM + k), (LOOP_FROM + k) % 2)
            for t in range(LOOP_TO + 1, LAST):
                step(t, t % 2)

        def has(n):
            return not isinstance(n, int) or 0 <= n < NB

        def upto(n):
            return min(n, NB) if isinstance(n, int) else n

        block = ctx.enter_context(nc.Block())

        @block.sync
        def _(sp):
            sp.dma_start(ident[:, :], io["ident"]).then_inc(s_const_in, 16)
            sp.dma_start(rope[:, :, :], io["rope"].rearrange("p (c j) -> p c j", c=2)).then_inc(s_const_in, 16)
            sp.dma_start(keep["iota"][:, :], io["iota"]).then_inc(s_const_in, 16)
            for i, w in enumerate((io["Wq"], io["Wk"], io["Wv"], io["Wo"])):
                sp.dma_start(w_raw[:, i, :, :], w.rearrange("(c p) d -> p c d", p=P)).then_inc(s_w_in, 16)
            sp.dma_start(rw1_raw[:, :, :], io["rw1"].rearrange("(c p) h -> p c h", p=P)).then_inc(s_w_in, 16)
            sp.dma_start(rw2_raw[:, :], io["rw2"]).then_inc(s_w_in, 16)
            for i, b in enumerate((io["bq"], io["bk"])):
                sp.dma_start(bqk[:, i, :], b.partition_broadcast(P)).then_inc(s_w_in, 16)
            for i, b in enumerate((io["bv"], io["bo"])):
                sp.dma_start(bvo[:, i, :], b.partition_broadcast(P)).then_inc(s_w_in, 16)
            for i, g in enumerate((io["g_xattn"], io["g_ffn"])):
                sp.dma_start(gates[:, i:i + 1], g.partition_broadcast(P)).then_inc(s_w_in, 16)

            def step(t, par):
                if has(t + 4):
                    n = t + 4
                    need(sp, s_xn_ready, n - 1)
                    sp.wait_ge(s_x_in_done, 16 * n)
                    sp.dma_start(x_in[:, par, :], io["x"][n]).then_inc(s_x_in_done, 16)
                    need(sp, s_xT_ps, n - 1)
                    sp.wait_ge(s_c_in_done, 16 * n)
                    sp.dma_start(c_in[:, par, :], io["ctx"][n]).then_inc(s_c_in_done, 16)
                if has(t):
                    need(sp, s_x1_done, t - 1)
                    need(sp, s_xr_in, 16 * t)
                    sp.dma_start(x_res[:, par, :], io["x"][t]).then_inc(s_xr_in, 16)
                if has(t - 2):
                    need(sp, s_x1_out, 16 * (t - 2))
                    sp.wait_ge(s_x1_done, t - 1)
                    sp.dma_start(io["out"][t - 2], x1[:, par, :]).then_inc(s_x1_out, 16)

            sp.dma_start(x_in[:, 0, :], io["x"][0]).then_inc(s_x_in_done, 16)
            sp.dma_start(c_in[:, 0, :], io["ctx"][0]).then_inc(s_c_in_done, 16)
            slots(sp, step)
            sp.wait_ge(s_x1_out, 16 * NB)

        @block.gpsimd
        def _(pool):
            pool.memset(KS[:, :, :, :, :, :], 0.0).then_inc(s_zero_set, 1)
            pool.memset(V[:, :, HI, :, HD:HD + 1], 1.0).then_inc(s_v_ones, 1)
            pool.memset(V[:, :, LO, :, HD:HD + 1], 0.0).then_inc(s_v_ones, 1)
            pool.memset(eps[:, :], LN_EPS).then_inc(s_zero_set, 1)
            pool.memset(minus_half[:, :], -0.5).then_inc(s_zero_set, 1)
            pool.memset(zeros[:, :], 0.0).then_inc(s_zero_set, 1)
            pool.wait_ge(s_zero_set, 4)
            pool.wait_ge(s_scales_set, 3)

            def rstd(n, which, mv, ve, rs, used):
                pool.wait_ge(mv, n + 1)
                pool.tensor_tensor(ln_ve[:, which:which + 1], ln_mv[:, which, 1:2], eps[:, :],
                                   ALU.add).then_inc(ve, 1)
                pool.wait_ge(ve, n + 1)
                need(pool, used, n)
                pool.tensor_tensor(ln_rs[:, which:which + 1], ln_ve[:, which:which + 1],
                                   minus_half[:, :], ALU.pow).then_inc(rs, 1)

            def step(t, par):
                if has(t - 1):
                    n = t - 1
                    pool.wait_ge(s_xr_in, 16 * (n + 1))
                    pool.tensor_tensor(x_res[:, 1 - par, :], x_res[:, 1 - par, :], bo_g[:, :],
                                       ALU.add).then_inc(s_xrb, 1)
                if has(t + 1):
                    n = t + 1
                    pool.wait_ge(s_qk_sb, n + 1)
                    need(pool, s_rot, n)
                    pool.tensor_tensor(
                        rot_a[:, :].rearrange("p (h j) -> p h j", j=HD),
                        qk[:, :].rearrange("p (h j) -> p h j", j=HD),
                        rope[:, 0:1, :].broadcast_to([P, 2 * HEADS, HD]), ALU.mult).then_inc(s_rot_cos, 1)
                if has(t - 1):
                    rstd(t - 1, 1, s_ln2_mv, s_ln2_ve, s_ln2_rstd, s_h_sb)
                if has(t + 3):
                    rstd(t + 3, 0, s_ln1_mv, s_ln1_ve, s_ln1_rstd, s_xn_ready)

            slots(pool, step)

        @block.tensor
        def _(pe):
            pe.wait_ge(s_const_in, CONST_IN)
            pe.wait_ge(s_w_in, W_IN)
            for w in range(4):
                dst = [*S_ps, *PT_ps][w]
                for k in range(K):
                    for c in range(K):
                        mm = pe.transpose(dst[:, (k * K + c) * P:(k * K + c + 1) * P],
                                          w_raw[:, w, c, k * P:(k + 1) * P], ident[:, :])
                mm.then_inc(s_wT_ps, 1)
            pe.wait_ge(s_wT_lo, 4)
            pe.wait_ge(s_rw_lo, 2)
            pe.wait_ge(s_ident16_set, 1)
            pe.wait_ge(s_v_ones, 2)

            def scores(n, c):
                g = 4 * n + c
                if c == 0:
                    pe.wait_ge(s_qkT_sb, 3 * (n + 1))
                need(pe, s_exp_done, g - 1)
                for u in range(2):
                    mm = pe.matmul(S_ps[c % 2][:, 2 * P * u:2 * P * (u + 1)], QT[:, 2 * c + u, :],
                                   KT[:, 4 * c + 2 * u:4 * c + 2 * u + 2, :], start=True, stop=True)
                mm.then_inc(s_scores, 1)

            def turn_p(n, c):
                g = 4 * n + c
                pe.wait_ge(s_exp_done, g + 1)
                need(pe, s_p_lo, g - 1)
                for h in range(4):
                    mm = pe.transpose(PT_ps[c % 2][:, h * P:(h + 1) * P], Pr[:, c % 2, h, :], ident[:, :])
                mm.then_inc(s_p_T, 1)

            def weigh_v(n, c, par):
                g = 4 * n + c
                if c == 0:
                    pe.wait_ge(s_v_lo, n + 1)
                    need(pe, s_att_sb, n)
                    need(pe, s_logit, n - 1)
                pe.wait_ge(s_p_lo, g + 1)
                for hh in range(4):
                    h = 4 * c + hh
                    mm = three_pass(pe, att_ps[:, h, :], lambda a, k: PT[:, c % 2, a, hh, :],
                                    lambda b, k: V[:, par, b, h, :], [0])
                mm.then_inc(s_pv, 1)

            def project(n):
                pe.wait_ge(s_xT_lo, n + 1)
                need(pe, s_qkT_sb, 3 * n)
                three_pass(pe, qk_bank[:, 0:D], lambda a, k: xT[:, a, k, :],
                           lambda b, k: WT4[:, 0, b, k, :], range(K))
                three_pass(pe, qk_bank[:, D:2 * D], lambda a, k: xT[:, a, K + k, :],
                           lambda b, k: WT4[:, 1, b, k, :], range(K)).then_inc(s_qk_ps, 1)
                three_pass(pe, v_ps, lambda a, k: xT[:, a, K + k, :],
                           lambda b, k: WT4[:, 2, b, k, :], range(K)).then_inc(s_v_done_ps, 1)

            def turn_att(n):
                pe.wait_ge(s_att_sb, n + 1)
                need(pe, s_hT_lo, n)
                for k in range(K):
                    mm = pe.transpose(T_ps[:, k * P:(k + 1) * P], att[:, 8 * k:8 * k + 8, :], ident[:, :])
                mm.then_inc(s_att_T, 1)

            def project_out(n):
                pe.wait_ge(s_attT_lo, n + 1)
                pe.wait_ge(s_qkT_sb, 3 * upto(n + 2))
                pe.wait_ge(s_v_sb, upto(n + 3))
                three_pass(pe, o_ps, lambda a, k: attT[:, a, k, :],
                           lambda b, k: WT4[:, 3, b, k, :], range(K)).then_inc(s_o_done, 1)

            def turn_x(n, par):
                pe.wait_ge(s_xn_ready, n + 1)
                pe.wait_ge(s_c_in_done, 16 * (n + 1))
                need(pe, s_attT_lo, n - 2)
                for k in range(K):
                    pe.transpose(T_ps[:, k * P:(k + 1) * P], xn[:, k * P:(k + 1) * P], ident[:, :])
                for k in range(K):
                    mm = pe.transpose(T_ps[:, (K + k) * P:(K + k + 1) * P],
                                      c_in[:, par, k * P:(k + 1) * P], ident[:, :])
                mm.then_inc(s_xT_ps, 1)

            def turn_h(n):
                pe.wait_ge(s_h_sb, n + 1)
                pe.wait_ge(s_xT_lo, upto(n + 4))
                for k in range(K):
                    mm = pe.transpose(T_ps[:, k * P:(k + 1) * P], h32[:, k * P:(k + 1) * P], ident[:, :])
                mm.then_inc(s_hT_ps, 1)

            def turn_qk(n):
                pe.wait_ge(s_qk_lo, n + 1)
                pe.wait_ge(s_v_sb, n + 1)
                need(pe, s_x1_done, n - 1)
                for p in range(PAIRS):
                    mm = pe.transpose(fill_a[0:96, p, :], QS[:, p, :, :], ident16[:, :])
                mm.then_inc(s_qkT_ps, 1)
                for h in range(HEADS // 2):
                    mm = pe.transpose(fill_b[0:96, h, :], KS[:, h // 2, h % 2, :, :, :], ident16[:, :])
                mm.then_inc(s_qkT_ps, 1)
                pe.wait_ge(s_qkT_sb, 3 * n + 1)
                for h in range(HEADS // 2, HEADS):
                    mm = pe.transpose(fill_a[0:96, h - HEADS // 2, :], KS[:, h // 2, h % 2, :, :, :],
                                      ident16[:, :])
                mm.then_inc(s_qkT_ps, 1)

            def route_1(n):
                pe.wait_ge(s_hT_lo, n + 1)
                three_pass(pe, r1_ps, lambda a, k: rw1[:, a, k, :],
                           lambda b, k: hT[:, b, k, :], range(K)).then_inc(s_r1, 1)

            def route_2(n):
                pe.wait_ge(s_a_lo, n + 1)
                pe.wait_ge(s_att_sb, upto(n + 2))
                three_pass(pe, r2_ps, lambda a, k: aT[:, a, :],
                           lambda b, k: rw2[:, b, :], [0]).then_inc(s_r2, 1)

            def step(t, par):
                if has(t):
                    scores(t, 0)
                    scores(t, 1)
                if has(t + 1):
                    project(t + 1)
                if has(t - 2):
                    route_2(t - 2)
                if has(t):
                    turn_p(t, 0)
                    scores(t, 2)
                if has(t - 1):
                    turn_att(t - 1)
                if has(t):
                    turn_p(t, 1)
                    scores(t, 3)
                    weigh_v(t, 0, par)
                if has(t - 1):
                    project_out(t - 1)
                if has(t):
                    turn_p(t, 2)
                    weigh_v(t, 1, par)
                if has(t + 2):
                    turn_x(t + 2, par)
                if has(t):
                    turn_p(t, 3)
                    weigh_v(t, 2, par)
                if has(t - 1):
                    turn_h(t - 1)
                if has(t + 1):
                    turn_qk(t + 1)
                if has(t):
                    weigh_v(t, 3, par)
                if has(t - 1):
                    route_1(t - 1)

            slots(pe, step)

            with pe.Fori(0, NB // GB) as g:
                pe.wait_ge(s_tk_copy, g + 1)
                pe.transpose(S_ps[0][:, 0:P], Lg[:, :], ident[:, :]).then_inc(s_tk_T, 1)
                pe.wait_ge(s_tk_res, 2 * (g + 1))
                pe.transpose(S_ps[1][:, 0:P], t_pos[:, :], ident[:, :])
                pe.transpose(S_ps[1][:, P:2 * P], t_wt[:, :], ident[:, :]).then_inc(s_tk_T2, 1)
                pe.wait_ge(s_tk_pos, g + 1)
                pe.wait_ge(s_tk_wt, g + 1)

        @block.scalar
        def _(act):
            def high(out, in_, scale=1.0):
                return act.activation(out, in_, ACT.Copy, scale=scale)

            act.wait_ge(s_w_in, W_IN)
            act.activation(tanh_g[:, :], gates[:, :], ACT.Tanh).then_inc(s_tanh_done, 1)
            for w in range(4):
                act.wait_ge(s_wT_ps, w + 1)
                high(WT4[:, w, HI, :, :], [*S_ps, *PT_ps][w][:, :], W_UP).then_inc(s_wT_hi, 1)
            high(rw1[:, HI, :, :], rw1_raw[:, :, :], W_UP).then_inc(s_rw_hi, 1)
            high(rw2[:, HI, :], rw2_raw[:, :], W_UP).then_inc(s_rw_hi, 1)
            act.wait_ge(s_const_in, CONST_IN)
            high(ident16[:, :], ident[:, :]).then_inc(s_ident16_set, 1)
            act.wait_ge(s_zero_set, 4)
            act.wait_ge(s_v_ones, 2)

            def exps(n, c):
                g = 4 * n + c
                act.wait_ge(s_neg_max, g + 1)
                need(act, s_p_T, g - 1)
                for h in range(4):
                    a = act.activation(Pr[:, c % 2, h, :], S_ps[c % 2][:, h * P:(h + 1) * P], ACT.Exp,
                                       bias=nm[:, c % 2, h:h + 1], scale=HD ** -0.5)
                a.then_inc(s_exp_done, 1)

            def p_high(n, c):
                g = 4 * n + c
                act.wait_ge(s_p_T, g + 1)
                need(act, s_pv, g - 1)
                high(PT[:, c % 2, HI, :, :], PT_ps[c % 2][:, :]).then_inc(s_p_hi, 1)

            def step(t, par):
                if has(t):
                    exps(t, 0)
                    exps(t, 1)
                if has(t):
                    p_high(t, 0)
                if has(t - 1):
                    n = t - 1
                    act.wait_ge(s_att_T, n + 1)
                    need(act, s_o_done, n)
                    high(attT[:, HI, :, :], T_ps[:, 0:D], ATT_UP).then_inc(s_attT_hi, 1)
                if has(t):
                    exps(t, 2)
                    p_high(t, 1)
                if has(t + 1):
                    n = t + 1
                    act.wait_ge(s_v_sb, n + 1)
                    need(act, s_pv, 4 * (n - 1))
                    high(V[:, 1 - par, HI, :, 0:HD],
                         v32[:, :].rearrange("p (h d) -> p h d", d=HD)).then_inc(s_v_hi, 1)
                if has(t):
                    exps(t, 3)
                    p_high(t, 2)
                if has(t + 1):
                    n = t + 1
                    act.wait_ge(s_rot, n + 1)
                    need(act, s_qkT_ps, 3 * n)
                    q = qkr[:, 0:D].rearrange("p (a o c) -> p a o c", a=PAIRS, o=1)
                    k = qkr[:, D:2 * D].rearrange("p (a u c) -> p a u c", a=PAIRS, u=2)
                    high(QS[:, :, 0:3:2, :], q.broadcast_to([P, PAIRS, 2, 32]))
                    for u in range(2):
                        a = high(KS[:, :, u, 0:2, u, :],
                                 k[:, :, u:u + 1, :].broadcast_to([P, PAIRS, 2, HD]))
                    a.then_inc(s_qk_hi, 1)
                if has(t + 2):
                    n = t + 2
                    act.wait_ge(s_xT_ps, n + 1)
                    need(act, s_v_done_ps, n)
                    high(xT[:, HI, :, :], T_ps[:, :]).then_inc(s_xT_hi, 1)
                if has(t - 1):
                    n = t - 1
                    act.wait_ge(s_h_sb, n + 1)
                    high(keep["H"][:, n, HI, :], h32[:, :]).then_inc(s_h_hi, 1)
                if has(t):
                    p_high(t, 3)
                if has(t - 1):
                    n = t - 1
                    act.wait_ge(s_hT_ps, n + 1)
                    need(act, s_r1, n)
                    high(hT[:, HI, :, :], T_ps[:, 0:D]).then_inc(s_hT_hi, 1)
                if has(t + 1):
                    n = t + 1
                    need(act, s_scores, 4 * n)
                    for i, (dst, src) in enumerate(((QT[:, :, :], fill_a), (KT[:, 0:8, :], fill_b),
                                                    (KT[:, 8:16, :], fill_a))):
                        act.wait_ge(s_qkT_ps, 3 * n + i + 1)
                        high(dst, src[0:96, :, :]).then_inc(s_qkT_sb, 1)
                if has(t - 1):
                    n = t - 1
                    act.wait_ge(s_r1, n + 1)
                    need(act, s_r_one, n)
                    act.activation(r_e[:, :], r1_ps, ACT.Exp, scale=-1.0 / W_UP).then_inc(s_r_exp, 1)
                    act.wait_ge(s_r_act, n + 1)
                    need(act, s_r2, n)
                    high(aT[:, HI, :], r_a[:, :]).then_inc(s_a_hi, 1)

            slots(act, step)

            with act.Fori(0, NB // GB) as g:
                act.wait_ge(s_tk_neg, g + 1)
                act.activation(t_e[:, :], S_ps[0][:, 0:P], ACT.Exp, bias=t_nm[:, :],
                               accum_out=t_sum[:, :]).then_inc(s_tk_exp, 1)
                act.wait_ge(s_tk_T2, g + 1)
                high(keep["POS"][:, g, :, :, :], S_ps[1][:, 0:P].rearrange(
                    "p (b q i) -> p q b i", b=GB, q=E // QE)).then_inc(s_tk_pos, 1)
                high(keep["WT"][:, g, :, :, :], S_ps[1][:, P:2 * P].rearrange(
                    "p (b q i) -> p q i b", b=GB, q=E // QE)).then_inc(s_tk_wt, 1)

        @block.vector
        def _(dve):
            def low(out, in_, hi, scale=1.0):
                return dve.scalar_tensor_tensor(out=out, in0=in_, scalar=scale, in1=hi,
                                                op0=ALU.mult, op1=ALU.subtract)

            for w in range(4):
                dve.wait_ge(s_wT_hi, w + 1)
                low(WT4[:, w, LO, :, :], [*S_ps, *PT_ps][w][:, :].rearrange("p (k e) -> p k e", k=K),
                    WT4[:, w, HI, :, :], W_UP).then_inc(s_wT_lo, 1)
            dve.wait_ge(s_rw_hi, 2)
            low(rw1[:, LO, :, :], rw1_raw[:, :, :], rw1[:, HI, :, :], W_UP).then_inc(s_rw_lo, 1)
            low(rw2[:, LO, :], rw2_raw[:, :], rw2[:, HI, :], W_UP).then_inc(s_rw_lo, 1)
            dve.wait_ge(s_tanh_done, 1)
            dve.tensor_scalar(x_scale[:, :], tanh_g[:, 0:1], 1.0 / (W_UP * ATT_UP), None,
                              ALU.mult).then_inc(s_scales_set, 1)
            dve.tensor_scalar(w_scale[:, :], tanh_g[:, 1:2], 1.0 / Y_DOWN, None,
                              ALU.mult).then_inc(s_scales_set, 1)
            dve.tensor_scalar(bo_g[:, :], bvo[:, 1, :], tanh_g[:, 0:1], None,
                              ALU.mult).then_inc(s_scales_set, 1)
            dve.wait_ge(s_scales_set, 3)
            dve.wait_ge(s_const_in, CONST_IN)

            def maxima(n, c):
                g = 4 * n + c
                dve.wait_ge(s_scores, g + 1)
                dve.tensor_reduce(mx[:, c % 2, :], S_ps[c % 2][:, :].rearrange("p (h k) -> p h k", h=4),
                                  AX_X, ALU.max).then_inc(s_max_done, 1)
                dve.wait_ge(s_max_done, g + 1)
                need(dve, s_exp_done, g - 1)
                dve.tensor_scalar(nm[:, c % 2, :], mx[:, c % 2, :], -(HD ** -0.5), None,
                                  ALU.mult).then_inc(s_neg_max, 1)

            def p_low(n, c):
                g = 4 * n + c
                dve.wait_ge(s_p_hi, g + 1)
                dve.tensor_tensor(PT[:, c % 2, LO, :, :], PT_ps[c % 2][:, :].rearrange("p (h q) -> p h q", h=4),
                                  PT[:, c % 2, HI, :, :], ALU.subtract).then_inc(s_p_lo, 1)

            def tick():
                dve.memset(spare[:, :], 0.0)

            def norm_stats(n, which, in_, stat, mv, used):
                dve.bn_stats(ln_st[:, which, :], in_).then_inc(stat, 1)
                need(dve, used, n)
                dve.wait_ge(stat, n + 1)
                tick()
                dve.bn_aggr(ln_mv[:, which, :], ln_st[:, which, :]).then_inc(mv, 1)

            def norm_apply(out, in_, which):
                return dve.tensor_scalar(out, in_, ln_mv[:, which, 0:1], ln_rs[:, which:which + 1],
                                         ALU.subtract, ALU.mult)

            def step(t, par):
                if has(t - 1):
                    n = t - 1
                    dve.wait_ge(s_pv, 4 * (n + 1))
                    dve.reciprocal(den[:, :], att_ps[:, :, HD]).then_inc(s_recip_den, 1)
                    dve.wait_ge(s_recip_den, n + 1)
                    need(dve, s_att_T, n)
                    dve.tensor_tensor(att[:, :, :], att_ps[:, :, 0:HD],
                                      den[:, :].unsqueeze(2).broadcast_to([P, HEADS, HD]),
                                      ALU.mult).then_inc(s_att_sb, 1)
                if has(t):
                    maxima(t, 0)
                    maxima(t, 1)
                if has(t - 2):
                    n = t - 2
                    dve.wait_ge(s_r2, n + 1)
                    dve.tensor_scalar(L[:, n, :], r2_ps, 1.0 / W_UP, None, ALU.mult).then_inc(s_logit, 1)
                if has(t + 1):
                    n = t + 1
                    dve.wait_ge(s_qk_ps, n + 1)
                    need(dve, s_rot_cos, n)
                    dve.scalar_tensor_tensor(out=qk[:, :], in0=qk_bank[:, :], scalar=1.0 / W_UP,
                                             in1=bqk[:, :, :].rearrange("p a d -> p (a d)"), op0=ALU.mult,
                                             op1=ALU.add).then_inc(s_qk_sb, 1)
                if has(t):
                    p_low(t, 0)
                if has(t + 1):
                    n = t + 1
                    dve.wait_ge(s_v_done_ps, n + 1)
                    need(dve, s_v_hi, n)
                    dve.scalar_tensor_tensor(out=v32[:, :], in0=v_ps, scalar=1.0 / W_UP, in1=bvo[:, 0, :],
                                             op0=ALU.mult, op1=ALU.add).then_inc(s_v_sb, 1)
                    dve.wait_ge(s_qk_sb, n + 1)
                    swapped = qk[:, :].rearrange("p (h t j) -> p h t j", t=2, j=HD // 2)
                    b4 = rot_b[:, :].rearrange("p (h t j) -> p h t j", t=2, j=HD // 2)
                    for half in range(2):
                        a = dve.tensor_tensor(
                            b4[:, :, half, :], swapped[:, :, 1 - half, :],
                            rope[:, 1:2, half * 8:half * 8 + 8].broadcast_to([P, 2 * HEADS, 8]), ALU.mult)
                    a.then_inc(s_rot_sin, 1)
                if has(t):
                    maxima(t, 2)
                if has(t - 1):
                    n = t - 1
                    dve.wait_ge(s_attT_hi, n + 1)
                    low(attT[:, LO, :, :], T_ps[:, 0:D].rearrange("p (k q) -> p k q", k=K),
                        attT[:, HI, :, :], ATT_UP).then_inc(s_attT_lo, 1)
                if has(t):
                    p_low(t, 1)
                if has(t + 1):
                    n = t + 1
                    dve.wait_ge(s_v_hi, n + 1)
                    dve.tensor_tensor(V[:, 1 - par, LO, :, 0:HD],
                                      v32[:, :].rearrange("p (h d) -> p h d", d=HD),
                                      V[:, 1 - par, HI, :, 0:HD], ALU.subtract).then_inc(s_v_lo, 1)
                if has(t):
                    maxima(t, 3)
                if has(t - 1):
                    n = t - 1
                    dve.wait_ge(s_o_done, n + 1)
                    dve.wait_ge(s_xrb, n + 1)
                    need(dve, s_x1_out, 16 * (n - 1))
                    dve.scalar_tensor_tensor(out=x1[:, 1 - par, :], in0=o_ps, scalar=x_scale[:, 0:1],
                                             in1=x_res[:, 1 - par, :], op0=ALU.mult,
                                             op1=ALU.add).then_inc(s_x1_done, 1)
                    dve.wait_ge(s_x1_done, n + 1)
                    norm_stats(n, 1, x1[:, 1 - par, :], s_ln2_stat, s_ln2_mv, s_ln2_rstd)
                if has(t + 1):
                    n = t + 1
                    dve.wait_ge(s_rot_cos, n + 1)
                    dve.wait_ge(s_rot_sin, n + 1)
                    need(dve, s_qk_lo, n)
                    dve.tensor_tensor(qkr[:, :], rot_a[:, :], rot_b[:, :], ALU.add).then_inc(s_rot, 1)
                if has(t):
                    p_low(t, 2)
                if has(t - 1):
                    n = t - 1
                    dve.wait_ge(s_ln2_rstd, n + 1)
                    need(dve, s_hT_ps, n)
                    need(dve, s_h_hi, n)
                    norm_apply(h32[:, :], x1[:, 1 - par, :], 1).then_inc(s_h_sb, 1)
                if has(t + 1):
                    n = t + 1
                    dve.wait_ge(s_qk_hi, n + 1)
                    dve.tensor_tensor(QS[:, :, 1, :], qkr[:, 0:D].rearrange("p (a c) -> p a c", a=PAIRS),
                                      QS[:, :, 0, :], ALU.subtract)
                    k = qkr[:, D:2 * D].rearrange("p (a u c) -> p a u c", a=PAIRS, u=2)
                    for u in range(2):
                        a = dve.tensor_tensor(KS[:, :, u, 2, u, :], k[:, :, u, :], KS[:, :, u, 0, u, :],
                                              ALU.subtract)
                    a.then_inc(s_qk_lo, 1)
                if has(t + 2):
                    n = t + 2
                    dve.wait_ge(s_xT_hi, n + 1)
                    dve.tensor_tensor(xT[:, LO, :, :], T_ps[:, :].rearrange("p (k q) -> p k q", q=P),
                                      xT[:, HI, :, :], ALU.subtract).then_inc(s_xT_lo, 1)
                if has(t - 1):
                    n = t - 1
                    dve.wait_ge(s_h_hi, n + 1)
                    dve.tensor_tensor(keep["H"][:, n, LO, :], h32[:, :], keep["H"][:, n, HI, :],
                                      ALU.subtract).then_inc(s_h_lo, 1)
                if has(t + 3):
                    n = t + 3
                    dve.wait_ge(s_x_in_done, 16 * (n + 1))
                    norm_stats(n, 0, x_in[:, 1 - par, :], s_ln1_stat, s_ln1_mv, s_ln1_rstd)
                if has(t):
                    p_low(t, 3)
                if has(t - 1):
                    n = t - 1
                    dve.wait_ge(s_hT_hi, n + 1)
                    dve.tensor_tensor(hT[:, LO, :, :], T_ps[:, 0:D].rearrange("p (k q) -> p k q", k=K),
                                      hT[:, HI, :, :], ALU.subtract).then_inc(s_hT_lo, 1)
                if has(t + 3):
                    n = t + 3
                    dve.wait_ge(s_ln1_rstd, n + 1)
                    need(dve, s_xT_ps, n)
                    norm_apply(xn[:, :], x_in[:, 1 - par, :], 0).then_inc(s_xn_ready, 1)
                if has(t - 1):
                    n = t - 1
                    dve.wait_ge(s_r_exp, n + 1)
                    dve.tensor_scalar(r_d[:, :], r_e[:, :], 1.0, None, ALU.add).then_inc(s_r_one, 1)
                    dve.wait_ge(s_r_one, n + 1)
                    dve.reciprocal(r_r[:, :], r_d[:, :]).then_inc(s_r_rec, 1)
                    dve.wait_ge(s_r_rec, n + 1)
                    need(dve, s_a_lo, n)
                    dve.scalar_tensor_tensor(out=r_a[:, :], in0=r1_ps, scalar=1.0 / W_UP, in1=r_r[:, :],
                                             op0=ALU.mult, op1=ALU.mult).then_inc(s_r_act, 1)
                    dve.wait_ge(s_a_hi, n + 1)
                    dve.tensor_tensor(aT[:, LO, :], r_a[:, :], aT[:, HI, :], ALU.subtract).then_inc(s_a_lo, 1)

            slots(dve, step)

            dve.wait_ge(s_logit, NB)
            dve.wait_ge(s_zero_set, 4)
            ROUNDS = TOP // 8
            with dve.Fori(0, NB // GB) as g:
                dve.tensor_copy(Lg[:, :], L[:, :, :].rearrange("p (g b) e -> p g (b e)", b=GB)[:, g, :]).then_inc(s_tk_copy, 1)
                dve.wait_ge(s_tk_T, g + 1)
                dve.tensor_reduce(t_mx[:, :], S_ps[0][:, 0:P], AX_X, ALU.max).then_inc(s_tk_max, 1)
                dve.wait_ge(s_tk_max, g + 1)
                dve.tensor_scalar(t_nm[:, :], t_mx[:, :], -1.0, None, ALU.mult).then_inc(s_tk_neg, 1)
                dve.wait_ge(s_tk_exp, g + 1)
                dve.reciprocal(t_rs[:, :], t_sum[:, :]).then_inc(s_tk_rec, 1)
                dve.wait_ge(s_tk_rec, g + 1)
                dve.tensor_scalar(t_p[:, :], t_e[:, :], t_rs[:, 0:1], None, ALU.mult).then_inc(s_tk_p, 1)
                for r in range(ROUNDS):
                    src = t_p[:, :] if r == 0 else t_w[:, (r - 1) % 2, :]
                    if r:
                        dve.wait_ge(s_tk_rest, ROUNDS * g + r)
                    else:
                        dve.wait_ge(s_tk_p, g + 1)
                    tick()
                    dve.max(t_m8[:, :], src).then_inc(s_tk_top, 1)
                    dve.wait_ge(s_tk_top, ROUNDS * g + r + 1)
                    tick()
                    dve.match_replace(t_w[:, r % 2, :], t_m8[:, :], src, -1.0).then_inc(s_tk_rest, 1)
                dve.wait_ge(s_tk_rest, ROUNDS * (g + 1))
                dve.tensor_scalar(t_msk[:, :], t_w[:, (ROUNDS - 1) % 2, :], 0.0, None,
                                  ALU.is_lt).then_inc(s_tk_msk, 1)
                dve.wait_ge(s_tk_msk, g + 1)
                dve.tensor_tensor_scan(t_cum[:, :], t_msk[:, :], zeros[:, :], 0.0, ALU.add,
                                       ALU.add).then_inc(s_tk_cum, 1)
                dve.scalar_tensor_tensor(out=t_pm[:, :], in0=t_p[:, :], scalar=1.0, in1=t_msk[:, :],
                                         op0=ALU.mult, op1=ALU.mult,
                                         accum_out=t_ps[:, :]).then_inc(s_tk_sum, 1)
                dve.wait_ge(s_tk_sum, g + 1)
                dve.tensor_scalar(t_dn[:, :], t_ps[:, :], 1e-9, None, ALU.add).then_inc(s_tk_den, 1)
                dve.wait_ge(s_tk_den, g + 1)
                dve.reciprocal(t_rd[:, :], t_dn[:, :]).then_inc(s_tk_rden, 1)
                dve.wait_ge(s_tk_rden, g + 1)
                dve.tensor_tensor(t_wr[:, :], t_rd[:, :], w_scale[:, :], ALU.mult).then_inc(s_tk_wr, 1)
                dve.wait_ge(s_tk_wr, g + 1)
                dve.wait_ge(s_tk_cum, g + 1)
                dve.tensor_scalar(t_wt[:, :], t_pm[:, :], t_wr[:, 0:1], None, ALU.mult).then_inc(s_tk_res, 1)
                dve.tensor_tensor(t_pos[:, :], t_cum[:, :], t_msk[:, :], ALU.mult).then_inc(s_tk_res, 1)
                dve.wait_ge(s_tk_T2, g + 1)


def expert_phase(nc, io, keep, dims):
    NB, D, E, F = dims["NB"], dims["D"], dims["E"], dims["F"]
    K = D // P
    FC = F // P
    TILES = GB * TOP // P
    NG, NQ = NB // GB, (NB // GB) * (E // QE)
    NT = GB * TOP
    assert FC == 4 and TILES == 4 and K == 2 and NQ % 2 == 0
    ctx = ExitStack()
    with ctx:
        def sb(name, shape, dt=F32):
            return ctx.enter_context(nc.sbuf_tensor(name, shape, dt))

        def bank(name):
            return ctx.enter_context(nc.psum_tensor(name, [P, 512], F32))

        def sem(name):
            return ctx.enter_context(nc.semaphore(name))

        raw = [sb("w1_raw", [P, K, F]), sb("w2_raw", [P, K, F]), sb("w3_raw", [P, FC, D])]
        W1 = sb("W1", [P, 2, 2, K, F], F16)
        W2 = sb("W2", [P, 2, 2, K, F], F16)
        W3 = sb("W3", [P, 2, 2, FC, D], F16)
        parts = [W1, W2, W3]
        ident16 = sb("ident16b", [P, P], F16)
        identf = sb("identb", [P, P])
        pick = sb("pick", [P, 2, TILES, QE, 2, TOP], F16)
        X = sb("X", [P, 2, QE, 2, K, NT], F16)
        sg = sb("sg", [P, 2, NT])
        u32 = sb("u32", [P, 2, NT])
        U = sb("U", [P, 2, 2, FC, NT], F16)
        place = sb("place", [P, 2, TILES, 2, P], F16)
        Y = sb("Y", [P, 2, 2, D], F16)
        acc = sb("acc", [P, 2, GB, D])

        G_ps = [bank("G0_ps"), bank("G1_ps")]
        V_ps = [bank("V0_ps"), bank("V1_ps")]
        Y_ps = bank("Y_ps")
        S_ps = bank("Sc_ps")
        X_ps = bank("X_ps")
        place_ps = bank("place_ps")
        place16 = place_ps[:, 0:256].bitcast(F16).rearrange("p (t s) -> p t s", t=TILES)

        s_ident_in = sem("ident_in")
        s_ident_set = sem("ident_set")
        s_place_zero = sem("place_zero")
        s_acc_in = sem("acc_in")
        s_acc_out = sem("acc_out")
        s_pick_set = sem("pick_set")
        s_x_ps = sem("x_ps")
        s_x_sb = sem("x_sb")
        s_g_ps = sem("g_ps")
        s_v_ps = sem("v_ps")
        s_silu_done = sem("silu_done")
        s_u_done = sem("u_done")
        s_u_hi = sem("u_hi")
        s_u_lo = sem("u_lo")
        s_place_ps_done = sem("place_ps_done")
        s_place_sb = sem("place_sb")
        s_y_ps = sem("y_ps")
        s_y_hi = sem("y_hi")
        s_y_lo = sem("y_lo")
        s_sc_ps = sem("sc_ps")
        s_acc_done = sem("acc_done")
        w_in = [sem(f"w{i + 1}_in") for i in range(3)]
        w_hi = [sem(f"w{i + 1}_hi") for i in range(3)]
        w_lo = [sem(f"w{i + 1}_lo") for i in range(3)]

        block = ctx.enter_context(nc.Block())

        def lin(unit):
            return QE * unit[0] + unit[2]

        def before(unit):
            if unit is None:
                return None
            q, par, i = unit
            if i:
                return q, par, i - 1
            return None if isinstance(q, int) and q == 0 else (q - 1, 1 - par, QE - 1)

        def units(eng, step, tail):
            for i in range(QE):
                step((0, 0, i), True)
            with eng.Fori(0, (NQ - 2) // 2) as j:
                for k in range(2):
                    for i in range(QE):
                        step((2 * j + 1 + k, (1 + k) % 2, i), True)
            for i in range(QE):
                step((NQ - 1, (NQ - 1) % 2, i), False)
            tail((NQ - 1, (NQ - 1) % 2, QE - 1))

        def group_of(q):
            return q // (E // QE)

        @block.sync
        def _(sp):
            sp.dma_start(identf[:, :], io["ident"]).then_inc(s_ident_in, 16)
            src = [w.rearrange("e (c p) f -> e p c f", p=P) for w in (io["w1"], io["w2"], io["w3"])]

            def load(e, u):
                for m in range(3):
                    need(sp, w_hi[m], u)
                    need(sp, w_lo[m], u)
                    sp.dma_start(raw[m][:, :, :], src[m][e]).then_inc(w_in[m], 16)

            out_g = io["out"].rearrange("(g b) p d -> g p b d", b=GB)

            def acc_load(g):
                return sp.dma_start(acc[:, g % 2, :, :],
                                    out_g[g])

            def acc_store(g):
                return sp.dma_start(out_g[g],
                                    acc[:, g % 2, :, :])

            load(0, 0)
            acc_load(0).then_inc(s_acc_in, 16)
            for e in range(1, 8):
                load(e, e)
            if NG > 1:
                sp.wait_ge(s_acc_in, 16)
                acc_load(1).then_inc(s_acc_in, 16)
            for e in range(8, E):
                load(e, e)
            if NG > 2:
                with sp.Fori(1, NG - 1) as g:
                    with sp.Fori(0, 4) as e:
                        load(e, E * g + e)
                    sp.wait_ge(s_acc_done, TILES * E * g)
                    acc_store(g - 1).then_inc(s_acc_out, 16)
                    with sp.Fori(4, 8) as e:
                        load(e, E * g + e)
                    sp.wait_ge(s_acc_out, 16 * g)
                    sp.wait_ge(s_acc_in, 16 * (g + 1))
                    acc_load(g + 1).then_inc(s_acc_in, 16)
                    with sp.Fori(8, E) as e:
                        load(e, E * g + e)
            if NG > 1:
                for e in range(4):
                    load(e, E * (NG - 1) + e)
                sp.wait_ge(s_acc_done, TILES * E * (NG - 1))
                acc_store(NG - 2).then_inc(s_acc_out, 16)
                for e in range(4, E):
                    load(e, E * (NG - 1) + e)
            sp.wait_ge(s_acc_done, TILES * E * NG)
            acc_store(NG - 1).then_inc(s_acc_out, 16)
            sp.wait_ge(s_acc_out, 16 * NG)

        @block.tensor
        def _(pe):
            def gather(q, par, j):
                b, part = j // 2, j % 2
                pe.wait_ge(s_pick_set, 4 * q + b // 2 + 1)
                need(pe, s_x_sb, 16 * q + j)
                for k in range(K):
                    mm = pe.matmul(X_ps[:, 256 * k:256 * (k + 1)],
                                   keep["H"][:, GB * group_of(q) + b, part, k * P:(k + 1) * P],
                                   pick[:, par, b // 2, :, b % 2, :], start=True, stop=True)
                mm.then_inc(s_x_ps, 1)

            def up(unit, f):
                q, par, i = unit
                n = 4 * lin(unit) + f
                if f == 0:
                    if i == 0:
                        pe.wait_ge(s_x_sb, 16 * (q + 1))
                    pe.wait_ge(w_lo[0], lin(unit) + 1)
                need(pe, s_silu_done, n - 1)
                three_pass(pe, G_ps[f % 2][:, :], lambda a, k: W1[:, i % 2, a, k, f * P:(f + 1) * P],
                           lambda b, k: X[:, par, i, b, k, :], range(K)).then_inc(s_g_ps, 1)
                if f == 0:
                    pe.wait_ge(w_lo[1], lin(unit) + 1)
                need(pe, s_u_done, n - 1)
                three_pass(pe, V_ps[f % 2][:, :], lambda a, k: W2[:, i % 2, a, k, f * P:(f + 1) * P],
                           lambda b, k: X[:, par, i, b, k, :], range(K)).then_inc(s_v_ps, 1)

            def down(unit, t):
                i = unit[2]
                n = 4 * lin(unit) + t
                if t == 0:
                    pe.wait_ge(s_u_hi, 4 * lin(unit) + 4)
                    pe.wait_ge(s_u_lo, 4 * lin(unit) + 4)
                    pe.wait_ge(w_lo[2], lin(unit) + 1)
                need(pe, s_y_lo, n)
                three_pass(pe, Y_ps[:, 0:D],
                           lambda a, k: U[:, i % 2, a, k, t * P:(t + 1) * P],
                           lambda b, k: W3[:, i % 2, b, k, :], range(FC)).then_inc(s_y_ps, 1)

            def scatter(unit, t):
                i = unit[2]
                n = 4 * lin(unit) + t
                if t == 0:
                    pe.wait_ge(s_place_sb, 2 * (lin(unit) + 1))
                pe.wait_ge(s_y_lo, n + 1)
                need(pe, s_acc_done, n)
                for b in range(2):
                    for part in (HI, LO):
                        mm = pe.matmul(S_ps[:, D * b:D * (b + 1)], place[:, i % 2, t, b, :],
                                       Y[:, t % 2, part, :], start=(part == HI), stop=(part == LO),
                                       skip_group_check=True)
                mm.then_inc(s_sc_ps, 1)

            def turn_pick(unit, t):
                q, par, i = unit
                if t == 0:
                    need(pe, s_place_sb, 2 * lin(unit))
                mm = pe.transpose(place16[:, t, :], pick[:, par, t, i, :, :], ident16[:, :])
                if t == TILES - 1:
                    mm.then_inc(s_place_ps_done, 1)

            def step(unit, more):
                q, par, i = unit
                last, last2 = before(unit), before(before(unit))
                for f in range(FC):
                    up(unit, f)
                    if last:
                        down(last, f)
                    if f and last:
                        scatter(last, f - 1)
                    if f == 0 and last2:
                        scatter(last2, TILES - 1)
                    if more:
                        gather(q + 1, 1 - par, QE * i + f)
                    turn_pick(unit, f)

            def tail(unit):
                for t in range(TILES):
                    down(unit, t)
                    if t:
                        scatter(unit, t - 1)
                    else:
                        scatter(before(unit), TILES - 1)
                scatter(unit, TILES - 1)

            pe.wait_ge(s_ident_set, 1)
            for j in range(16):
                gather(0, 0, j)
            units(pe, step, tail)

        @block.scalar
        def _(act):
            def high(out, in_, scale=1.0):
                return act.activation(out, in_, ACT.Copy, scale=scale)

            def weights(m, unit):
                n, i = lin(unit), unit[2]
                act.wait_ge(w_in[m], 16 * (n + 1))
                need(act, [s_g_ps, s_v_ps, s_y_ps][m], 4 * (n - 1))
                high(parts[m][:, i % 2, HI, :, :], raw[m][:, :, :], W_UP).then_inc(w_hi[m], 1)

            def tokens(q, par, j):
                b, part = j // 2, j % 2
                act.wait_ge(s_x_ps, 16 * q + j + 1)
                need(act, s_v_ps, 16 * (q - 1))
                high(X[:, par, :, part, :, b * TOP:(b + 1) * TOP].rearrange("p e k c -> p k e c"),
                     X_ps[:, :].rearrange("p (k e c) -> p k e c", k=K, e=QE)).then_inc(s_x_sb, 1)

            def places(unit):
                n, i = lin(unit), unit[2]
                act.wait_ge(s_place_ps_done, n + 1)
                need(act, s_sc_ps, 4 * (n - 1))
                for b in range(2):
                    rows = slice(64 * b, 64 * b + 64)
                    high(place[rows, i % 2, :, b, :], place16[rows, :, :]).then_inc(s_place_sb, 1)

            def u_high(unit, f):
                n, i = 4 * lin(unit) + f, unit[2]
                act.wait_ge(s_u_done, n + 1)
                need(act, s_y_ps, 4 * (lin(unit) - 1))
                high(U[:, i % 2, HI, f, :], u32[:, f % 2, :]).then_inc(s_u_hi, 1)

            def y_high(unit, t):
                n = 4 * lin(unit) + t
                act.wait_ge(s_y_ps, n + 1)
                need(act, s_sc_ps, n - 1)
                high(Y[:, t % 2, HI, :], Y_ps[:, 0:D],
                     Y_DOWN / W_UP).then_inc(s_y_hi, 1)

            def step(unit, more):
                q, par, i = unit
                last = before(unit)
                for f in range(FC):
                    n = 4 * lin(unit) + f
                    act.wait_ge(s_g_ps, n + 1)
                    need(act, s_u_done, n - 1)
                    act.activation(sg[:, f % 2, :], G_ps[f % 2][:, :], ACT.Silu,
                                   scale=1.0 / W_UP).then_inc(s_silu_done, 1)
                    if f:
                        u_high(unit, f - 1)
                    if f == 0 and last:
                        places(last)
                    if last:
                        y_high(last, f)
                    if more:
                        tokens(q + 1, 1 - par, QE * i + f)
                    if f == 0:
                        weights(2, unit)
                    if f in (1, 2) and (more or i < QE - 1):
                        weights(f - 1, (q, par, i + 1) if i < QE - 1 else (q + 1, 1 - par, 0))
                u_high(unit, FC - 1)

            def tail(unit):
                places(unit)
                for t in range(TILES):
                    y_high(unit, t)

            act.wait_ge(s_ident_in, 16)
            high(ident16[:, :], identf[:, :]).then_inc(s_ident_set, 1)
            weights(0, (0, 0, 0))
            weights(1, (0, 0, 0))
            act.wait_ge(s_place_zero, 1)
            for j in range(16):
                tokens(0, 0, j)
            units(act, step, tail)

        @block.vector
        def _(dve):
            def low(out, in_, hi, scale):
                return dve.scalar_tensor_tensor(out=out, in0=in_, scalar=scale, in1=hi,
                                                op0=ALU.mult, op1=ALU.subtract)

            def weights(m, unit):
                n, i = lin(unit), unit[2]
                dve.wait_ge(w_hi[m], n + 1)
                low(parts[m][:, i % 2, LO, :, :], raw[m][:, :, :], parts[m][:, i % 2, HI, :, :],
                    W_UP).then_inc(w_lo[m], 1)

            def picks(q, par, b2):
                need(dve, s_place_ps_done, 4 * (q - 1))
                pos = keep["POS"][:, group_of(q), q % (E // QE), 2 * b2:2 * b2 + 2, :]
                dve.tensor_tensor(
                    pick[:, par, b2, :, :, :],
                    pos.rearrange("p b i -> p i b").unsqueeze(3).broadcast_to([P, QE, 2, TOP]),
                    keep["iota"][:, :].unsqueeze(1).unsqueeze(1).broadcast_to([P, QE, 2, TOP]),
                    ALU.is_equal).then_inc(s_pick_set, 1)

            def y_low(unit, t):
                n = 4 * lin(unit) + t
                dve.wait_ge(s_y_hi, n + 1)
                low(Y[:, t % 2, LO, :], Y_ps[:, 0:D], Y[:, t % 2, HI, :],
                    Y_DOWN / W_UP).then_inc(s_y_lo, 1)

            def add(unit, t):
                q, par, i = unit
                n = 4 * lin(unit) + t
                g = group_of(q)
                dve.wait_ge(s_sc_ps, n + 1)
                dve.wait_ge(s_acc_in, 16 * (g + 1))
                need(dve, s_acc_done, n - 3)
                for b in range(2):
                    tile = acc[:, g % 2, 2 * t + b, :]
                    a = dve.scalar_tensor_tensor(
                        out=tile, in0=S_ps[:, D * b:D * (b + 1)],
                        scalar=keep["WT"][:, g, q % (E // QE), i, 2 * t + b:2 * t + b + 1], in1=tile,
                        op0=ALU.mult, op1=ALU.add)
                a.then_inc(s_acc_done, 1)

            def step(unit, more):
                q, par, i = unit
                last, last2 = before(unit), before(before(unit))
                for f in range(FC):
                    n = 4 * lin(unit) + f
                    if f == 0 and more:
                        picks(q + 1, 1 - par, i)
                    dve.wait_ge(s_v_ps, n + 1)
                    dve.wait_ge(s_silu_done, n + 1)
                    need(dve, s_u_hi, n - 1)
                    need(dve, s_u_lo, n - 1)
                    dve.scalar_tensor_tensor(out=u32[:, f % 2, :], in0=V_ps[f % 2][:, :],
                                             scalar=1.0 / W_UP, in1=sg[:, f % 2, :], op0=ALU.mult,
                                             op1=ALU.mult).then_inc(s_u_done, 1)
                    if last:
                        y_low(last, f)
                    if f and last:
                        add(last, f - 1)
                    if f == 0 and last2:
                        add(last2, TILES - 1)
                    if f == 0:
                        weights(2, unit)
                    if f in (1, 2) and (more or i < QE - 1):
                        weights(f - 1, (q, par, i + 1) if i < QE - 1 else (q + 1, 1 - par, 0))

            def tail(unit):
                for t in range(TILES):
                    y_low(unit, t)
                    if t:
                        add(unit, t - 1)
                    else:
                        add(before(unit), TILES - 1)
                add(unit, TILES - 1)

            weights(0, (0, 0, 0))
            weights(1, (0, 0, 0))
            for b2 in range(4):
                picks(0, 0, b2)
            units(dve, step, tail)

        @block.gpsimd
        def _(pool):
            pool.memset(place[:, :, :, :, :], 0.0).then_inc(s_place_zero, 1)

            def step(unit, more):
                q, par, i = unit
                for f in range(FC):
                    n = 4 * lin(unit) + f
                    pool.wait_ge(s_u_hi, n + 1)
                    pool.tensor_tensor(U[:, i % 2, LO, f, :], u32[:, f % 2, :], U[:, i % 2, HI, f, :],
                                       ALU.subtract).then_inc(s_u_lo, 1)

            units(pool, step, lambda unit: None)


def flamingo_kernel(nc, io):
    NB, S, D = io["x"].shape
    E, _, F = io["w1"].shape
    dims = dict(NB=NB, D=D, E=E, F=F, RH=io["rw1"].shape[1])
    assert S == P and D == HEADS * HD and dims["RH"] == P and E * GB == P and NB % GB == 0
    with ExitStack() as ctx:
        keep = dict(
            H=ctx.enter_context(nc.sbuf_tensor("H", [P, NB, 2, D], F16)),
            POS=ctx.enter_context(nc.sbuf_tensor("POS", [P, NB // GB, E // QE, GB, QE], F16)),
            WT=ctx.enter_context(nc.sbuf_tensor("WT", [P, NB // GB, E // QE, QE, GB], F32)),
            iota=ctx.enter_context(nc.sbuf_tensor("iota", [P, TOP], F32)),
        )
        attention_phase(nc, io, keep, dims)
        expert_phase(nc, io, keep, dims)


_INS = {
    'x': 'x', 'ctx_1024': 'ctx', 'g_xattn': 'g_xattn', 'g_ffn': 'g_ffn',
    'L0_xattn_Wq': 'Wq', 'L0_xattn_bq': 'bq', 'L0_xattn_Wk': 'Wk', 'L0_xattn_bk': 'bk',
    'L0_xattn_Wv': 'Wv', 'L0_xattn_bv': 'bv', 'L0_xattn_Wo': 'Wo', 'L0_xattn_bo': 'bo',
    'L0_ffn_router_w1': 'rw1', 'L0_ffn_router_w2': 'rw2',
    'L0_ffn_w1': 'w1', 'L0_ffn_w2': 'w2', 'L0_ffn_w3': 'w3',
}


def _constants():
    import numpy as np
    inv_freq = (1.0 / 10000.0 ** (np.arange(0, HD, 2, dtype=np.float32) / HD)).astype(np.float32)
    freqs = np.arange(P, dtype=np.float32)[:, None] * inv_freq[None, :]
    cos, sin = np.cos(freqs), np.sin(freqs)
    return {
        'ident': np.eye(P, dtype=np.float32),
        'rope': np.concatenate([cos, cos, -sin, sin], axis=1).astype(np.float32),
        'iota': np.tile(np.arange(1, TOP + 1, dtype=np.float32), (P, 1)),
    }


def kernel(**inputs):
    import numpy as _np
    import concourse.bacc as _bacc
    from concourse import mybir as _mybir
    from concourse.bass_utils import run_bass_kernel_spmd as _run

    nc = _bacc.Bacc("TRN2", target_bir_lowering=False, num_devices=1)
    arrays, aps = {}, {}
    for name, short in _INS.items():
        arrays[f"in_{short}_dram"] = _np.ascontiguousarray(inputs[name])
    for short, a in _constants().items():
        arrays[f"in_{short}_dram"] = a
    for key, a in arrays.items():
        aps[key[3:-5]] = nc.dram_tensor(key, a.shape, _mybir.dt.from_np(a.dtype), kind="ExternalInput").ap()
    shape = arrays["in_x_dram"].shape
    aps["out"] = nc.dram_tensor("out_0_dram", shape, _mybir.dt.float32, kind="ExternalOutput").ap()
    flamingo_kernel(nc, aps)
    r = _run(nc, [arrays], core_ids=[0])
    return r.results[0]["out_0_dram"]
```

```python
from contextlib import ExitStack

import concourse.bass as bass
from concourse import mybir

F32 = mybir.dt.float32
F16 = mybir.dt.float16
ALU = mybir.AluOpType
ACT = mybir.ActivationFunctionType
AX_X = mybir.AxisListType.X

P = 128
HEADS = 16
HD = 16
PAIRS = HEADS // 2
CHUNKS = 4
TOP = 64
GB = 8
QE = 4
LN_EPS = 1e-5
W_UP = 64.0
ATT_UP = 16.0
Y_DOWN = 1.0 / 64
HI, LO = 0, 1


def need(engine, semaphore, value):
    if isinstance(value, int) and value <= 0:
        return
    engine.wait_ge(semaphore, value)


def three_pass(eng, out, stationary, moving, ks, first=True, last=True):
    todo = [(k, a, b) for k in ks for a, b in ((HI, HI), (HI, LO), (LO, HI))]
    for n, (k, a, b) in enumerate(todo):
        mm = eng.matmul(out, stationary(a, k), moving(b, k), start=(first and n == 0),
                        stop=(last and n == len(todo) - 1), skip_group_check=True)
    return mm


def attention_phase(nc, io, keep, dims):
    NB, D, E, RH = dims["NB"], dims["D"], dims["E"], dims["RH"]
    K = D // P
    ctx = ExitStack()
    with ctx:
        def sb(name, shape, dt=F32):
            return ctx.enter_context(nc.sbuf_tensor(name, shape, dt))

        def bank(name):
            return ctx.enter_context(nc.psum_tensor(name, [P, 512], F32))

        def sem(name):
            return ctx.enter_context(nc.semaphore(name))

        ident = sb("ident", [P, P])
        ident16 = keep["ident16"]
        rope = sb("rope", [P, 2, 2, HD])
        w_raw = sb("w_raw", [P, 4, K, D])
        WT4 = sb("WT4", [P, 4, 2, K, D], F16)
        rw1_raw = sb("rw1_raw", [P, K, RH])
        rw1 = sb("rw1", [P, 2, K, RH], F16)
        rw2_raw = sb("rw2_raw", [P, E])
        rw2 = sb("rw2", [P, 2, E], F16)
        bqk = sb("bqk", [P, 2, D])
        bvo = sb("bvo", [P, 2, D])
        gates = sb("gates", [P, 2])
        tanh_g = sb("tanh_g", [P, 2])
        x_scale = sb("x_scale", [P, 1])
        w_scale = sb("w_scale", [P, 1])
        bo_g = sb("bo_g", [P, D])
        eps = sb("eps", [P, 1])
        minus_half = sb("minus_half", [P, 1])
        zeros = sb("zeros", [P, P])

        x_in = sb("x_in", [P, 2, D])
        c_in = sb("c_in", [P, 2, D])
        x_res = sb("x_res", [P, 2, D])
        ln_st = sb("ln_st", [P, 2, 6])
        ln_mv = sb("ln_mv", [P, 2, 2])
        ln_ve = sb("ln_ve", [P, 2])
        ln_rs = sb("ln_rs", [P, 2])
        xn = sb("xn", [P, D])
        xT = sb("xT", [P, 2, 2, 2 * K, P], F16)
        qk = sb("qk", [P, 2 * D])
        rot_a = sb("rot_a", [P, 2 * D])
        rot_b = sb("rot_b", [P, 2 * D])
        qkr = sb("qkr", [P, 2 * D])
        QS = sb("QS", [P, PAIRS, 3, 32], F16)
        KS = sb("KS", [P, PAIRS, 2, 3, 2, HD], F16)
        QT = sb("QT", [96, 2, PAIRS, P], F16)
        KT = sb("KT", [96, 2, HEADS, P], F16)
        v32 = sb("v32", [P, D])
        V = sb("V", [P, 2, 2, HEADS, HD + 1], F16)
        mn = sb("mn", [P, 2, 4])
        Pr = sb("Pr", [P, 2, 4, P])
        PT = sb("PT", [P, 2, 2, 4, P], F16)
        den = sb("den", [P, HEADS])
        att = sb("att", [P, HEADS, HD])
        attT = sb("attT", [P, 2, K, P], F16)
        x1 = sb("x1", [P, 2, D])
        h32 = sb("h32", [P, D])
        hT = sb("hT", [P, 2, K, P], F16)
        r_e = sb("r_e", [P, P])
        r_z = sb("r_z", [P, P])
        r_d = sb("r_d", [P, P])
        r_r = sb("r_r", [P, P])
        r_a = sb("r_a", [P, P])
        aT = sb("aT", [P, 2, P], F16)
        L = sb("L", [P, NB, E])

        Lg = sb("Lg", [P, P])
        t_mx = sb("t_mx", [P, 1])
        t_nm = sb("t_nm", [P, 1])
        t_e = sb("t_e", [P, P])
        t_sum = sb("t_sum", [P, 1])
        t_rs = sb("t_rs", [P, 1])
        t_p = sb("t_p", [P, P])
        t_w = sb("t_w", [P, 2, P])
        t_m8 = sb("t_m8", [P, 8])
        t_msk = sb("t_msk", [P, P])
        t_pm = sb("t_pm", [P, P])
        t_ps = sb("t_ps", [P, 1])
        t_dn = sb("t_dn", [P, 1])
        t_rd = sb("t_rd", [P, 1])
        t_wr = sb("t_wr", [P, 1])
        t_wt = sb("t_wt", [P, P])
        t_cum = sb("t_cum", [P, P])
        t_pos = sb("t_pos", [P, P])
        spare = sb("spare", [P, 1])

        S_ps = [bank("S0_ps"), bank("S1_ps")]
        PT_ps = [bank("PT0_ps"), bank("PT1_ps")]
        qk_bank = bank("qk_bank")
        small = bank("small_ps")
        vo_bank = bank("vo_bank")
        T_ps = bank("T_ps")
        att_ps = small[:, 0:HEADS * (HD + 1)].rearrange("p (h d) -> p h d", d=HD + 1)
        r1_ps = qk_bank[:, 0:P]
        r2_ps = small[:, 400:400 + E]
        v_ps = vo_bank[:, 0:D]
        o_ps = vo_bank[:, D:2 * D]
        fill_a = vo_bank[:, :].bitcast(F16).rearrange("p (h s) -> p h s", s=P)
        fill_b = qk_bank[:, :].bitcast(F16).rearrange("p (h s) -> p h s", s=P)

        s_const_in = sem("const_in")
        s_w_in = sem("w_in")
        s_zero_set = sem("zero_set")
        s_ident16_set = sem("ident16_set")
        s_v_ones = sem("v_ones")
        s_wT_ps = sem("wT_ps")
        s_wT_hi = sem("wT_hi")
        s_wT_lo = sem("wT_lo")
        s_rw_hi = sem("rw_hi")
        s_rw_lo = sem("rw_lo")
        s_tanh_done = sem("tanh_done")
        s_scales_set = sem("scales_set")
        s_x_in_done = sem("x_in_done")
        s_c_in_done = sem("c_in_done")
        s_xr_in = sem("xr_in")
        s_ln1_stat = sem("ln1_stat")
        s_ln1_mv = sem("ln1_mv")
        s_ln1_ve = sem("ln1_ve")
        s_ln1_rstd = sem("ln1_rstd")
        s_xn_ready = sem("xn_ready")
        s_xT_ps = sem("xT_ps")
        s_xT_hi = sem("xT_hi")
        s_xT_lo = sem("xT_lo")
        s_qk_ps = sem("qk_ps")
        s_v_done_ps = sem("v_done_ps")
        s_qk_sb = sem("qk_sb")
        s_v_sb = sem("v_sb")
        s_v_hi = sem("v_hi")
        s_v_lo = sem("v_lo")
        s_rot_cos = sem("rot_cos")
        s_rot_sin = sem("rot_sin")
        s_rot = sem("rot")
        s_qk_hi = sem("qk_hi")
        s_qk_lo = sem("qk_lo")
        s_qkT_ps = sem("qkT_ps")
        s_qkT_sb = sem("qkT_sb")
        s_scores = sem("scores")
        s_min_done = sem("min_done")
        s_exp_done = sem("exp_done")
        s_p_T = sem("p_T")
        s_p_hi = sem("p_hi")
        s_p_lo = sem("p_lo")
        s_pv = sem("pv")
        s_recip_den = sem("recip_den")
        s_att_sb = sem("att_sb")
        s_att_T = sem("att_T")
        s_attT_hi = sem("attT_hi")
        s_attT_lo = sem("attT_lo")
        s_o_done = sem("o_done")
        s_xrb = sem("xrb")
        s_x1_done = sem("x1_done")
        s_x1_out = sem("x1_out")
        s_ln2_stat = sem("ln2_stat")
        s_ln2_mv = sem("ln2_mv")
        s_ln2_ve = sem("ln2_ve")
        s_ln2_rstd = sem("ln2_rstd")
        s_h_sb = sem("h_sb")
        s_h_hi = sem("h_hi")
        s_h_lo = sem("h_lo")
        s_hT_ps = sem("hT_ps")
        s_hT_hi = sem("hT_hi")
        s_hT_lo = sem("hT_lo")
        s_r1 = sem("r1")
        s_r_exp = sem("r_exp")
        s_r_one = sem("r_one")
        s_r_rec = sem("r_rec")
        s_r_act = sem("r_act")
        s_a_hi = sem("a_hi")
        s_a_lo = sem("a_lo")
        s_r2 = sem("r2")
        s_logit = sem("logit")
        s_tk_copy = sem("tk_copy")
        s_tk_T = sem("tk_T")
        s_tk_max = sem("tk_max")
        s_tk_neg = sem("tk_neg")
        s_tk_exp = sem("tk_exp")
        s_tk_rec = sem("tk_rec")
        s_tk_p = sem("tk_p")
        s_tk_top = sem("tk_top")
        s_tk_rest = sem("tk_rest")
        s_tk_msk = sem("tk_msk")
        s_tk_sum = sem("tk_sum")
        s_tk_den = sem("tk_den")
        s_tk_rden = sem("tk_rden")
        s_tk_wr = sem("tk_wr")
        s_tk_cum = sem("tk_cum")
        s_tk_res = sem("tk_res")
        s_tk_T2 = sem("tk_T2")
        s_tk_pos = sem("tk_pos")
        s_tk_wt = sem("tk_wt")
        CONST_IN = 16 * 3
        W_IN = 16 * 12

        FIRST, LAST = -4, NB + 4
        LOOP_FROM, LOOP_TO = 5, NB - 6

        def slots(eng, step):
            for t in range(FIRST, LOOP_FROM):
                step(t, t % 2)
            with eng.Fori(0, (LOOP_TO - LOOP_FROM + 1) // 2) as j:
                for k in range(2):
                    step(2 * j + (LOOP_FROM + k), (LOOP_FROM + k) % 2)
            for t in range(LOOP_TO + 1, LAST):
                step(t, t % 2)

        def has(n):
            return not isinstance(n, int) or 0 <= n < NB

        def upto(n):
            return min(n, NB) if isinstance(n, int) else n

        block = ctx.enter_context(nc.Block())

        @block.sync
        def _(sp):
            sp.dma_start(ident[:, :], io["ident"]).then_inc(s_const_in, 16)
            sp.dma_start(rope[:, :, :, :], io["rope"].rearrange("p (c a j) -> p c a j", c=2, a=2)).then_inc(s_const_in, 16)
            sp.dma_start(keep["iota"][:, :], io["iota"]).then_inc(s_const_in, 16)
            for i, w in enumerate((io["Wq"], io["Wk"], io["Wv"], io["Wo"])):
                sp.dma_start(w_raw[:, i, :, :], w.rearrange("(c p) d -> p c d", p=P)).then_inc(s_w_in, 16)
            sp.dma_start(rw1_raw[:, :, :], io["rw1"].rearrange("(c p) h -> p c h", p=P)).then_inc(s_w_in, 16)
            sp.dma_start(rw2_raw[:, :], io["rw2"]).then_inc(s_w_in, 16)
            for i, b in enumerate((io["bq"], io["bk"])):
                sp.dma_start(bqk[:, i, :], b.partition_broadcast(P)).then_inc(s_w_in, 16)
            for i, b in enumerate((io["bv"], io["bo"])):
                sp.dma_start(bvo[:, i, :], b.partition_broadcast(P)).then_inc(s_w_in, 16)
            for i, g in enumerate((io["g_xattn"], io["g_ffn"])):
                sp.dma_start(gates[:, i:i + 1], g.partition_broadcast(P)).then_inc(s_w_in, 16)

            def step(t, par):
                if has(t + 5):
                    n = t + 5
                    need(sp, s_xn_ready, n - 1)
                    sp.wait_ge(s_x_in_done, 16 * n)
                    sp.dma_start(x_in[:, 1 - par, :], io["x"][n]).then_inc(s_x_in_done, 16)
                    need(sp, s_xT_ps, n - 1)
                    sp.wait_ge(s_c_in_done, 16 * n)
                    sp.dma_start(c_in[:, 1 - par, :], io["ctx"][n]).then_inc(s_c_in_done, 16)
                if has(t):
                    need(sp, s_x1_done, t - 1)
                    need(sp, s_xr_in, 16 * t)
                    sp.dma_start(x_res[:, par, :], io["x"][t]).then_inc(s_xr_in, 16)
                if has(t - 2):
                    need(sp, s_x1_out, 16 * (t - 2))
                    sp.wait_ge(s_x1_done, t - 1)
                    sp.dma_start(io["out"][t - 2], x1[:, par, :]).then_inc(s_x1_out, 16)

            sp.dma_start(x_in[:, 0, :], io["x"][0]).then_inc(s_x_in_done, 16)
            sp.dma_start(c_in[:, 0, :], io["ctx"][0]).then_inc(s_c_in_done, 16)
            slots(sp, step)
            sp.wait_ge(s_x1_out, 16 * NB)

        @block.gpsimd
        def _(pool):
            pool.memset(KS[:, :, :, :, :, :], 0.0).then_inc(s_zero_set, 1)
            pool.memset(V[:, :, HI, :, HD:HD + 1], 1.0).then_inc(s_v_ones, 1)
            pool.memset(V[:, :, LO, :, HD:HD + 1], 0.0).then_inc(s_v_ones, 1)
            pool.memset(eps[:, :], LN_EPS).then_inc(s_zero_set, 1)
            pool.memset(minus_half[:, :], -0.5).then_inc(s_zero_set, 1)
            pool.memset(zeros[:, :], 0.0).then_inc(s_zero_set, 1)
            pool.wait_ge(s_zero_set, 4)
            pool.wait_ge(s_scales_set, 3)

            def rstd(n, which, mv, ve, rs, used):
                pool.wait_ge(mv, n + 1)
                pool.tensor_tensor(ln_ve[:, which:which + 1], ln_mv[:, which, 1:2], eps[:, :],
                                   ALU.add).then_inc(ve, 1)
                pool.wait_ge(ve, n + 1)
                need(pool, used, n)
                pool.tensor_tensor(ln_rs[:, which:which + 1], ln_ve[:, which:which + 1],
                                   minus_half[:, :], ALU.pow).then_inc(rs, 1)

            def split(a):
                return a.rearrange("p (c h j) -> p c h j", c=2, j=HD)

            def step(t, par):
                if has(t + 1):
                    n = t + 1
                    pool.wait_ge(s_qk_hi, n + 1)
                    pool.tensor_tensor(QS[:, :, 1, :], qkr[:, 0:D].rearrange("p (a c) -> p a c", a=PAIRS),
                                       QS[:, :, 0, :], ALU.subtract)
                    k = qkr[:, D:2 * D].rearrange("p (a u c) -> p a u c", a=PAIRS, u=2)
                    for u in range(2):
                        a = pool.tensor_tensor(KS[:, :, u, 2, u, :], k[:, :, u, :], KS[:, :, u, 0, u, :],
                                               ALU.subtract)
                    a.then_inc(s_qk_lo, 1)
                if has(t + 1):
                    n = t + 1
                    pool.wait_ge(s_v_hi, n + 1)
                    pool.tensor_tensor(V[:, 1 - par, LO, :, 0:HD],
                                       v32[:, :].rearrange("p (h d) -> p h d", d=HD),
                                       V[:, 1 - par, HI, :, 0:HD], ALU.subtract).then_inc(s_v_lo, 1)
                if has(t - 1):
                    n = t - 1
                    pool.wait_ge(s_xr_in, 16 * (n + 1))
                    pool.tensor_tensor(x_res[:, 1 - par, :], x_res[:, 1 - par, :], bo_g[:, :],
                                       ALU.add).then_inc(s_xrb, 1)
                if has(t + 4):
                    rstd(t + 4, 0, s_ln1_mv, s_ln1_ve, s_ln1_rstd, s_xn_ready)
                if has(t + 2):
                    n = t + 2
                    pool.wait_ge(s_qk_sb, n + 1)
                    pool.tensor_tensor(
                        split(rot_a[:, :]), split(qk[:, :]),
                        rope[:, 0, :, :].unsqueeze(2).broadcast_to([P, 2, HEADS, HD]),
                        ALU.mult).then_inc(s_rot_cos, 1)
                    pool.wait_ge(s_rot_cos, n + 1)
                    pool.wait_ge(s_rot_sin, n + 1)
                    need(pool, s_qk_hi, n)
                    pool.tensor_tensor(qkr[:, :], rot_a[:, :], rot_b[:, :], ALU.add).then_inc(s_rot, 1)
                if has(t - 2):
                    n = t - 2
                    pool.wait_ge(s_h_hi, n + 1)
                    pool.tensor_tensor(keep["H"][:, n, LO, :], h32[:, :], keep["H"][:, n, HI, :],
                                       ALU.subtract).then_inc(s_h_lo, 1)
                if has(t - 1):
                    rstd(t - 1, 1, s_ln2_mv, s_ln2_ve, s_ln2_rstd, s_h_sb)

            slots(pool, step)

        @block.tensor
        def _(pe):
            pe.wait_ge(s_const_in, CONST_IN)
            pe.wait_ge(s_w_in, W_IN)
            for w in range(4):
                dst = [*S_ps, *PT_ps][w]
                for k in range(K):
                    for c in range(K):
                        mm = pe.transpose(dst[:, (k * K + c) * P:(k * K + c + 1) * P],
                                          w_raw[:, w, c, k * P:(k + 1) * P], ident[:, :])
                mm.then_inc(s_wT_ps, 1)
            pe.wait_ge(s_wT_lo, 4)
            pe.wait_ge(s_rw_lo, 2)
            pe.wait_ge(s_ident16_set, 1)
            pe.wait_ge(s_v_ones, 2)

            def scores(n, c, par):
                g = 4 * n + c
                if c == 0:
                    pe.wait_ge(s_qkT_sb, 3 * n + 2)
                if c == 2:
                    pe.wait_ge(s_qkT_sb, 3 * n + 3)
                need(pe, s_exp_done, g - 1)
                for u in range(2):
                    mm = pe.matmul(S_ps[c % 2][:, 2 * P * u:2 * P * (u + 1)], QT[:, par, 2 * c + u, :],
                                   KT[:, par, 4 * c + 2 * u:4 * c + 2 * u + 2, :], start=True, stop=True)
                mm.then_inc(s_scores, 1)

            def turn_p(n, c):
                g = 4 * n + c
                pe.wait_ge(s_exp_done, g + 1)
                need(pe, s_p_lo, g - 1)
                for h in range(4):
                    mm = pe.transpose(PT_ps[c % 2][:, h * P:(h + 1) * P], Pr[:, c % 2, h, :], ident[:, :])
                mm.then_inc(s_p_T, 1)

            def weigh_v(n, c, par):
                g = 4 * n + c
                if c == 0:
                    pe.wait_ge(s_v_lo, n + 1)
                    need(pe, s_att_sb, n)
                    need(pe, s_logit, n - 3)
                pe.wait_ge(s_p_lo, g + 1)
                for hh in range(4):
                    h = 4 * c + hh
                    mm = three_pass(pe, att_ps[:, h, :], lambda a, k: PT[:, c % 2, a, hh, :],
                                    lambda b, k: V[:, par, b, h, :], [0])
                mm.then_inc(s_pv, 1)

            def project_qk(n, par):
                pe.wait_ge(s_xT_lo, n + 1)
                need(pe, s_qkT_sb, 3 * n - 1)
                three_pass(pe, qk_bank[:, 0:D], lambda a, k: xT[:, par, a, k, :],
                           lambda b, k: WT4[:, 0, b, k, :], range(K))
                three_pass(pe, qk_bank[:, D:2 * D], lambda a, k: xT[:, par, a, K + k, :],
                           lambda b, k: WT4[:, 1, b, k, :], range(K)).then_inc(s_qk_ps, 1)

            def project_v(n, par):
                need(pe, s_qkT_sb, 3 * n)
                need(pe, s_x1_done, n - 2)
                three_pass(pe, v_ps, lambda a, k: xT[:, par, a, K + k, :],
                           lambda b, k: WT4[:, 2, b, k, :], range(K)).then_inc(s_v_done_ps, 1)

            def turn_att(n):
                pe.wait_ge(s_att_sb, n + 1)
                need(pe, s_xT_lo, upto(n + 4))
                need(pe, s_hT_lo, n - 1)
                need(pe, s_attT_lo, n)
                for k in range(K):
                    mm = pe.transpose(T_ps[:, k * P:(k + 1) * P], att[:, 8 * k:8 * k + 8, :], ident[:, :])
                mm.then_inc(s_att_T, 1)

            def turn_h(n):
                pe.wait_ge(s_h_sb, n + 1)
                need(pe, s_attT_lo, upto(n + 2))
                need(pe, s_xT_lo, upto(n + 5))
                need(pe, s_hT_lo, n)
                for k in range(K):
                    mm = pe.transpose(T_ps[:, k * P:(k + 1) * P], h32[:, k * P:(k + 1) * P], ident[:, :])
                mm.then_inc(s_hT_ps, 1)

            def turn_x(n, par):
                pe.wait_ge(s_xn_ready, n + 1)
                pe.wait_ge(s_c_in_done, 16 * (n + 1))
                need(pe, s_hT_lo, n - 4)
                need(pe, s_attT_lo, n - 3)
                need(pe, s_xT_lo, n)
                for k in range(K):
                    pe.transpose(T_ps[:, k * P:(k + 1) * P], xn[:, k * P:(k + 1) * P], ident[:, :])
                for k in range(K):
                    mm = pe.transpose(T_ps[:, (K + k) * P:(K + k + 1) * P],
                                      c_in[:, par, k * P:(k + 1) * P], ident[:, :])
                mm.then_inc(s_xT_ps, 1)

            def project_out(n):
                pe.wait_ge(s_attT_lo, n + 1)
                need(pe, s_qkT_sb, 3 * upto(n + 3))
                need(pe, s_x1_done, n)
                three_pass(pe, o_ps, lambda a, k: attT[:, a, k, :],
                           lambda b, k: WT4[:, 3, b, k, :], range(K)).then_inc(s_o_done, 1)

            def turn_q_k0(n):
                pe.wait_ge(s_qk_lo, n + 1)
                pe.wait_ge(s_v_sb, n + 1)
                for p in range(PAIRS):
                    mm = pe.transpose(fill_a[0:96, p, :], QS[:, p, :, :], ident16[:, :])
                mm.then_inc(s_qkT_ps, 1)
                need(pe, s_r_exp, n - 3)
                for h in range(HEADS // 2):
                    mm = pe.transpose(fill_b[0:96, h, :], KS[:, h // 2, h % 2, :, :, :], ident16[:, :])
                mm.then_inc(s_qkT_ps, 1)

            def turn_k1(n):
                pe.wait_ge(s_qkT_sb, 3 * n + 1)
                for h in range(HEADS // 2, HEADS):
                    mm = pe.transpose(fill_a[0:96, h - HEADS // 2, :], KS[:, h // 2, h % 2, :, :, :],
                                      ident16[:, :])
                mm.then_inc(s_qkT_ps, 1)

            def route_1(n):
                pe.wait_ge(s_hT_lo, n + 1)
                pe.wait_ge(s_qk_sb, upto(n + 5))
                pe.wait_ge(s_qkT_sb, 3 * upto(n + 4))
                need(pe, s_r_exp, n)
                three_pass(pe, r1_ps, lambda a, k: rw1[:, a, k, :],
                           lambda b, k: hT[:, b, k, :], range(K)).then_inc(s_r1, 1)

            def route_2(n):
                pe.wait_ge(s_a_lo, n + 1)
                need(pe, s_logit, n)
                need(pe, s_att_sb, upto(n + 3))
                three_pass(pe, r2_ps, lambda a, k: aT[:, a, :],
                           lambda b, k: rw2[:, b, :], [0]).then_inc(s_r2, 1)

            def step(t, par):
                if has(t - 1):
                    weigh_v(t - 1, 3, 1 - par)
                if has(t):
                    turn_p(t, 0)
                if has(t + 1):
                    turn_q_k0(t + 1)
                if has(t):
                    scores(t, 2, par)
                if has(t - 1):
                    turn_att(t - 1)
                if has(t):
                    weigh_v(t, 0, par)
                    scores(t, 3, par)
                    turn_p(t, 1)
                if has(t + 1):
                    turn_k1(t + 1)
                if has(t + 2):
                    project_qk(t + 2, par)
                if has(t - 2):
                    turn_h(t - 2)
                if has(t - 1):
                    project_out(t - 1)
                if has(t):
                    weigh_v(t, 1, par)
                if has(t + 1):
                    scores(t + 1, 0, 1 - par)
                if has(t):
                    turn_p(t, 2)
                if has(t + 3):
                    turn_x(t + 3, 1 - par)
                if has(t):
                    turn_p(t, 3)
                if has(t - 2):
                    route_1(t - 2)
                if has(t):
                    weigh_v(t, 2, par)
                if has(t + 2):
                    project_v(t + 2, par)
                if has(t - 3):
                    route_2(t - 3)
                if has(t + 1):
                    scores(t + 1, 1, 1 - par)

            slots(pe, step)

            with pe.Fori(0, NB // GB) as g:
                pe.wait_ge(s_tk_copy, g + 1)
                pe.transpose(S_ps[0][:, 0:P], Lg[:, :], ident[:, :]).then_inc(s_tk_T, 1)
                pe.wait_ge(s_tk_res, 2 * (g + 1))
                pe.transpose(S_ps[1][:, 0:P], t_pos[:, :], ident[:, :])
                pe.transpose(S_ps[1][:, P:2 * P], t_wt[:, :], ident[:, :]).then_inc(s_tk_T2, 1)
                pe.wait_ge(s_tk_pos, g + 1)
                pe.wait_ge(s_tk_wt, g + 1)

        @block.scalar
        def _(act):
            def high(out, in_, scale=1.0):
                return act.activation(out, in_, ACT.Copy, scale=scale)

            act.wait_ge(s_w_in, W_IN)
            act.activation(tanh_g[:, :], gates[:, :], ACT.Tanh).then_inc(s_tanh_done, 1)
            for w in range(4):
                act.wait_ge(s_wT_ps, w + 1)
                high(WT4[:, w, HI, :, :], [*S_ps, *PT_ps][w][:, :], W_UP).then_inc(s_wT_hi, 1)
            high(rw1[:, HI, :, :], rw1_raw[:, :, :], W_UP).then_inc(s_rw_hi, 1)
            high(rw2[:, HI, :], rw2_raw[:, :], W_UP).then_inc(s_rw_hi, 1)
            act.wait_ge(s_const_in, CONST_IN)
            high(ident16[:, :], ident[:, :]).then_inc(s_ident16_set, 1)
            act.wait_ge(s_zero_set, 4)
            act.wait_ge(s_v_ones, 2)

            def exps(n, c):
                g = 4 * n + c
                act.wait_ge(s_min_done, g + 1)
                need(act, s_p_T, g - 1)
                for h in range(4):
                    a = act.activation(Pr[:, c % 2, h, :], S_ps[c % 2][:, h * P:(h + 1) * P], ACT.Exp,
                                       bias=mn[:, c % 2, h:h + 1], scale=-1.0)
                a.then_inc(s_exp_done, 1)

            def p_high(n, c):
                g = 4 * n + c
                act.wait_ge(s_p_T, g + 1)
                need(act, s_pv, g - 1)
                high(PT[:, c % 2, HI, :, :], PT_ps[c % 2][:, :]).then_inc(s_p_hi, 1)

            def turned_high(n, i, par):
                dst, src = ((QT[:, par, :, :], fill_a), (KT[:, par, 0:8, :], fill_b),
                            (KT[:, par, 8:16, :], fill_a))[i]
                act.wait_ge(s_qkT_ps, 3 * n + i + 1)
                need(act, s_scores, 4 * (n - 1))
                high(dst, src[0:96, :, :]).then_inc(s_qkT_sb, 1)

            def step(t, par):
                if has(t):
                    exps(t, 0)
                if has(t - 3):
                    n = t - 3
                    act.wait_ge(s_r1, n + 1)
                    need(act, s_r_act, n)
                    act.activation(r_e[:, :], r1_ps, ACT.Exp, scale=-1.0 / W_UP)
                    act.activation(r_z[:, :], r1_ps, ACT.Copy, scale=1.0 / W_UP).then_inc(s_r_exp, 1)
                if has(t):
                    p_high(t, 0)
                if has(t + 1):
                    turned_high(t + 1, 0, 1 - par)
                if has(t - 1):
                    n = t - 1
                    act.wait_ge(s_att_T, n + 1)
                    need(act, s_o_done, n)
                    high(attT[:, HI, :, :], T_ps[:, 0:D], ATT_UP).then_inc(s_attT_hi, 1)
                if has(t):
                    exps(t, 1)
                if has(t + 1):
                    turned_high(t + 1, 1, 1 - par)
                if has(t + 1):
                    n = t + 1
                    act.wait_ge(s_v_sb, n + 1)
                    need(act, s_pv, 4 * (n - 1))
                    high(V[:, 1 - par, HI, :, 0:HD],
                         v32[:, :].rearrange("p (h d) -> p h d", d=HD)).then_inc(s_v_hi, 1)
                if has(t):
                    p_high(t, 1)
                if has(t + 1):
                    turned_high(t + 1, 2, 1 - par)
                if has(t):
                    exps(t, 2)
                if has(t - 3):
                    n = t - 3
                    act.wait_ge(s_r_act, n + 1)
                    need(act, s_r2, n)
                    high(aT[:, HI, :], r_a[:, :]).then_inc(s_a_hi, 1)
                if has(t - 2):
                    n = t - 2
                    act.wait_ge(s_h_sb, n + 1)
                    high(keep["H"][:, n, HI, :], h32[:, :]).then_inc(s_h_hi, 1)
                if has(t):
                    p_high(t, 2)
                if has(t - 2):
                    n = t - 2
                    act.wait_ge(s_hT_ps, n + 1)
                    need(act, s_r1, n)
                    high(hT[:, HI, :, :], T_ps[:, 0:D]).then_inc(s_hT_hi, 1)
                if has(t):
                    exps(t, 3)
                if has(t + 3):
                    n = t + 3
                    act.wait_ge(s_xT_ps, n + 1)
                    need(act, s_v_done_ps, n - 1)
                    high(xT[:, 1 - par, HI, :, :], T_ps[:, :]).then_inc(s_xT_hi, 1)
                if has(t + 2):
                    n = t + 2
                    act.wait_ge(s_rot, n + 1)
                    need(act, s_qkT_ps, 3 * n)
                    q = qkr[:, 0:D].rearrange("p (a o c) -> p a o c", a=PAIRS, o=1)
                    k = qkr[:, D:2 * D].rearrange("p (a u c) -> p a u c", a=PAIRS, u=2)
                    high(QS[:, :, 0:3:2, :], q.broadcast_to([P, PAIRS, 2, 32]))
                    for u in range(2):
                        a = high(KS[:, :, u, 0:2, u, :],
                                 k[:, :, u:u + 1, :].broadcast_to([P, PAIRS, 2, HD]))
                    a.then_inc(s_qk_hi, 1)
                if has(t):
                    p_high(t, 3)

            slots(act, step)

            with act.Fori(0, NB // GB) as g:
                act.wait_ge(s_tk_neg, g + 1)
                act.activation(t_e[:, :], S_ps[0][:, 0:P], ACT.Exp, bias=t_nm[:, :],
                               accum_out=t_sum[:, :]).then_inc(s_tk_exp, 1)
                act.wait_ge(s_tk_T2, g + 1)
                high(keep["POS"][:, g, :, :, :], S_ps[1][:, 0:P].rearrange(
                    "p (b q i) -> p q b i", b=GB, q=E // QE)).then_inc(s_tk_pos, 1)
                high(keep["WT"][:, g, :, :, :], S_ps[1][:, P:2 * P].rearrange(
                    "p (b q i) -> p q i b", b=GB, q=E // QE)).then_inc(s_tk_wt, 1)

        @block.vector
        def _(dve):
            def low(out, in_, hi, scale=1.0):
                return dve.scalar_tensor_tensor(out=out, in0=in_, scalar=scale, in1=hi,
                                                op0=ALU.mult, op1=ALU.subtract)

            def halves(a):
                return a[:, :].rearrange("p (c h t j) -> p c h t j", c=2, t=2, j=HD // 2)

            for w in range(4):
                dve.wait_ge(s_wT_hi, w + 1)
                low(WT4[:, w, LO, :, :], [*S_ps, *PT_ps][w][:, :].rearrange("p (k e) -> p k e", k=K),
                    WT4[:, w, HI, :, :], W_UP).then_inc(s_wT_lo, 1)
            dve.wait_ge(s_rw_hi, 2)
            low(rw1[:, LO, :, :], rw1_raw[:, :, :], rw1[:, HI, :, :], W_UP).then_inc(s_rw_lo, 1)
            low(rw2[:, LO, :], rw2_raw[:, :], rw2[:, HI, :], W_UP).then_inc(s_rw_lo, 1)
            dve.wait_ge(s_tanh_done, 1)
            dve.tensor_scalar(x_scale[:, :], tanh_g[:, 0:1], 1.0 / (W_UP * ATT_UP), None,
                              ALU.mult).then_inc(s_scales_set, 1)
            dve.tensor_scalar(w_scale[:, :], tanh_g[:, 1:2], 1.0 / Y_DOWN, None,
                              ALU.mult).then_inc(s_scales_set, 1)
            dve.tensor_scalar(bo_g[:, :], bvo[:, 1, :], tanh_g[:, 0:1], None,
                              ALU.mult).then_inc(s_scales_set, 1)
            dve.wait_ge(s_scales_set, 3)
            dve.wait_ge(s_const_in, CONST_IN)

            def minima(n, c):
                g = 4 * n + c
                dve.wait_ge(s_scores, g + 1)
                need(dve, s_exp_done, g - 1)
                dve.tensor_reduce(mn[:, c % 2, :], S_ps[c % 2][:, :].rearrange("p (h k) -> p h k", h=4),
                                  AX_X, ALU.min).then_inc(s_min_done, 1)

            def p_low(n, c):
                g = 4 * n + c
                dve.wait_ge(s_p_hi, g + 1)
                dve.tensor_tensor(PT[:, c % 2, LO, :, :], PT_ps[c % 2][:, :].rearrange("p (h q) -> p h q", h=4),
                                  PT[:, c % 2, HI, :, :], ALU.subtract).then_inc(s_p_lo, 1)

            def tick():
                dve.memset(spare[:, :], 0.0)

            def norm_stats(n, which, in_, stat):
                dve.bn_stats(ln_st[:, which, :], in_).then_inc(stat, 1)

            def norm_moments(n, which, stat, mv, used):
                need(dve, used, n)
                dve.wait_ge(stat, n + 1)
                tick()
                dve.bn_aggr(ln_mv[:, which, :], ln_st[:, which, :]).then_inc(mv, 1)

            def norm_apply(out, in_, which):
                return dve.tensor_scalar(out, in_, ln_mv[:, which, 0:1], ln_rs[:, which:which + 1],
                                         ALU.subtract, ALU.mult)

            def step(t, par):
                if has(t + 1):
                    n = t + 1
                    dve.wait_ge(s_v_done_ps, n + 1)
                    need(dve, s_v_lo, n)
                    dve.scalar_tensor_tensor(out=v32[:, :], in0=v_ps, scalar=1.0 / W_UP, in1=bvo[:, 0, :],
                                             op0=ALU.mult, op1=ALU.add).then_inc(s_v_sb, 1)
                if has(t - 1):
                    n = t - 1
                    need(dve, s_r2, upto(n - 2))
                    dve.wait_ge(s_pv, 4 * (n + 1))
                    dve.reciprocal(den[:, :], att_ps[:, :, HD]).then_inc(s_recip_den, 1)
                if has(t):
                    minima(t, 1)
                if has(t - 4):
                    n = t - 4
                    dve.wait_ge(s_pv, 4 * upto(n + 4))
                    dve.wait_ge(s_r2, n + 1)
                    dve.tensor_scalar(L[:, n, :], r2_ps, 1.0 / W_UP, None, ALU.mult).then_inc(s_logit, 1)
                if has(t - 1):
                    n = t - 1
                    dve.wait_ge(s_recip_den, n + 1)
                    need(dve, s_att_T, n)
                    dve.tensor_tensor(att[:, :, :], att_ps[:, :, 0:HD],
                                      den[:, :].unsqueeze(2).broadcast_to([P, HEADS, HD]),
                                      ALU.mult).then_inc(s_att_sb, 1)
                if has(t - 3):
                    n = t - 3
                    dve.wait_ge(s_r_exp, n + 1)
                    dve.tensor_scalar(r_d[:, :], r_e[:, :], 1.0, None, ALU.add).then_inc(s_r_one, 1)
                if has(t - 2):
                    n = t - 2
                    dve.wait_ge(s_ln2_rstd, n + 1)
                    need(dve, s_hT_ps, n)
                    need(dve, s_h_lo, n)
                    norm_apply(h32[:, :], x1[:, par, :], 1).then_inc(s_h_sb, 1)
                if has(t + 4):
                    n = t + 4
                    dve.wait_ge(s_x_in_done, 16 * (n + 1))
                    norm_stats(n, 0, x_in[:, par, :], s_ln1_stat)
                if has(t):
                    p_low(t, 0)
                if has(t - 1):
                    n = t - 1
                    dve.wait_ge(s_attT_hi, n + 1)
                    low(attT[:, LO, :, :], T_ps[:, 0:D].rearrange("p (k q) -> p k q", k=K),
                        attT[:, HI, :, :], ATT_UP).then_inc(s_attT_lo, 1)
                if has(t - 3):
                    n = t - 3
                    dve.wait_ge(s_r_one, n + 1)
                    dve.reciprocal(r_r[:, :], r_d[:, :]).then_inc(s_r_rec, 1)
                if has(t + 4):
                    norm_moments(t + 4, 0, s_ln1_stat, s_ln1_mv, s_ln1_rstd)
                if has(t):
                    minima(t, 2)
                    minima(t, 3)
                    p_low(t, 1)
                if has(t - 3):
                    n = t - 3
                    dve.wait_ge(s_r_rec, n + 1)
                    need(dve, s_a_lo, n)
                    dve.tensor_tensor(r_a[:, :], r_z[:, :], r_r[:, :], ALU.mult).then_inc(s_r_act, 1)
                if has(t + 2):
                    n = t + 2
                    dve.wait_ge(s_qk_ps, n + 1)
                    need(dve, s_rot_cos, n)
                    dve.scalar_tensor_tensor(out=qk[:, :], in0=qk_bank[:, :], scalar=1.0 / W_UP,
                                             in1=bqk[:, :, :].rearrange("p a d -> p (a d)"), op0=ALU.mult,
                                             op1=ALU.add).then_inc(s_qk_sb, 1)
                if has(t - 3):
                    n = t - 3
                    dve.wait_ge(s_a_hi, n + 1)
                    dve.tensor_tensor(aT[:, LO, :], r_a[:, :], aT[:, HI, :], ALU.subtract).then_inc(s_a_lo, 1)
                if has(t + 2):
                    n = t + 2
                    dve.wait_ge(s_qk_sb, n + 1)
                    need(dve, s_rot, n)
                    for half in range(2):
                        a = dve.tensor_tensor(
                            halves(rot_b)[:, :, :, half, :], halves(qk)[:, :, :, 1 - half, :],
                            rope[:, 1, :, half * 8:half * 8 + 8].unsqueeze(2).broadcast_to([P, 2, HEADS, 8]),
                            ALU.mult)
                    a.then_inc(s_rot_sin, 1)
                if has(t - 2):
                    n = t - 2
                    dve.wait_ge(s_hT_hi, n + 1)
                    dve.tensor_tensor(hT[:, LO, :, :], T_ps[:, 0:D].rearrange("p (k q) -> p k q", k=K),
                                      hT[:, HI, :, :], ALU.subtract).then_inc(s_hT_lo, 1)
                if has(t - 1):
                    n = t - 1
                    dve.wait_ge(s_o_done, n + 1)
                    dve.wait_ge(s_xrb, n + 1)
                    need(dve, s_x1_out, 16 * (n - 1))
                    dve.scalar_tensor_tensor(out=x1[:, 1 - par, :], in0=o_ps, scalar=x_scale[:, 0:1],
                                             in1=x_res[:, 1 - par, :], op0=ALU.mult,
                                             op1=ALU.add).then_inc(s_x1_done, 1)
                if has(t + 1):
                    minima(t + 1, 0)
                if has(t):
                    p_low(t, 2)
                if has(t - 1):
                    n = t - 1
                    dve.wait_ge(s_x1_done, n + 1)
                    norm_stats(n, 1, x1[:, 1 - par, :], s_ln2_stat)
                if has(t - 1):
                    norm_moments(t - 1, 1, s_ln2_stat, s_ln2_mv, s_ln2_rstd)
                if has(t + 3):
                    n = t + 3
                    dve.wait_ge(s_xT_hi, n + 1)
                    dve.tensor_tensor(xT[:, 1 - par, LO, :, :], T_ps[:, :].rearrange("p (k q) -> p k q", q=P),
                                      xT[:, 1 - par, HI, :, :], ALU.subtract).then_inc(s_xT_lo, 1)
                if has(t + 4):
                    n = t + 4
                    dve.wait_ge(s_ln1_rstd, n + 1)
                    need(dve, s_xT_ps, n)
                    norm_apply(xn[:, :], x_in[:, par, :], 0).then_inc(s_xn_ready, 1)
                if has(t):
                    p_low(t, 3)

            slots(dve, step)

            dve.wait_ge(s_logit, NB)
            dve.wait_ge(s_zero_set, 4)
            ROUNDS = TOP // 8
            with dve.Fori(0, NB // GB) as g:
                dve.tensor_copy(Lg[:, :], L[:, :, :].rearrange("p (g b) e -> p g (b e)", b=GB)[:, g, :]).then_inc(s_tk_copy, 1)
                dve.wait_ge(s_tk_T, g + 1)
                dve.tensor_reduce(t_mx[:, :], S_ps[0][:, 0:P], AX_X, ALU.max).then_inc(s_tk_max, 1)
                dve.wait_ge(s_tk_max, g + 1)
                dve.tensor_scalar(t_nm[:, :], t_mx[:, :], -1.0, None, ALU.mult).then_inc(s_tk_neg, 1)
                dve.wait_ge(s_tk_exp, g + 1)
                dve.reciprocal(t_rs[:, :], t_sum[:, :]).then_inc(s_tk_rec, 1)
                dve.wait_ge(s_tk_rec, g + 1)
                dve.tensor_scalar(t_p[:, :], t_e[:, :], t_rs[:, 0:1], None, ALU.mult).then_inc(s_tk_p, 1)
                for r in range(ROUNDS):
                    src = t_p[:, :] if r == 0 else t_w[:, (r - 1) % 2, :]
                    if r:
                        dve.wait_ge(s_tk_rest, ROUNDS * g + r)
                    else:
                        dve.wait_ge(s_tk_p, g + 1)
                    tick()
                    dve.max(t_m8[:, :], src).then_inc(s_tk_top, 1)
                    dve.wait_ge(s_tk_top, ROUNDS * g + r + 1)
                    tick()
                    dve.match_replace(t_w[:, r % 2, :], t_m8[:, :], src, -1.0).then_inc(s_tk_rest, 1)
                dve.wait_ge(s_tk_rest, ROUNDS * (g + 1))
                dve.tensor_scalar(t_msk[:, :], t_w[:, (ROUNDS - 1) % 2, :], 0.0, None,
                                  ALU.is_lt).then_inc(s_tk_msk, 1)
                dve.wait_ge(s_tk_msk, g + 1)
                dve.tensor_tensor_scan(t_cum[:, :], t_msk[:, :], zeros[:, :], 0.0, ALU.add,
                                       ALU.add).then_inc(s_tk_cum, 1)
                dve.scalar_tensor_tensor(out=t_pm[:, :], in0=t_p[:, :], scalar=1.0, in1=t_msk[:, :],
                                         op0=ALU.mult, op1=ALU.mult,
                                         accum_out=t_ps[:, :]).then_inc(s_tk_sum, 1)
                dve.wait_ge(s_tk_sum, g + 1)
                dve.tensor_scalar(t_dn[:, :], t_ps[:, :], 1e-9, None, ALU.add).then_inc(s_tk_den, 1)
                dve.wait_ge(s_tk_den, g + 1)
                dve.reciprocal(t_rd[:, :], t_dn[:, :]).then_inc(s_tk_rden, 1)
                dve.wait_ge(s_tk_rden, g + 1)
                dve.tensor_tensor(t_wr[:, :], t_rd[:, :], w_scale[:, :], ALU.mult).then_inc(s_tk_wr, 1)
                dve.wait_ge(s_tk_wr, g + 1)
                dve.wait_ge(s_tk_cum, g + 1)
                dve.tensor_scalar(t_wt[:, :], t_pm[:, :], t_wr[:, 0:1], None, ALU.mult).then_inc(s_tk_res, 1)
                dve.tensor_tensor(t_pos[:, :], t_cum[:, :], t_msk[:, :], ALU.mult).then_inc(s_tk_res, 1)
                dve.wait_ge(s_tk_T2, g + 1)


def expert_phase(nc, io, keep, dims):
    NB, D, E, F = dims["NB"], dims["D"], dims["E"], dims["F"]
    K = D // P
    FC = F // P
    TILES = GB * TOP // P
    NG, NQ = NB // GB, (NB // GB) * (E // QE)
    NT = GB * TOP
    assert FC == 4 and TILES == 4 and K == 2 and NQ % 2 == 0
    ctx = ExitStack()
    with ctx:
        def sb(name, shape, dt=F32):
            return ctx.enter_context(nc.sbuf_tensor(name, shape, dt))

        def bank(name):
            return ctx.enter_context(nc.psum_tensor(name, [P, 512], F32))

        def sem(name):
            return ctx.enter_context(nc.semaphore(name))

        raw = [sb("w1_raw", [P, K, F]), sb("w2_raw", [P, K, F]), sb("w3_raw", [P, FC, D])]
        W1 = sb("W1", [P, 2, 2, K, F], F16)
        W2 = sb("W2", [P, 2, 2, K, F], F16)
        W3 = sb("W3", [P, 2, 2, FC, D], F16)
        parts = [W1, W2, W3]
        ident16 = keep["ident16"]
        pick = sb("pick", [P, 2, TILES, QE, 2, TOP], F16)
        X = sb("X", [P, 2, QE, 2, K, NT], F16)
        sg = sb("sg", [P, 2, NT])
        u32 = sb("u32", [P, 2, NT])
        U = sb("U", [P, 2, 2, FC, NT], F16)
        place = sb("place", [P, 2, TILES, 2, P], F16)
        Y = sb("Y", [P, 2, 2, D], F16)
        acc = sb("acc", [P, 2, GB, D])

        G_ps = [bank("G0_ps"), bank("G1_ps")]
        V_ps = [bank("V0_ps"), bank("V1_ps")]
        Y_ps = bank("Y_ps")
        S_ps = bank("Sc_ps")
        X_ps = bank("X_ps")
        place_ps = bank("place_ps")
        first_banks = [X_ps, Y_ps, S_ps, V_ps[1]]
        place16 = place_ps[:, 0:256].bitcast(F16).rearrange("p (t s) -> p t s", t=TILES)

        s_acc_in = sem("acc_in")
        s_acc_out = sem("acc_out")
        s_pick_set = sem("pick_set")
        s_x_ps = sem("x_ps")
        s_x_sb = sem("x_sb")
        s_g_ps = sem("g_ps")
        s_v_ps = sem("v_ps")
        s_silu_done = sem("silu_done")
        s_u_done = sem("u_done")
        s_u_hi = sem("u_hi")
        s_u_lo = sem("u_lo")
        s_place_ps_done = sem("place_ps_done")
        s_place_sb = sem("place_sb")
        s_y_ps = sem("y_ps")
        s_y_hi = sem("y_hi")
        s_y_lo = sem("y_lo")
        s_sc_ps = sem("sc_ps")
        s_acc_done = sem("acc_done")
        w_in = [sem(f"w{i + 1}_in") for i in range(3)]
        w_hi = [sem(f"w{i + 1}_hi") for i in range(3)]
        w_lo = [sem(f"w{i + 1}_lo") for i in range(3)]

        block = ctx.enter_context(nc.Block())

        def lin(unit):
            return QE * unit[0] + unit[2]

        def before(unit):
            if unit is None:
                return None
            q, par, i = unit
            if i:
                return q, par, i - 1
            return None if isinstance(q, int) and q == 0 else (q - 1, 1 - par, QE - 1)

        def units(eng, step, tail):
            for i in range(QE):
                step((0, 0, i), True)
            with eng.Fori(0, (NQ - 2) // 2) as j:
                for k in range(2):
                    for i in range(QE):
                        step((2 * j + 1 + k, (1 + k) % 2, i), True)
            for i in range(QE):
                step((NQ - 1, (NQ - 1) % 2, i), False)
            tail((NQ - 1, (NQ - 1) % 2, QE - 1))

        def rows(b):
            return slice(TOP * b, TOP * (b + 1))

        def group_of(q):
            return q // (E // QE)

        @block.sync
        def _(sp):
            src = [w.rearrange("e (c p) f -> e p c f", p=P) for w in (io["w1"], io["w2"], io["w3"])]

            def load(e, u):
                for m in range(3):
                    need(sp, w_hi[m], u)
                    need(sp, w_lo[m], u)
                    sp.dma_start(raw[m][:, :, :], src[m][e]).then_inc(w_in[m], 16)

            out_g = io["out"].rearrange("(g b) p d -> g p b d", b=GB)

            def acc_load(g):
                return sp.dma_start(acc[:, g % 2, :, :],
                                    out_g[g])

            def acc_store(g):
                return sp.dma_start(out_g[g],
                                    acc[:, g % 2, :, :])

            load(0, 0)
            acc_load(0).then_inc(s_acc_in, 16)
            for e in range(1, 8):
                load(e, e)
            if NG > 1:
                sp.wait_ge(s_acc_in, 16)
                acc_load(1).then_inc(s_acc_in, 16)
            for e in range(8, E):
                load(e, e)
            if NG > 2:
                with sp.Fori(1, NG - 1) as g:
                    with sp.Fori(0, 4) as e:
                        load(e, E * g + e)
                    sp.wait_ge(s_acc_done, TILES * E * g)
                    acc_store(g - 1).then_inc(s_acc_out, 16)
                    with sp.Fori(4, 8) as e:
                        load(e, E * g + e)
                    sp.wait_ge(s_acc_out, 16 * g)
                    sp.wait_ge(s_acc_in, 16 * (g + 1))
                    acc_load(g + 1).then_inc(s_acc_in, 16)
                    with sp.Fori(8, E) as e:
                        load(e, E * g + e)
            if NG > 1:
                for e in range(4):
                    load(e, E * (NG - 1) + e)
                sp.wait_ge(s_acc_done, TILES * E * (NG - 1))
                acc_store(NG - 2).then_inc(s_acc_out, 16)
                for e in range(4, E):
                    load(e, E * (NG - 1) + e)
            sp.wait_ge(s_acc_done, TILES * E * NG)
            acc_store(NG - 1).then_inc(s_acc_out, 16)
            sp.wait_ge(s_acc_out, 16 * NG)

        @block.tensor
        def _(pe):
            def gather(q, par, j, dst=X_ps, banks=1):
                b, part = j // 2, j % 2
                pe.wait_ge(s_pick_set, 4 * q + b // 2 + 1)
                need(pe, s_x_sb, 16 * q + j + 1 - banks)
                for k in range(K):
                    mm = pe.matmul(dst[:, 256 * k:256 * (k + 1)],
                                   keep["H"][:, GB * group_of(q) + b, part, k * P:(k + 1) * P],
                                   pick[:, par, b // 2, :, b % 2, :], start=True, stop=True)
                mm.then_inc(s_x_ps, 1)

            def up(unit, f):
                q, par, i = unit
                n = 4 * lin(unit) + f
                if f == 0:
                    if i == 0:
                        pe.wait_ge(s_x_sb, 16 * (q + 1))
                    pe.wait_ge(w_lo[0], lin(unit) + 1)
                need(pe, s_silu_done, n - 1)
                three_pass(pe, G_ps[f % 2][:, :], lambda a, k: W1[:, i % 2, a, k, f * P:(f + 1) * P],
                           lambda b, k: X[:, par, i, b, k, :], range(K)).then_inc(s_g_ps, 1)
                if f == 0:
                    pe.wait_ge(w_lo[1], lin(unit) + 1)
                need(pe, s_u_done, n - 1)
                three_pass(pe, V_ps[f % 2][:, :], lambda a, k: W2[:, i % 2, a, k, f * P:(f + 1) * P],
                           lambda b, k: X[:, par, i, b, k, :], range(K)).then_inc(s_v_ps, 1)

            def down(unit, t):
                i = unit[2]
                n = 4 * lin(unit) + t
                if t == 0:
                    pe.wait_ge(s_u_hi, 4 * lin(unit) + 4)
                    pe.wait_ge(s_u_lo, 4 * lin(unit) + 4)
                    pe.wait_ge(w_lo[2], lin(unit) + 1)
                need(pe, s_y_lo, n)
                three_pass(pe, Y_ps[:, 0:D],
                           lambda a, k: U[:, i % 2, a, k, t * P:(t + 1) * P],
                           lambda b, k: W3[:, i % 2, b, k, :], range(FC)).then_inc(s_y_ps, 1)

            def scatter(unit, t):
                i = unit[2]
                n = 4 * lin(unit) + t
                if t == 0:
                    pe.wait_ge(s_place_sb, 4 * (lin(unit) + 1))
                pe.wait_ge(s_y_lo, n + 1)
                need(pe, s_acc_done, n)
                for b in range(2):
                    mm = pe.matmul(S_ps[:, D * b:D * (b + 1)], place[:, i % 2, t, b, :],
                                   Y[:, t % 2, b, :], start=True, stop=True)
                mm.then_inc(s_sc_ps, 1)

            def turn_pick(unit, t):
                q, par, i = unit
                if t == 0:
                    need(pe, s_place_sb, 4 * lin(unit))
                mm = pe.transpose(place16[:, t, :], pick[:, par, t, i, :, :], ident16[:, :])
                if t == TILES - 1:
                    mm.then_inc(s_place_ps_done, 1)

            def step(unit, more):
                q, par, i = unit
                last, last2 = before(unit), before(before(unit))
                for f in range(FC):
                    up(unit, f)
                    if last:
                        down(last, f)
                    if f and last:
                        scatter(last, f - 1)
                    if f == 0 and last2:
                        scatter(last2, TILES - 1)
                    if more:
                        gather(q + 1, 1 - par, QE * i + f)
                    turn_pick(unit, f)

            def tail(unit):
                for t in range(TILES):
                    down(unit, t)
                    if t:
                        scatter(unit, t - 1)
                    else:
                        scatter(before(unit), TILES - 1)
                scatter(unit, TILES - 1)

            for j in range(16):
                gather(0, 0, j, first_banks[j % 4], 4)
            units(pe, step, tail)

        @block.scalar
        def _(act):
            def high(out, in_, scale=1.0):
                return act.activation(out, in_, ACT.Copy, scale=scale)

            def weights(m, unit):
                n, i = lin(unit), unit[2]
                act.wait_ge(w_in[m], 16 * (n + 1))
                need(act, [s_g_ps, s_v_ps, s_y_ps][m], 4 * (n - 1))
                high(parts[m][:, i % 2, HI, :, :], raw[m][:, :, :], W_UP).then_inc(w_hi[m], 1)

            def tokens(q, par, j, src=X_ps):
                b, part = j // 2, j % 2
                act.wait_ge(s_x_ps, 16 * q + j + 1)
                need(act, s_v_ps, 16 * (q - 1))
                high(X[:, par, :, part, :, b * TOP:(b + 1) * TOP].rearrange("p e k c -> p k e c"),
                     src[:, :].rearrange("p (k e c) -> p k e c", k=K, e=QE)).then_inc(s_x_sb, 1)

            def places(unit):
                n, i = lin(unit), unit[2]
                act.wait_ge(s_place_ps_done, n + 1)
                need(act, s_sc_ps, 4 * (n - 1))
                for b in range(2):
                    for half in range(2):
                        high(place[rows(half), i % 2, :, b, :],
                             place16[rows(b), :, :]).then_inc(s_place_sb, 1)

            def u_high(unit, f):
                n, i = 4 * lin(unit) + f, unit[2]
                act.wait_ge(s_u_done, n + 1)
                need(act, s_y_ps, 4 * (lin(unit) - 1))
                high(U[:, i % 2, HI, f, :], u32[:, f % 2, :]).then_inc(s_u_hi, 1)

            def y_high(unit, t):
                n = 4 * lin(unit) + t
                act.wait_ge(s_y_ps, n + 1)
                need(act, s_sc_ps, n - 1)
                for b in range(2):
                    a = high(Y[rows(b), t % 2, b, :], Y_ps[rows(b), 0:D], Y_DOWN / W_UP)
                a.then_inc(s_y_hi, 1)

            def step(unit, more):
                q, par, i = unit
                last = before(unit)
                for f in range(FC):
                    n = 4 * lin(unit) + f
                    act.wait_ge(s_g_ps, n + 1)
                    need(act, s_u_done, n - 1)
                    act.activation(sg[:, f % 2, :], G_ps[f % 2][:, :], ACT.Silu,
                                   scale=1.0 / W_UP).then_inc(s_silu_done, 1)
                    if f:
                        u_high(unit, f - 1)
                    if f == 0 and last:
                        places(last)
                    if last:
                        y_high(last, f)
                    if more:
                        tokens(q + 1, 1 - par, QE * i + f)
                    if f == 0:
                        weights(2, unit)
                    if f in (1, 2) and (more or i < QE - 1):
                        weights(f - 1, (q, par, i + 1) if i < QE - 1 else (q + 1, 1 - par, 0))
                u_high(unit, FC - 1)

            def tail(unit):
                places(unit)
                for t in range(TILES):
                    y_high(unit, t)

            for j in range(16):
                tokens(0, 0, j, first_banks[j % 4])
                if j in (7, 11):
                    weights((j - 7) // 4, (0, 0, 0))
            units(act, step, tail)

        @block.vector
        def _(dve):
            def low(out, in_, hi, scale):
                return dve.scalar_tensor_tensor(out=out, in0=in_, scalar=scale, in1=hi,
                                                op0=ALU.mult, op1=ALU.subtract)

            def weights(m, unit):
                n, i = lin(unit), unit[2]
                dve.wait_ge(w_hi[m], n + 1)
                low(parts[m][:, i % 2, LO, :, :], raw[m][:, :, :], parts[m][:, i % 2, HI, :, :],
                    W_UP).then_inc(w_lo[m], 1)

            def picks(q, par, b2):
                need(dve, s_place_ps_done, 4 * (q - 1))
                pos = keep["POS"][:, group_of(q), q % (E // QE), 2 * b2:2 * b2 + 2, :]
                dve.tensor_tensor(
                    pick[:, par, b2, :, :, :],
                    pos.rearrange("p b i -> p i b").unsqueeze(3).broadcast_to([P, QE, 2, TOP]),
                    keep["iota"][:, :].unsqueeze(1).unsqueeze(1).broadcast_to([P, QE, 2, TOP]),
                    ALU.is_equal).then_inc(s_pick_set, 1)

            def y_low(unit, t):
                n = 4 * lin(unit) + t
                dve.wait_ge(s_y_hi, n + 1)
                for b in range(2):
                    a = low(Y[rows(1 - b), t % 2, b, :], Y_ps[rows(b), 0:D], Y[rows(b), t % 2, b, :],
                            Y_DOWN / W_UP)
                a.then_inc(s_y_lo, 1)

            def add(unit, t):
                q, par, i = unit
                n = 4 * lin(unit) + t
                g = group_of(q)
                dve.wait_ge(s_sc_ps, n + 1)
                dve.wait_ge(s_acc_in, 16 * (g + 1))
                need(dve, s_acc_done, n - 3)
                for b in range(2):
                    tile = acc[:, g % 2, 2 * t + b, :]
                    a = dve.scalar_tensor_tensor(
                        out=tile, in0=S_ps[:, D * b:D * (b + 1)],
                        scalar=keep["WT"][:, g, q % (E // QE), i, 2 * t + b:2 * t + b + 1], in1=tile,
                        op0=ALU.mult, op1=ALU.add)
                a.then_inc(s_acc_done, 1)

            def step(unit, more):
                q, par, i = unit
                last, last2 = before(unit), before(before(unit))
                for f in range(FC):
                    n = 4 * lin(unit) + f
                    if f == 0 and more:
                        picks(q + 1, 1 - par, i)
                    dve.wait_ge(s_v_ps, n + 1)
                    dve.wait_ge(s_silu_done, n + 1)
                    need(dve, s_u_hi, n - 1)
                    need(dve, s_u_lo, n - 1)
                    dve.scalar_tensor_tensor(out=u32[:, f % 2, :], in0=V_ps[f % 2][:, :],
                                             scalar=1.0 / W_UP, in1=sg[:, f % 2, :], op0=ALU.mult,
                                             op1=ALU.mult).then_inc(s_u_done, 1)
                    if last:
                        y_low(last, f)
                    if f and last:
                        add(last, f - 1)
                    if f == 0 and last2:
                        add(last2, TILES - 1)
                    if f == 0:
                        weights(2, unit)
                    if f in (1, 2) and (more or i < QE - 1):
                        weights(f - 1, (q, par, i + 1) if i < QE - 1 else (q + 1, 1 - par, 0))

            def tail(unit):
                for t in range(TILES):
                    y_low(unit, t)
                    if t:
                        add(unit, t - 1)
                    else:
                        add(before(unit), TILES - 1)
                add(unit, TILES - 1)

            for b2 in range(4):
                picks(0, 0, b2)
            weights(0, (0, 0, 0))
            weights(1, (0, 0, 0))
            units(dve, step, tail)

        @block.gpsimd
        def _(pool):
            def step(unit, more):
                q, par, i = unit
                for f in range(FC):
                    n = 4 * lin(unit) + f
                    pool.wait_ge(s_u_hi, n + 1)
                    pool.tensor_tensor(U[:, i % 2, LO, f, :], u32[:, f % 2, :], U[:, i % 2, HI, f, :],
                                       ALU.subtract).then_inc(s_u_lo, 1)

            units(pool, step, lambda unit: None)


def flamingo_kernel(nc, io):
    NB, S, D = io["x"].shape
    E, _, F = io["w1"].shape
    dims = dict(NB=NB, D=D, E=E, F=F, RH=io["rw1"].shape[1])
    assert S == P and D == HEADS * HD and dims["RH"] == P and E * GB == P and NB % GB == 0
    with ExitStack() as ctx:
        keep = dict(
            H=ctx.enter_context(nc.sbuf_tensor("H", [P, NB, 2, D], F16)),
            POS=ctx.enter_context(nc.sbuf_tensor("POS", [P, NB // GB, E // QE, GB, QE], F16)),
            WT=ctx.enter_context(nc.sbuf_tensor("WT", [P, NB // GB, E // QE, QE, GB], F32)),
            ident16=ctx.enter_context(nc.sbuf_tensor("ident16", [P, P], F16)),
            iota=ctx.enter_context(nc.sbuf_tensor("iota", [P, TOP], F32)),
        )
        attention_phase(nc, io, keep, dims)
        expert_phase(nc, io, keep, dims)


_INS = {
    'x': 'x', 'ctx_1024': 'ctx', 'g_xattn': 'g_xattn', 'g_ffn': 'g_ffn',
    'L0_xattn_Wq': 'Wq', 'L0_xattn_bq': 'bq', 'L0_xattn_Wk': 'Wk', 'L0_xattn_bk': 'bk',
    'L0_xattn_Wv': 'Wv', 'L0_xattn_bv': 'bv', 'L0_xattn_Wo': 'Wo', 'L0_xattn_bo': 'bo',
    'L0_ffn_router_w1': 'rw1', 'L0_ffn_router_w2': 'rw2',
    'L0_ffn_w1': 'w1', 'L0_ffn_w2': 'w2', 'L0_ffn_w3': 'w3',
}


def _constants():
    import numpy as np
    inv_freq = (1.0 / 10000.0 ** (np.arange(0, HD, 2, dtype=np.float32) / HD)).astype(np.float32)
    freqs = np.arange(P, dtype=np.float32)[:, None] * inv_freq[None, :]
    cos, sin = np.cos(freqs), np.sin(freqs)
    q_scale = np.float32(-HD ** -0.5)
    table = np.concatenate([np.concatenate([a * q_scale, a], axis=1) for a in (
        np.concatenate([cos, cos], axis=1), np.concatenate([-sin, sin], axis=1))], axis=1)
    return {
        'ident': np.eye(P, dtype=np.float32),
        'rope': table.astype(np.float32),
        'iota': np.tile(np.arange(1, TOP + 1, dtype=np.float32), (P, 1)),
    }


def kernel(**inputs):
    import numpy as _np
    import concourse.bacc as _bacc
    from concourse import mybir as _mybir
    from concourse.bass_utils import run_bass_kernel_spmd as _run

    nc = _bacc.Bacc("TRN2", target_bir_lowering=False, num_devices=1)
    arrays, aps = {}, {}
    for name, short in _INS.items():
        arrays[f"in_{short}_dram"] = _np.ascontiguousarray(inputs[name])
    for short, a in _constants().items():
        arrays[f"in_{short}_dram"] = a
    for key, a in arrays.items():
        aps[key[3:-5]] = nc.dram_tensor(key, a.shape, _mybir.dt.from_np(a.dtype), kind="ExternalInput").ap()
    shape = arrays["in_x_dram"].shape
    aps["out"] = nc.dram_tensor("out_0_dram", shape, _mybir.dt.float32, kind="ExternalOutput").ap()
    flamingo_kernel(nc, aps)
    r = _run(nc, [arrays], core_ids=[0])
    return r.results[0]["out_0_dram"]
```

```python
from contextlib import ExitStack

import concourse.bass as bass
from concourse import mybir

F32 = mybir.dt.float32
F16 = mybir.dt.float16
ALU = mybir.AluOpType
ACT = mybir.ActivationFunctionType
AX_X = mybir.AxisListType.X

P = 128
HEADS = 16
HD = 16
PAIRS = HEADS // 2
CHUNKS = 4
TOP = 64
GB = 8
QE = 4
LN_EPS = 1e-5
W_UP = 64.0
ATT_UP = 16.0
Y_DOWN = 1.0 / 64
HI, LO = 0, 1


def need(engine, semaphore, value):
    if isinstance(value, int) and value <= 0:
        return
    engine.wait_ge(semaphore, value)


def three_pass(eng, out, stationary, moving, ks, first=True, last=True):
    todo = [(k, a, b) for k in ks for a, b in ((HI, HI), (HI, LO), (LO, HI))]
    for n, (k, a, b) in enumerate(todo):
        mm = eng.matmul(out, stationary(a, k), moving(b, k), start=(first and n == 0),
                        stop=(last and n == len(todo) - 1), skip_group_check=True)
    return mm


def attention_phase(nc, io, keep, dims):
    NB, D, E, RH = dims["NB"], dims["D"], dims["E"], dims["RH"]
    K = D // P
    ctx = ExitStack()
    with ctx:
        def sb(name, shape, dt=F32):
            return ctx.enter_context(nc.sbuf_tensor(name, shape, dt))

        def bank(name):
            return ctx.enter_context(nc.psum_tensor(name, [P, 512], F32))

        def sem(name):
            return ctx.enter_context(nc.semaphore(name))

        ident = sb("ident", [P, P])
        ident16 = keep["ident16"]
        rope = sb("rope", [P, 2, 2, HD])
        w_raw = sb("w_raw", [P, 4, K, D])
        WT4 = sb("WT4", [P, 4, 2, K, D], F16)
        rw1_raw = sb("rw1_raw", [P, K, RH])
        rw1 = sb("rw1", [P, 2, K, RH], F16)
        rw2_raw = sb("rw2_raw", [P, E])
        rw2 = sb("rw2", [P, 2, E], F16)
        bqk = sb("bqk", [P, 2, D])
        bvo = sb("bvo", [P, 2, D])
        gates = sb("gates", [P, 2])
        tanh_g = sb("tanh_g", [P, 2])
        x_scale = sb("x_scale", [P, 1])
        w_scale = sb("w_scale", [P, 1])
        bo_g = sb("bo_g", [P, D])
        eps = sb("eps", [P, 1])
        minus_half = sb("minus_half", [P, 1])
        zeros = sb("zeros", [P, P])

        x_in = sb("x_in", [P, 2, D])
        c_in = sb("c_in", [P, 2, D])
        x_res = sb("x_res", [P, 2, D])
        ln_st = sb("ln_st", [P, 2, 6])
        ln_mv = sb("ln_mv", [P, 2, 2])
        ln_ve = sb("ln_ve", [P, 2])
        ln_rs = sb("ln_rs", [P, 2])
        xn = sb("xn", [P, D])
        xT = sb("xT", [P, 2, 2, 2 * K, P], F16)
        qk = sb("qk", [P, 2 * D])
        rot_a = sb("rot_a", [P, 2 * D])
        rot_b = sb("rot_b", [P, 2 * D])
        qkr = sb("qkr", [P, 2 * D])
        QS = sb("QS", [P, PAIRS, 3, 32], F16)
        KS = sb("KS", [P, PAIRS, 2, 3, 2, HD], F16)
        QT = sb("QT", [96, 2, PAIRS, P], F16)
        KT = sb("KT", [96, 2, HEADS, P], F16)
        v32 = sb("v32", [P, D])
        V = sb("V", [P, 2, 2, HEADS, HD + 1], F16)
        mn = sb("mn", [P, 2, 4])
        Pr = sb("Pr", [P, 2, 4, P])
        PT = sb("PT", [P, 2, 2, 4, P], F16)
        den = sb("den", [P, HEADS])
        att = sb("att", [P, HEADS, HD])
        attT = sb("attT", [P, 2, K, P], F16)
        x1 = sb("x1", [P, 2, D])
        h32 = sb("h32", [P, D])
        hT = sb("hT", [P, 2, K, P], F16)
        r_t = sb("r_t", [P, P])
        r_z = sb("r_z", [P, P])
        r_a = sb("r_a", [P, P])
        aT = sb("aT", [P, 2, P], F16)
        L = sb("L", [P, NB, E])

        Lg = sb("Lg", [P, P])
        t_mx = sb("t_mx", [P, 1])
        t_nm = sb("t_nm", [P, 1])
        t_e = sb("t_e", [P, P])
        t_sum = sb("t_sum", [P, 1])
        t_rs = sb("t_rs", [P, 1])
        t_p = sb("t_p", [P, P])
        t_w = sb("t_w", [P, 2, P])
        t_m8 = sb("t_m8", [P, 8])
        t_msk = sb("t_msk", [P, P])
        t_pm = sb("t_pm", [P, P])
        t_ps = sb("t_ps", [P, 1])
        t_dn = sb("t_dn", [P, 1])
        t_rd = sb("t_rd", [P, 1])
        t_wr = sb("t_wr", [P, 1])
        t_wt = sb("t_wt", [P, P])
        t_cum = sb("t_cum", [P, P])
        t_pos = sb("t_pos", [P, P])
        spare = sb("spare", [P, 4])

        S_ps = [bank("S0_ps"), bank("S1_ps")]
        PT_ps = [bank("PT0_ps"), bank("PT1_ps")]
        qk_bank = bank("qk_bank")
        small = bank("small_ps")
        vo_bank = bank("vo_bank")
        T_ps = bank("T_ps")
        att_ps = small[:, 0:HEADS * (HD + 1)].rearrange("p (h d) -> p h d", d=HD + 1)
        r1_ps = qk_bank[:, 0:P]
        r2_ps = small[:, 400:400 + E]
        v_ps = vo_bank[:, 0:D]
        o_ps = vo_bank[:, D:2 * D]
        fill_a = vo_bank[:, :].bitcast(F16).rearrange("p (h s) -> p h s", s=P)
        fill_b = qk_bank[:, :].bitcast(F16).rearrange("p (h s) -> p h s", s=P)

        s_ident_in = sem("ident_in")
        s_w4_in = [sem(f"{w}_in") for w in ("wq", "wk", "wv", "wo")]
        s_small_in = sem("small_in")
        s_zero_set = sem("zero_set")
        s_ident16_set = sem("ident16_set")
        s_v_ones = sem("v_ones")
        s_wT_ps = sem("wT_ps")
        s_wT_hi = sem("wT_hi")
        s_wT_lo = sem("wT_lo")
        s_rw_hi = sem("rw_hi")
        s_rw_lo = sem("rw_lo")
        s_tanh_done = sem("tanh_done")
        s_scales_set = sem("scales_set")
        s_x_in_done = sem("x_in_done")
        s_c_in_done = sem("c_in_done")
        s_xr_in = sem("xr_in")
        s_ln1_stat = sem("ln1_stat")
        s_ln1_mv = sem("ln1_mv")
        s_ln1_ve = sem("ln1_ve")
        s_ln1_rstd = sem("ln1_rstd")
        s_xn_ready = sem("xn_ready")
        s_xT_ps = sem("xT_ps")
        s_xT_hi = sem("xT_hi")
        s_xT_lo = sem("xT_lo")
        s_qk_ps = sem("qk_ps")
        s_v_done_ps = sem("v_done_ps")
        s_qk_sb = sem("qk_sb")
        s_v_sb = sem("v_sb")
        s_v_hi = sem("v_hi")
        s_v_lo = sem("v_lo")
        s_rot_cos = sem("rot_cos")
        s_rot_sin = sem("rot_sin")
        s_rot = sem("rot")
        s_qk_hi = sem("qk_hi")
        s_qk_lo = sem("qk_lo")
        s_qkT_ps = sem("qkT_ps")
        s_qkT_sb = sem("qkT_sb")
        s_scores = sem("scores")
        s_min_done = sem("min_done")
        s_exp_done = sem("exp_done")
        s_p_T = sem("p_T")
        s_p_hi = sem("p_hi")
        s_p_lo = sem("p_lo")
        s_pv = sem("pv")
        s_recip_den = sem("recip_den")
        s_att_sb = sem("att_sb")
        s_att_T = sem("att_T")
        s_attT_hi = sem("attT_hi")
        s_attT_lo = sem("attT_lo")
        s_o_done = sem("o_done")
        s_xrb = sem("xrb")
        s_x1_done = sem("x1_done")
        s_x1_out = sem("x1_out")
        s_ln2_stat = sem("ln2_stat")
        s_ln2_mv = sem("ln2_mv")
        s_ln2_ve = sem("ln2_ve")
        s_ln2_rstd = sem("ln2_rstd")
        s_h_sb = sem("h_sb")
        s_h_hi = sem("h_hi")
        s_h_lo = sem("h_lo")
        s_hT_ps = sem("hT_ps")
        s_hT_hi = sem("hT_hi")
        s_hT_lo = sem("hT_lo")
        s_r1 = sem("r1")
        s_r_tanh = sem("r_tanh")
        s_r_act = sem("r_act")
        s_a_hi = sem("a_hi")
        s_a_lo = sem("a_lo")
        s_r2 = sem("r2")
        s_logit = sem("logit")
        s_tk_copy = sem("tk_copy")
        s_tk_T = sem("tk_T")
        s_tk_max = sem("tk_max")
        s_tk_neg = sem("tk_neg")
        s_tk_exp = sem("tk_exp")
        s_tk_rec = sem("tk_rec")
        s_tk_top = sem("tk_top")
        s_tk_rest = sem("tk_rest")
        s_tk_msk = sem("tk_msk")
        s_tk_sum = sem("tk_sum")
        s_tk_den = sem("tk_den")
        s_tk_rden = sem("tk_rden")
        s_tk_wr = sem("tk_wr")
        s_tk_cum = sem("tk_cum")
        s_tk_res = sem("tk_res")
        s_tk_T2 = sem("tk_T2")
        s_tk_free = sem("tk_free")
        SMALL_IN = 16 * 10

        FIRST, ALONE, ROUTED = -4, 6, GB + 4
        NG = NB // GB
        ROUNDS = TOP // 8
        assert GB == 8 and ROUNDS == 8 and NG > 1

        def slots(eng, step):
            def eight(g, rounds):
                t = GB * g + ROUTED
                step(t, 0, "softmax", g)
                step(t + 1, 1, "probabilities", g)
                rounds(t + 2, g)
                step(t + 6, 0, "weights", g)
                step(t + 7, 1, "places", g)

            def looped(t, g):
                with eng.Fori(0, 2) as i:
                    for k in range(2):
                        step(2 * i + t + k, k, "rounds", g, 4 * i + 2 * k)

            def unrolled(t, g):
                for k in range(4):
                    step(t + k, k % 2, "rounds", g, 2 * k)

            for t in range(FIRST, ALONE):
                step(t, t % 2)
            with eng.Fori(0, (ROUTED - ALONE) // 2) as j:
                for k in range(2):
                    step(2 * j + (ALONE + k), k)
            if NG > 2:
                with eng.Fori(0, NG - 2) as g:
                    eight(g, looped)
            eight(NG - 2, unrolled)

        def has(n):
            return not isinstance(n, int) or 0 <= n < NB

        def upto(n):
            return min(n, NB) if isinstance(n, int) else n

        block = ctx.enter_context(nc.Block())

        @block.sync
        def _(sp):
            sp.dma_start(ident[:, :], io["ident"]).then_inc(s_ident_in, 16)
            sp.dma_start(x_in[:, 0, :], io["x"][0]).then_inc(s_x_in_done, 16)
            sp.dma_start(c_in[:, 0, :], io["ctx"][0]).then_inc(s_c_in_done, 16)
            for i, w in enumerate((io["Wq"], io["Wk"], io["Wv"], io["Wo"])):
                sp.dma_start(w_raw[:, i, :, :], w.rearrange("(c p) d -> p c d", p=P)).then_inc(s_w4_in[i], 16)
            sp.dma_start(rope[:, :, :, :], io["rope"].rearrange("p (c a j) -> p c a j", c=2, a=2)).then_inc(s_small_in, 16)
            for i, b in enumerate((io["bq"], io["bk"])):
                sp.dma_start(bqk[:, i, :], b.partition_broadcast(P)).then_inc(s_small_in, 16)
            for i, b in enumerate((io["bv"], io["bo"])):
                sp.dma_start(bvo[:, i, :], b.partition_broadcast(P)).then_inc(s_small_in, 16)
            for i, g in enumerate((io["g_xattn"], io["g_ffn"])):
                sp.dma_start(gates[:, i:i + 1], g.partition_broadcast(P)).then_inc(s_small_in, 16)
            sp.dma_start(rw1_raw[:, :, :], io["rw1"].rearrange("(c p) h -> p c h", p=P)).then_inc(s_small_in, 16)
            sp.dma_start(rw2_raw[:, :], io["rw2"]).then_inc(s_small_in, 16)
            sp.dma_start(keep["iota"][:, :], io["iota"]).then_inc(s_small_in, 16)

            def step(t, par):
                if has(t + 5):
                    n = t + 5
                    need(sp, s_xn_ready, n - 1)
                    sp.wait_ge(s_x_in_done, 16 * n)
                    sp.dma_start(x_in[:, 1 - par, :], io["x"][n]).then_inc(s_x_in_done, 16)
                    need(sp, s_xT_ps, n - 1)
                    sp.wait_ge(s_c_in_done, 16 * n)
                    sp.dma_start(c_in[:, 1 - par, :], io["ctx"][n]).then_inc(s_c_in_done, 16)
                if has(t):
                    need(sp, s_x1_done, t - 1)
                    need(sp, s_xr_in, 16 * t)
                    sp.dma_start(x_res[:, par, :], io["x"][t]).then_inc(s_xr_in, 16)
                if has(t - 2):
                    need(sp, s_x1_out, 16 * (t - 2))
                    sp.wait_ge(s_x1_done, t - 1)
                    sp.dma_start(io["out"][t - 2], x1[:, par, :]).then_inc(s_x1_out, 16)

            for t in range(FIRST, 5):
                step(t, t % 2)
            with sp.Fori(0, (NB - 10) // 2) as j:
                for k in range(2):
                    step(2 * j + (5 + k), (5 + k) % 2)
            for t in range(NB - 5, NB + 4):
                step(t, t % 2)
            sp.wait_ge(s_x1_out, 16 * NB)

        @block.gpsimd
        def _(pool):
            pool.memset(KS[:, :, :, :, :, :], 0.0).then_inc(s_zero_set, 1)
            pool.memset(V[:, :, HI, :, HD:HD + 1], 1.0).then_inc(s_v_ones, 1)
            pool.memset(V[:, :, LO, :, HD:HD + 1], 0.0).then_inc(s_v_ones, 1)
            pool.memset(eps[:, :], LN_EPS).then_inc(s_zero_set, 1)
            pool.memset(minus_half[:, :], -0.5).then_inc(s_zero_set, 1)
            pool.memset(zeros[:, :], 0.0).then_inc(s_tk_free, 1)
            pool.wait_ge(s_zero_set, 3)
            pool.wait_ge(s_tk_free, 1)
            pool.wait_ge(s_scales_set, 3)

            def rstd(n, which, mv, ve, rs, used):
                pool.wait_ge(mv, n + 1)
                pool.tensor_tensor(ln_ve[:, which:which + 1], ln_mv[:, which, 1:2], eps[:, :],
                                   ALU.add).then_inc(ve, 1)
                pool.wait_ge(ve, n + 1)
                need(pool, used, n)
                pool.tensor_tensor(ln_rs[:, which:which + 1], ln_ve[:, which:which + 1],
                                   minus_half[:, :], ALU.pow).then_inc(rs, 1)

            def split(a):
                return a.rearrange("p (c h j) -> p c h j", c=2, j=HD)

            def step(t, par, part=None, g=None, r=None):
                if has(t + 1):
                    n = t + 1
                    pool.wait_ge(s_qk_hi, n + 1)
                    pool.tensor_tensor(QS[:, :, 1, :], qkr[:, 0:D].rearrange("p (a c) -> p a c", a=PAIRS),
                                       QS[:, :, 0, :], ALU.subtract)
                    k = qkr[:, D:2 * D].rearrange("p (a u c) -> p a u c", a=PAIRS, u=2)
                    for u in range(2):
                        a = pool.tensor_tensor(KS[:, :, u, 2, u, :], k[:, :, u, :], KS[:, :, u, 0, u, :],
                                               ALU.subtract)
                    a.then_inc(s_qk_lo, 1)
                if has(t + 1):
                    n = t + 1
                    pool.wait_ge(s_v_hi, n + 1)
                    pool.tensor_tensor(V[:, 1 - par, LO, :, 0:HD],
                                       v32[:, :].rearrange("p (h d) -> p h d", d=HD),
                                       V[:, 1 - par, HI, :, 0:HD], ALU.subtract).then_inc(s_v_lo, 1)
                if has(t + 4):
                    rstd(t + 4, 0, s_ln1_mv, s_ln1_ve, s_ln1_rstd, s_xn_ready)
                if has(t - 2):
                    n = t - 2
                    pool.wait_ge(s_h_hi, n + 1)
                    pool.tensor_tensor(keep["H"][:, n, LO, :], h32[:, :], keep["H"][:, n, HI, :],
                                       ALU.subtract).then_inc(s_h_lo, 1)
                if has(t - 1):
                    n = t - 1
                    pool.wait_ge(s_xr_in, 16 * (n + 1))
                    pool.tensor_tensor(x_res[:, 1 - par, :], x_res[:, 1 - par, :], bo_g[:, :],
                                       ALU.add).then_inc(s_xrb, 1)
                if has(t - 3):
                    n = t - 3
                    pool.wait_ge(s_r_act, n + 1)
                    need(pool, s_r2, n)
                    pool.tensor_tensor(aT[:, HI, :], r_a[:, :], zeros[:, :], ALU.add).then_inc(s_a_hi, 1)
                if has(t + 2):
                    n = t + 2
                    pool.wait_ge(s_qk_sb, n + 1)
                    pool.tensor_tensor(
                        split(rot_a[:, :]), split(qk[:, :]),
                        rope[:, 0, :, :].unsqueeze(2).broadcast_to([P, 2, HEADS, HD]),
                        ALU.mult).then_inc(s_rot_cos, 1)
                    pool.wait_ge(s_rot_cos, n + 1)
                    pool.wait_ge(s_rot_sin, n + 1)
                    need(pool, s_qk_hi, n)
                    pool.tensor_tensor(qkr[:, :], rot_a[:, :], rot_b[:, :], ALU.add).then_inc(s_rot, 1)
                if has(t - 3):
                    n = t - 3
                    pool.wait_ge(s_a_hi, n + 1)
                    pool.tensor_tensor(aT[:, LO, :], r_a[:, :], aT[:, HI, :],
                                       ALU.subtract).then_inc(s_a_lo, 1)
                if has(t - 1):
                    rstd(t - 1, 1, s_ln2_mv, s_ln2_ve, s_ln2_rstd, s_h_sb)

            slots(pool, step)

        @block.tensor
        def _(pe):
            pe.wait_ge(s_ident_in, 16)
            for w in range(4):
                pe.wait_ge(s_w4_in[w], 16)
                dst = [*S_ps, *PT_ps][w]
                for k in range(K):
                    for c in range(K):
                        mm = pe.transpose(dst[:, (k * K + c) * P:(k * K + c + 1) * P],
                                          w_raw[:, w, c, k * P:(k + 1) * P], ident[:, :])
                mm.then_inc(s_wT_ps, 1)
            pe.wait_ge(s_wT_lo, 4)
            pe.wait_ge(s_rw_lo, 2)
            pe.wait_ge(s_ident16_set, 1)
            pe.wait_ge(s_v_ones, 2)

            def scores(n, c, par):
                g = 4 * n + c
                if c == 0:
                    pe.wait_ge(s_qkT_sb, 3 * n + 2)
                if c == 2:
                    pe.wait_ge(s_qkT_sb, 3 * n + 3)
                need(pe, s_exp_done, g - 1)
                for u in range(2):
                    mm = pe.matmul(S_ps[c % 2][:, 2 * P * u:2 * P * (u + 1)], QT[:, par, 2 * c + u, :],
                                   KT[:, par, 4 * c + 2 * u:4 * c + 2 * u + 2, :], start=True, stop=True)
                mm.then_inc(s_scores, 1)

            def turn_p(n, c):
                g = 4 * n + c
                pe.wait_ge(s_exp_done, g + 1)
                need(pe, s_p_lo, g - 1)
                for h in range(4):
                    mm = pe.transpose(PT_ps[c % 2][:, h * P:(h + 1) * P], Pr[:, c % 2, h, :], ident[:, :])
                mm.then_inc(s_p_T, 1)

            def weigh_v(n, c, par):
                g = 4 * n + c
                if c == 0:
                    pe.wait_ge(s_v_lo, n + 1)
                    need(pe, s_att_sb, n)
                    need(pe, s_logit, n - 3)
                pe.wait_ge(s_p_lo, g + 1)
                for hh in range(4):
                    h = 4 * c + hh
                    mm = three_pass(pe, att_ps[:, h, :], lambda a, k: PT[:, c % 2, a, hh, :],
                                    lambda b, k: V[:, par, b, h, :], [0])
                mm.then_inc(s_pv, 1)

            def project_qk(n, par):
                pe.wait_ge(s_xT_lo, n + 1)
                need(pe, s_qkT_sb, 3 * n - 1)
                three_pass(pe, qk_bank[:, 0:D], lambda a, k: xT[:, par, a, k, :],
                           lambda b, k: WT4[:, 0, b, k, :], range(K))
                three_pass(pe, qk_bank[:, D:2 * D], lambda a, k: xT[:, par, a, K + k, :],
                           lambda b, k: WT4[:, 1, b, k, :], range(K)).then_inc(s_qk_ps, 1)

            def project_v(n, par):
                need(pe, s_qkT_sb, 3 * n)
                need(pe, s_x1_done, n - 2)
                three_pass(pe, v_ps, lambda a, k: xT[:, par, a, K + k, :],
                           lambda b, k: WT4[:, 2, b, k, :], range(K)).then_inc(s_v_done_ps, 1)

            def turn_att(n, part, g):
                if part == "softmax":
                    pe.wait_ge(s_tk_exp, g + 1)
                pe.wait_ge(s_att_sb, n + 1)
                need(pe, s_xT_lo, upto(n + 4))
                need(pe, s_hT_lo, n - 1)
                need(pe, s_attT_lo, n)
                for k in range(K):
                    mm = pe.transpose(T_ps[:, k * P:(k + 1) * P], att[:, 8 * k:8 * k + 8, :], ident[:, :])
                mm.then_inc(s_att_T, 1)

            def turn_h(n, part, g):
                if part == "places":
                    pe.wait_ge(s_tk_free, g + 2)
                pe.wait_ge(s_h_sb, n + 1)
                need(pe, s_attT_lo, upto(n + 2))
                need(pe, s_xT_lo, upto(n + 5))
                need(pe, s_hT_lo, n)
                for k in range(K):
                    mm = pe.transpose(T_ps[:, k * P:(k + 1) * P], h32[:, k * P:(k + 1) * P], ident[:, :])
                mm.then_inc(s_hT_ps, 1)

            def turn_x(n, par):
                pe.wait_ge(s_xn_ready, n + 1)
                pe.wait_ge(s_c_in_done, 16 * (n + 1))
                need(pe, s_hT_lo, n - 4)
                need(pe, s_attT_lo, n - 3)
                need(pe, s_xT_lo, n)
                for k in range(K):
                    pe.transpose(T_ps[:, k * P:(k + 1) * P], xn[:, k * P:(k + 1) * P], ident[:, :])
                for k in range(K):
                    mm = pe.transpose(T_ps[:, (K + k) * P:(K + k + 1) * P],
                                      c_in[:, par, k * P:(k + 1) * P], ident[:, :])
                mm.then_inc(s_xT_ps, 1)

            def project_out(n):
                pe.wait_ge(s_attT_lo, n + 1)
                need(pe, s_qkT_sb, 3 * upto(n + 3))
                need(pe, s_x1_done, n)
                three_pass(pe, o_ps, lambda a, k: attT[:, a, k, :],
                           lambda b, k: WT4[:, 3, b, k, :], range(K)).then_inc(s_o_done, 1)

            def turn_q_k0(n):
                pe.wait_ge(s_qk_lo, n + 1)
                pe.wait_ge(s_v_sb, n + 1)
                for p in range(PAIRS):
                    mm = pe.transpose(fill_a[0:96, p, :], QS[:, p, :, :], ident16[:, :])
                mm.then_inc(s_qkT_ps, 1)
                need(pe, s_r_tanh, n - 3)
                for h in range(HEADS // 2):
                    mm = pe.transpose(fill_b[0:96, h, :], KS[:, h // 2, h % 2, :, :, :], ident16[:, :])
                mm.then_inc(s_qkT_ps, 1)

            def turn_k1(n):
                pe.wait_ge(s_qkT_sb, 3 * n + 1)
                for h in range(HEADS // 2, HEADS):
                    mm = pe.transpose(fill_a[0:96, h - HEADS // 2, :], KS[:, h // 2, h % 2, :, :, :],
                                      ident16[:, :])
                mm.then_inc(s_qkT_ps, 1)

            def route_1(n):
                pe.wait_ge(s_hT_lo, n + 1)
                pe.wait_ge(s_qk_sb, upto(n + 5))
                pe.wait_ge(s_qkT_sb, 3 * upto(n + 4))
                need(pe, s_r_tanh, n)
                three_pass(pe, r1_ps, lambda a, k: rw1[:, a, k, :],
                           lambda b, k: hT[:, b, k, :], range(K)).then_inc(s_r1, 1)

            def route_2(n):
                pe.wait_ge(s_a_lo, n + 1)
                need(pe, s_logit, n)
                need(pe, s_att_sb, upto(n + 3))
                three_pass(pe, r2_ps, lambda a, k: aT[:, a, :],
                           lambda b, k: rw2[:, b, :], [0]).then_inc(s_r2, 1)

            def turn_logits(g, t):
                pe.wait_ge(s_tk_copy, g + 1)
                pe.wait_ge(s_tk_free, g + 1)
                pe.wait_ge(s_xT_lo, upto(t + 3))
                pe.wait_ge(s_attT_lo, upto(t - 1))
                pe.wait_ge(s_hT_lo, upto(t - 2))
                pe.transpose(T_ps[:, 0:P], Lg[:, :], ident[:, :]).then_inc(s_tk_T, 1)

            def turn_routing(g, t):
                pe.wait_ge(s_tk_res, 2 * (g + 1))
                pe.wait_ge(s_xT_lo, upto(t + 3))
                pe.wait_ge(s_attT_lo, upto(t))
                pe.wait_ge(s_hT_lo, upto(t - 2))
                pe.transpose(T_ps[:, 0:P], t_pos[:, :], ident[:, :])
                pe.transpose(T_ps[:, P:2 * P], t_wt[:, :], ident[:, :]).then_inc(s_tk_T2, 1)

            def step(t, par, part=None, g=None, r=None):
                if has(t - 1):
                    weigh_v(t - 1, 3, 1 - par)
                if has(t):
                    scores(t, 2, par)
                    turn_p(t, 0)
                if part == "softmax":
                    turn_logits(g, t)
                if has(t + 1):
                    turn_q_k0(t + 1)
                if has(t - 1):
                    turn_att(t - 1, part, g)
                if has(t):
                    turn_p(t, 1)
                    scores(t, 3, par)
                if has(t + 1):
                    turn_k1(t + 1)
                if has(t + 2):
                    project_qk(t + 2, par)
                if part == "places":
                    turn_routing(g, t)
                if has(t + 1):
                    scores(t + 1, 0, 1 - par)
                if has(t):
                    weigh_v(t, 0, par)
                if has(t - 2):
                    turn_h(t - 2, part, g)
                if has(t):
                    turn_p(t, 2)
                if has(t - 1):
                    project_out(t - 1)
                if has(t):
                    weigh_v(t, 1, par)
                    turn_p(t, 3)
                if has(t + 3):
                    turn_x(t + 3, 1 - par)
                if has(t + 2):
                    project_v(t + 2, par)
                if has(t + 1):
                    scores(t + 1, 1, 1 - par)
                if has(t):
                    weigh_v(t, 2, par)
                if has(t - 2):
                    route_1(t - 2)
                if has(t - 3):
                    route_2(t - 3)

            slots(pe, step)

            turn_logits(NG - 1, NB + 4)
            turn_routing(NG - 1, NB + 4)

        @block.scalar
        def _(act):
            def high(out, in_, scale=1.0):
                return act.activation(out, in_, ACT.Copy, scale=scale)

            act.wait_ge(s_ident_in, 16)
            high(ident16[:, :], ident[:, :]).then_inc(s_ident16_set, 1)
            for w in range(4):
                act.wait_ge(s_wT_ps, w + 1)
                high(WT4[:, w, HI, :, :], [*S_ps, *PT_ps][w][:, :], W_UP).then_inc(s_wT_hi, 1)
            act.wait_ge(s_small_in, SMALL_IN)
            act.activation(tanh_g[:, :], gates[:, :], ACT.Tanh).then_inc(s_tanh_done, 1)
            high(rw1[:, HI, :, :], rw1_raw[:, :, :], W_UP).then_inc(s_rw_hi, 1)
            high(rw2[:, HI, :], rw2_raw[:, :], W_UP).then_inc(s_rw_hi, 1)
            act.wait_ge(s_zero_set, 3)
            act.wait_ge(s_v_ones, 2)

            def exps(n, c):
                g = 4 * n + c
                act.wait_ge(s_min_done, g + 1)
                need(act, s_p_T, g - 1)
                for h in range(4):
                    a = act.activation(Pr[:, c % 2, h, :], S_ps[c % 2][:, h * P:(h + 1) * P], ACT.Exp,
                                       bias=mn[:, c % 2, h:h + 1], scale=-1.0)
                a.then_inc(s_exp_done, 1)

            def p_high(n, c):
                g = 4 * n + c
                act.wait_ge(s_p_T, g + 1)
                need(act, s_pv, g - 1)
                high(PT[:, c % 2, HI, :, :], PT_ps[c % 2][:, :]).then_inc(s_p_hi, 1)

            def turned_high(n, i, par):
                dst, src = ((QT[:, par, :, :], fill_a), (KT[:, par, 0:8, :], fill_b),
                            (KT[:, par, 8:16, :], fill_a))[i]
                act.wait_ge(s_qkT_ps, 3 * n + i + 1)
                need(act, s_scores, 4 * (n - 1))
                high(dst, src[0:96, :, :]).then_inc(s_qkT_sb, 1)

            def tk_exp(g):
                act.wait_ge(s_tk_neg, g + 1)
                act.activation(t_e[:, :], T_ps[:, 0:P], ACT.Exp, bias=t_nm[:, :],
                               accum_out=t_sum[:, :]).then_inc(s_tk_exp, 1)

            def tk_keep(g):
                act.wait_ge(s_tk_T2, g + 1)
                high(keep["POS"][:, g, :, :, :], T_ps[:, 0:P].rearrange(
                    "p (b q i) -> p q b i", b=GB, q=E // QE))
                high(keep["WT"][:, g, :, :, :], T_ps[:, P:2 * P].rearrange(
                    "p (b q i) -> p q i b", b=GB, q=E // QE)).then_inc(s_tk_free, 1)

            def step(t, par, part=None, g=None, r=None):
                if has(t):
                    exps(t, 0)
                if has(t - 3):
                    n = t - 3
                    act.wait_ge(s_r1, n + 1)
                    need(act, s_r_act, n)
                    act.activation(r_t[:, :], r1_ps, ACT.Tanh, scale=0.5 / W_UP)
                    act.activation(r_z[:, :], r1_ps, ACT.Copy, scale=1.0 / W_UP).then_inc(s_r_tanh, 1)
                if has(t):
                    exps(t, 1)
                    p_high(t, 0)
                if part == "softmax":
                    tk_exp(g)
                if has(t + 1):
                    turned_high(t + 1, 0, 1 - par)
                    turned_high(t + 1, 1, 1 - par)
                if has(t - 1):
                    n = t - 1
                    act.wait_ge(s_att_T, n + 1)
                    need(act, s_o_done, n)
                    high(attT[:, HI, :, :], T_ps[:, 0:D], ATT_UP).then_inc(s_attT_hi, 1)
                if has(t):
                    exps(t, 2)
                    p_high(t, 1)
                if part == "places":
                    tk_keep(g)
                if has(t + 1):
                    turned_high(t + 1, 2, 1 - par)
                if has(t - 2):
                    n = t - 2
                    act.wait_ge(s_hT_ps, n + 1)
                    need(act, s_r1, n)
                    high(hT[:, HI, :, :], T_ps[:, 0:D]).then_inc(s_hT_hi, 1)
                if has(t):
                    exps(t, 3)
                    p_high(t, 2)
                    p_high(t, 3)
                if has(t + 3):
                    n = t + 3
                    act.wait_ge(s_xT_ps, n + 1)
                    need(act, s_v_done_ps, n - 1)
                    high(xT[:, 1 - par, HI, :, :], T_ps[:, :]).then_inc(s_xT_hi, 1)
                if has(t + 2):
                    n = t + 2
                    act.wait_ge(s_rot, n + 1)
                    need(act, s_qkT_ps, 3 * n)
                    q = qkr[:, 0:D].rearrange("p (a o c) -> p a o c", a=PAIRS, o=1)
                    k = qkr[:, D:2 * D].rearrange("p (a u c) -> p a u c", a=PAIRS, u=2)
                    high(QS[:, :, 0:3:2, :], q.broadcast_to([P, PAIRS, 2, 32]))
                    for u in range(2):
                        a = high(KS[:, :, u, 0:2, u, :],
                                 k[:, :, u:u + 1, :].broadcast_to([P, PAIRS, 2, HD]))
                    a.then_inc(s_qk_hi, 1)

            slots(act, step)

            tk_exp(NG - 1)
            tk_keep(NG - 1)

        @block.vector
        def _(dve):
            def low(out, in_, hi, scale=1.0):
                return dve.scalar_tensor_tensor(out=out, in0=in_, scalar=scale, in1=hi,
                                                op0=ALU.mult, op1=ALU.subtract)

            def halves(a):
                return a[:, :].rearrange("p (c h t j) -> p c h t j", c=2, t=2, j=HD // 2)

            for w in range(4):
                dve.wait_ge(s_wT_hi, w + 1)
                low(WT4[:, w, LO, :, :], [*S_ps, *PT_ps][w][:, :].rearrange("p (k e) -> p k e", k=K),
                    WT4[:, w, HI, :, :], W_UP).then_inc(s_wT_lo, 1)
            dve.wait_ge(s_rw_hi, 2)
            low(rw1[:, LO, :, :], rw1_raw[:, :, :], rw1[:, HI, :, :], W_UP).then_inc(s_rw_lo, 1)
            low(rw2[:, LO, :], rw2_raw[:, :], rw2[:, HI, :], W_UP).then_inc(s_rw_lo, 1)
            dve.wait_ge(s_tanh_done, 1)
            dve.tensor_scalar(x_scale[:, :], tanh_g[:, 0:1], 1.0 / (W_UP * ATT_UP), None,
                              ALU.mult).then_inc(s_scales_set, 1)
            dve.tensor_scalar(w_scale[:, :], tanh_g[:, 1:2], 1.0 / Y_DOWN, None,
                              ALU.mult).then_inc(s_scales_set, 1)
            dve.tensor_scalar(bo_g[:, :], bvo[:, 1, :], tanh_g[:, 0:1], None,
                              ALU.mult).then_inc(s_scales_set, 1)
            dve.wait_ge(s_scales_set, 3)
            dve.wait_ge(s_small_in, SMALL_IN)

            def minima(n, c):
                g = 4 * n + c
                dve.wait_ge(s_scores, g + 1)
                need(dve, s_exp_done, g - 1)
                dve.tensor_reduce(mn[:, c % 2, :], S_ps[c % 2][:, :].rearrange("p (h k) -> p h k", h=4),
                                  AX_X, ALU.min).then_inc(s_min_done, 1)

            def p_low(n, c):
                g = 4 * n + c
                dve.wait_ge(s_p_hi, g + 1)
                dve.tensor_tensor(PT[:, c % 2, LO, :, :], PT_ps[c % 2][:, :].rearrange("p (h q) -> p h q", h=4),
                                  PT[:, c % 2, HI, :, :], ALU.subtract).then_inc(s_p_lo, 1)

            def tick(use):
                dve.memset(spare[:, use:use + 1], 0.0)

            def norm_stats(n, which, in_, stat):
                dve.bn_stats(ln_st[:, which, :], in_).then_inc(stat, 1)

            def norm_moments(n, which, stat, mv, used):
                need(dve, used, n)
                dve.wait_ge(stat, n + 1)
                tick(which)
                dve.bn_aggr(ln_mv[:, which, :], ln_st[:, which, :]).then_inc(mv, 1)

            def norm_apply(out, in_, which):
                return dve.tensor_scalar(out, in_, ln_mv[:, which, 0:1], ln_rs[:, which:which + 1],
                                         ALU.subtract, ALU.mult)

            def top(g, r, w):
                dve.wait_ge(s_tk_rest, (ROUNDS + 1) * g + r + 1)
                tick(2)
                dve.max(t_m8[:, :], t_w[:, w, :]).then_inc(s_tk_top, 1)

            def replace(g, r, w):
                dve.wait_ge(s_tk_top, ROUNDS * g + r + 1)
                tick(3)
                dve.match_replace(t_w[:, 1 - w, :], t_m8[:, :], t_w[:, w, :], -1.0).then_inc(s_tk_rest, 1)

            def routing(at, part, g, r):
                if part == "softmax":
                    if at == 0:
                        dve.wait_ge(s_logit, GB * (g + 1))
                        dve.tensor_copy(Lg[:, :], L[:, :, :].rearrange(
                            "p (g b) e -> p g (b e)", b=GB)[:, g, :]).then_inc(s_tk_copy, 1)
                    if at == 1:
                        dve.wait_ge(s_tk_T, g + 1)
                        dve.tensor_reduce(t_mx[:, :], T_ps[:, 0:P], AX_X, ALU.max).then_inc(s_tk_max, 1)
                        dve.wait_ge(s_tk_max, g + 1)
                        dve.tensor_scalar(t_nm[:, :], t_mx[:, :], -1.0, None, ALU.mult).then_inc(s_tk_neg, 1)
                if part == "probabilities":
                    if at == 0:
                        dve.wait_ge(s_tk_exp, g + 1)
                        dve.reciprocal(t_rs[:, :], t_sum[:, :]).then_inc(s_tk_rec, 1)
                    if at == 1:
                        dve.wait_ge(s_tk_rec, g + 1)
                        for p in (t_p[:, :], t_w[:, 1, :]):
                            a = dve.tensor_scalar(p, t_e[:, :], t_rs[:, 0:1], None, ALU.mult)
                        a.then_inc(s_tk_rest, 1)
                if part == "rounds":
                    if at == 0:
                        top(g, r, 1)
                    if at == 1:
                        replace(g, r, 1)
                    if at == 2:
                        top(g, r + 1, 0)
                    if at == 3:
                        replace(g, r + 1, 0)
                if part == "weights":
                    if at == 0:
                        dve.wait_ge(s_tk_rest, (ROUNDS + 1) * (g + 1))
                        dve.tensor_scalar(t_msk[:, :], t_w[:, 1, :], 0.0, None,
                                          ALU.is_lt).then_inc(s_tk_msk, 1)
                    if at == 1:
                        dve.wait_ge(s_tk_msk, g + 1)
                        dve.tensor_tensor_scan(t_cum[:, :], t_msk[:, :], zeros[:, :], 0.0, ALU.add,
                                               ALU.add).then_inc(s_tk_cum, 1)
                        dve.scalar_tensor_tensor(out=t_pm[:, :], in0=t_p[:, :], scalar=1.0,
                                                 in1=t_msk[:, :], op0=ALU.mult, op1=ALU.mult,
                                                 accum_out=t_ps[:, :]).then_inc(s_tk_sum, 1)
                    if at == 2:
                        dve.wait_ge(s_tk_sum, g + 1)
                        dve.tensor_scalar(t_dn[:, :], t_ps[:, :], 1e-9, None, ALU.add).then_inc(s_tk_den, 1)
                    if at == 3:
                        dve.wait_ge(s_tk_den, g + 1)
                        dve.reciprocal(t_rd[:, :], t_dn[:, :]).then_inc(s_tk_rden, 1)
                if part == "places":
                    if at == 0:
                        dve.wait_ge(s_tk_rden, g + 1)
                        dve.tensor_tensor(t_wr[:, :], t_rd[:, :], w_scale[:, :], ALU.mult).then_inc(s_tk_wr, 1)
                    if at == 1:
                        dve.wait_ge(s_tk_wr, g + 1)
                        dve.wait_ge(s_tk_cum, g + 1)
                        dve.tensor_scalar(t_wt[:, :], t_pm[:, :], t_wr[:, 0:1], None,
                                          ALU.mult).then_inc(s_tk_res, 1)
                        dve.tensor_tensor(t_pos[:, :], t_cum[:, :], t_msk[:, :],
                                          ALU.mult).then_inc(s_tk_res, 1)

            def step(t, par, part=None, g=None, r=None):
                if has(t):
                    minima(t, 1)
                if has(t + 1):
                    n = t + 1
                    dve.wait_ge(s_v_done_ps, n + 1)
                    need(dve, s_v_lo, n)
                    dve.scalar_tensor_tensor(out=v32[:, :], in0=v_ps, scalar=1.0 / W_UP, in1=bvo[:, 0, :],
                                             op0=ALU.mult, op1=ALU.add).then_inc(s_v_sb, 1)
                routing(0, part, g, r)
                if has(t - 1):
                    n = t - 1
                    need(dve, s_r2, upto(n - 2))
                    dve.wait_ge(s_pv, 4 * (n + 1))
                    dve.reciprocal(den[:, :], att_ps[:, :, HD]).then_inc(s_recip_den, 1)
                routing(1, part, g, r)
                if has(t - 4):
                    n = t - 4
                    dve.wait_ge(s_pv, 4 * upto(n + 4))
                    dve.wait_ge(s_r2, n + 1)
                    dve.tensor_scalar(L[:, n, :], r2_ps, 0.5 / W_UP, None, ALU.mult).then_inc(s_logit, 1)
                if has(t - 1):
                    n = t - 1
                    dve.wait_ge(s_recip_den, n + 1)
                    need(dve, s_att_T, n)
                    dve.tensor_tensor(att[:, :, :], att_ps[:, :, 0:HD],
                                      den[:, :].unsqueeze(2).broadcast_to([P, HEADS, HD]),
                                      ALU.mult).then_inc(s_att_sb, 1)
                if has(t):
                    minima(t, 2)
                if has(t + 4):
                    n = t + 4
                    dve.wait_ge(s_x_in_done, 16 * (n + 1))
                    norm_stats(n, 0, x_in[:, par, :], s_ln1_stat)
                if has(t - 2):
                    n = t - 2
                    dve.wait_ge(s_ln2_rstd, n + 1)
                    need(dve, s_hT_ps, n)
                    need(dve, s_h_lo, n)
                    norm_apply(h32[:, :], x1[:, par, :], 1).then_inc(s_h_sb, 1)
                if has(t + 1):
                    n = t + 1
                    dve.wait_ge(s_v_sb, n + 1)
                    need(dve, s_pv, 4 * (n - 1))
                    dve.tensor_copy(V[:, 1 - par, HI, :, 0:HD],
                                    v32[:, :].rearrange("p (h d) -> p h d", d=HD)).then_inc(s_v_hi, 1)
                if has(t - 3):
                    n = t - 3
                    dve.wait_ge(s_r_tanh, n + 1)
                    need(dve, s_a_lo, n)
                    dve.scalar_tensor_tensor(out=r_a[:, :], in0=r_t[:, :], scalar=1.0, in1=r_z[:, :],
                                             op0=ALU.add, op1=ALU.mult).then_inc(s_r_act, 1)
                if has(t + 4):
                    norm_moments(t + 4, 0, s_ln1_stat, s_ln1_mv, s_ln1_rstd)
                if has(t):
                    p_low(t, 0)
                if has(t - 2):
                    n = t - 2
                    dve.wait_ge(s_h_sb, n + 1)
                    dve.tensor_copy(keep["H"][:, n, HI, :], h32[:, :]).then_inc(s_h_hi, 1)
                routing(2, part, g, r)
                if has(t - 1):
                    n = t - 1
                    dve.wait_ge(s_attT_hi, n + 1)
                    low(attT[:, LO, :, :], T_ps[:, 0:D].rearrange("p (k q) -> p k q", k=K),
                        attT[:, HI, :, :], ATT_UP).then_inc(s_attT_lo, 1)
                if has(t):
                    minima(t, 3)
                if has(t + 2):
                    n = t + 2
                    dve.wait_ge(s_qk_ps, n + 1)
                    need(dve, s_rot_cos, n)
                    dve.scalar_tensor_tensor(out=qk[:, :], in0=qk_bank[:, :], scalar=1.0 / W_UP,
                                             in1=bqk[:, :, :].rearrange("p a d -> p (a d)"), op0=ALU.mult,
                                             op1=ALU.add).then_inc(s_qk_sb, 1)
                if has(t):
                    p_low(t, 1)
                if has(t + 2):
                    n = t + 2
                    dve.wait_ge(s_qk_sb, n + 1)
                    need(dve, s_rot, n)
                    for half in range(2):
                        a = dve.tensor_tensor(
                            halves(rot_b)[:, :, :, half, :], halves(qk)[:, :, :, 1 - half, :],
                            rope[:, 1, :, half * 8:half * 8 + 8].unsqueeze(2).broadcast_to([P, 2, HEADS, 8]),
                            ALU.mult)
                    a.then_inc(s_rot_sin, 1)
                routing(3, part, g, r)
                if has(t - 2):
                    n = t - 2
                    dve.wait_ge(s_hT_hi, n + 1)
                    dve.tensor_tensor(hT[:, LO, :, :], T_ps[:, 0:D].rearrange("p (k q) -> p k q", k=K),
                                      hT[:, HI, :, :], ALU.subtract).then_inc(s_hT_lo, 1)
                if has(t + 1):
                    minima(t + 1, 0)
                if has(t - 1):
                    n = t - 1
                    dve.wait_ge(s_o_done, n + 1)
                    dve.wait_ge(s_xrb, n + 1)
                    need(dve, s_x1_out, 16 * (n - 1))
                    dve.scalar_tensor_tensor(out=x1[:, 1 - par, :], in0=o_ps, scalar=x_scale[:, 0:1],
                                             in1=x_res[:, 1 - par, :], op0=ALU.mult,
                                             op1=ALU.add).then_inc(s_x1_done, 1)
                if has(t):
                    p_low(t, 2)
                if has(t - 1):
                    n = t - 1
                    dve.wait_ge(s_x1_done, n + 1)
                    norm_stats(n, 1, x1[:, 1 - par, :], s_ln2_stat)
                if has(t + 4):
                    n = t + 4
                    dve.wait_ge(s_ln1_rstd, n + 1)
                    need(dve, s_xT_ps, n)
                    norm_apply(xn[:, :], x_in[:, par, :], 0).then_inc(s_xn_ready, 1)
                if has(t - 1):
                    norm_moments(t - 1, 1, s_ln2_stat, s_ln2_mv, s_ln2_rstd)
                if has(t + 3):
                    n = t + 3
                    dve.wait_ge(s_xT_hi, n + 1)
                    dve.tensor_tensor(xT[:, 1 - par, LO, :, :], T_ps[:, :].rearrange("p (k q) -> p k q", q=P),
                                      xT[:, 1 - par, HI, :, :], ALU.subtract).then_inc(s_xT_lo, 1)
                if has(t):
                    p_low(t, 3)

            slots(dve, step)

            for part in ("softmax", "probabilities"):
                for at in range(4):
                    routing(at, part, NG - 1, None)
            for r in range(0, ROUNDS, 2):
                for at in range(4):
                    routing(at, "rounds", NG - 1, r)
            for part in ("weights", "places"):
                for at in range(4):
                    routing(at, part, NG - 1, None)


def expert_phase(nc, io, keep, dims):
    NB, D, E, F = dims["NB"], dims["D"], dims["E"], dims["F"]
    K = D // P
    FC = F // P
    TILES = GB * TOP // P
    NG, NQ = NB // GB, (NB // GB) * (E // QE)
    NT = GB * TOP
    assert FC == 4 and TILES == 4 and K == 2 and NQ % 2 == 0
    ctx = ExitStack()
    with ctx:
        def sb(name, shape, dt=F32):
            return ctx.enter_context(nc.sbuf_tensor(name, shape, dt))

        def bank(name):
            return ctx.enter_context(nc.psum_tensor(name, [P, 512], F32))

        def sem(name):
            return ctx.enter_context(nc.semaphore(name))

        raw = [sb("w1_raw", [P, K, F]), sb("w2_raw", [P, K, F]), sb("w3_raw", [P, FC, D])]
        W1 = sb("W1", [P, 2, 2, K, F], F16)
        W2 = sb("W2", [P, 2, 2, K, F], F16)
        W3 = sb("W3", [P, 2, 2, FC, D], F16)
        parts = [W1, W2, W3]
        ident16 = keep["ident16"]
        pick = sb("pick", [P, 2, TILES, QE, 2, TOP], F16)
        X = sb("X", [P, 2, QE, 2, K, NT], F16)
        sg = sb("sg", [P, 2, NT])
        u32 = sb("u32", [P, 2, NT])
        U = sb("U", [P, 2, 2, FC, NT], F16)
        place = sb("place", [P, 2, TILES, 2, P], F16)
        Y = sb("Y", [P, 2, 2, D], F16)
        acc = sb("acc", [P, 2, GB, D])

        G_ps = [bank("G0_ps"), bank("G1_ps")]
        V_ps = [bank("V0_ps"), bank("V1_ps")]
        Y_ps = bank("Y_ps")
        S_ps = bank("Sc_ps")
        X_ps = bank("X_ps")
        place_ps = bank("place_ps")
        first_banks = [X_ps, Y_ps, S_ps, V_ps[1]]
        last_banks = [X_ps, Y_ps]
        place16 = place_ps[:, 0:256].bitcast(F16).rearrange("p (t s) -> p t s", t=TILES)

        s_acc_in = sem("acc_in")
        s_acc_out = sem("acc_out")
        s_pick_set = sem("pick_set")
        s_x_ps = sem("x_ps")
        s_x_sb = sem("x_sb")
        s_g_ps = sem("g_ps")
        s_v_ps = sem("v_ps")
        s_silu_done = sem("silu_done")
        s_u_done = sem("u_done")
        s_u_hi = sem("u_hi")
        s_u_lo = sem("u_lo")
        s_place_ps_done = sem("place_ps_done")
        s_place_sb = sem("place_sb")
        s_y_ps = sem("y_ps")
        s_y_hi = sem("y_hi")
        s_y_lo = sem("y_lo")
        s_sc_ps = sem("sc_ps")
        s_acc_done = sem("acc_done")
        w_in = [sem(f"w{i + 1}_in") for i in range(3)]
        w_hi = [sem(f"w{i + 1}_hi") for i in range(3)]
        w_lo = [sem(f"w{i + 1}_lo") for i in range(3)]

        block = ctx.enter_context(nc.Block())

        def lin(unit):
            return QE * unit[0] + unit[2]

        def before(unit):
            if unit is None:
                return None
            q, par, i = unit
            if i:
                return q, par, i - 1
            return None if isinstance(q, int) and q == 0 else (q - 1, 1 - par, QE - 1)

        def units(eng, step, tail):
            for i in range(QE):
                step((0, 0, i), True)
            with eng.Fori(0, (NQ - 2) // 2) as j:
                for k in range(2):
                    for i in range(QE):
                        step((2 * j + 1 + k, (1 + k) % 2, i), True)
            for i in range(QE):
                step((NQ - 1, (NQ - 1) % 2, i), False)
            tail((NQ - 1, (NQ - 1) % 2, QE - 1))

        def rows(b):
            return slice(TOP * b, TOP * (b + 1))

        def ends(i, f):
            return i == QE - 1 and f == FC - 1

        def group_of(q):
            return q // (E // QE)

        @block.sync
        def _(sp):
            src = [w.rearrange("e (c p) f -> e p c f", p=P) for w in (io["w1"], io["w2"], io["w3"])]

            def load(e, u):
                for m in range(3):
                    need(sp, w_hi[m], u)
                    need(sp, w_lo[m], u)
                    sp.dma_start(raw[m][:, :, :], src[m][e]).then_inc(w_in[m], 16)

            out_g = io["out"].rearrange("(g b) p d -> g p b d", b=GB)

            def acc_load(g):
                return sp.dma_start(acc[:, g % 2, :, :],
                                    out_g[g])

            def acc_store(g):
                return sp.dma_start(out_g[g],
                                    acc[:, g % 2, :, :])

            load(0, 0)
            acc_load(0).then_inc(s_acc_in, 16)
            for e in range(1, 8):
                load(e, e)
            if NG > 1:
                sp.wait_ge(s_acc_in, 16)
                acc_load(1).then_inc(s_acc_in, 16)
            for e in range(8, E):
                load(e, e)
            if NG > 2:
                with sp.Fori(1, NG - 1) as g:
                    with sp.Fori(0, 4) as e:
                        load(e, E * g + e)
                    sp.wait_ge(s_acc_done, TILES * E * g)
                    acc_store(g - 1).then_inc(s_acc_out, 16)
                    with sp.Fori(4, 8) as e:
                        load(e, E * g + e)
                    sp.wait_ge(s_acc_out, 16 * g)
                    sp.wait_ge(s_acc_in, 16 * (g + 1))
                    acc_load(g + 1).then_inc(s_acc_in, 16)
                    with sp.Fori(8, E) as e:
                        load(e, E * g + e)
            if NG > 1:
                for e in range(4):
                    load(e, E * (NG - 1) + e)
                sp.wait_ge(s_acc_done, TILES * E * (NG - 1))
                acc_store(NG - 2).then_inc(s_acc_out, 16)
                for e in range(4, E):
                    load(e, E * (NG - 1) + e)
            for t in range(TILES):
                sp.wait_ge(s_acc_done, TILES * (E * NG - 1) + t + 1)
                pair = slice(2 * t, 2 * t + 2)
                sp.dma_start(out_g[NG - 1][:, pair, :], acc[:, (NG - 1) % 2, pair, :]).then_inc(s_acc_out, 16)
            sp.wait_ge(s_acc_out, 16 * (NG - 1 + TILES))

        @block.tensor
        def _(pe):
            def gather(q, par, j, dst=X_ps, banks=1):
                b, part = j // 2, j % 2
                pe.wait_ge(s_pick_set, 4 * q + b // 2 + 1)
                need(pe, s_x_sb, 16 * q + j + 1 - banks)
                for k in range(K):
                    mm = pe.matmul(dst[:, 256 * k:256 * (k + 1)],
                                   keep["H"][:, GB * group_of(q) + b, part, k * P:(k + 1) * P],
                                   pick[:, par, b // 2, :, b % 2, :], start=True, stop=True)
                mm.then_inc(s_x_ps, 1)

            def up(unit, f):
                q, par, i = unit
                n = 4 * lin(unit) + f
                if f == 0:
                    if i == 0:
                        pe.wait_ge(s_x_sb, 16 * (q + 1))
                    pe.wait_ge(w_lo[0], lin(unit) + 1)
                need(pe, s_silu_done, n - 1)
                three_pass(pe, G_ps[f % 2][:, :], lambda a, k: W1[:, i % 2, a, k, f * P:(f + 1) * P],
                           lambda b, k: X[:, par, i, b, k, :], range(K)).then_inc(s_g_ps, 1)
                if f == 0:
                    pe.wait_ge(w_lo[1], lin(unit) + 1)
                need(pe, s_u_done, n - 1)
                three_pass(pe, V_ps[f % 2][:, :], lambda a, k: W2[:, i % 2, a, k, f * P:(f + 1) * P],
                           lambda b, k: X[:, par, i, b, k, :], range(K)).then_inc(s_v_ps, 1)

            def down(unit, t, dst=Y_ps, banks=1):
                i = unit[2]
                n = 4 * lin(unit) + t
                if t == 0:
                    pe.wait_ge(s_u_hi, 4 * lin(unit) + 4)
                    pe.wait_ge(s_u_lo, 4 * lin(unit) + 4)
                    pe.wait_ge(w_lo[2], lin(unit) + 1)
                need(pe, s_y_lo, n + 1 - banks)
                three_pass(pe, dst[:, 0:D],
                           lambda a, k: U[:, i % 2, a, k, t * P:(t + 1) * P],
                           lambda b, k: W3[:, i % 2, b, k, :], range(FC)).then_inc(s_y_ps, 1)

            def scatter(unit, t):
                i = unit[2]
                n = 4 * lin(unit) + t
                if t == 0:
                    pe.wait_ge(s_place_sb, 4 * (lin(unit) + 1))
                pe.wait_ge(s_y_lo, n + 1)
                need(pe, s_acc_done, n)
                for b in range(2):
                    mm = pe.matmul(S_ps[:, D * b:D * (b + 1)], place[:, i % 2, t, b, :],
                                   Y[:, t % 2, b, :], start=True, stop=True)
                mm.then_inc(s_sc_ps, 1)

            def turn_pick(unit, t):
                q, par, i = unit
                if t == 0:
                    need(pe, s_place_sb, 4 * lin(unit))
                mm = pe.transpose(place16[:, t, :], pick[:, par, t, i, :, :], ident16[:, :])
                if t == TILES - 1:
                    mm.then_inc(s_place_ps_done, 1)

            def step(unit, more):
                q, par, i = unit
                last, last2 = before(unit), before(before(unit))
                for f in range(FC):
                    up(unit, f)
                    if more and ends(i, f):
                        gather(q + 1, 1 - par, QE * i + f)
                    if last:
                        down(last, f)
                    if f and last:
                        scatter(last, f - 1)
                    if f == 0 and last2:
                        scatter(last2, TILES - 1)
                    if more and not ends(i, f):
                        gather(q + 1, 1 - par, QE * i + f)
                    turn_pick(unit, f)

            def tail(unit):
                for t in range(TILES):
                    down(unit, t, last_banks[t % 2], 2)
                    if t:
                        scatter(unit, t - 1)
                    else:
                        scatter(before(unit), TILES - 1)
                scatter(unit, TILES - 1)

            for j in range(16):
                gather(0, 0, j, first_banks[j % 4], 4)
            units(pe, step, tail)

        @block.scalar
        def _(act):
            def high(out, in_, scale=1.0):
                return act.activation(out, in_, ACT.Copy, scale=scale)

            def weights(m, unit):
                n, i = lin(unit), unit[2]
                act.wait_ge(w_in[m], 16 * (n + 1))
                need(act, [s_g_ps, s_v_ps, s_y_ps][m], 4 * (n - 1))
                high(parts[m][:, i % 2, HI, :, :], raw[m][:, :, :], W_UP).then_inc(w_hi[m], 1)

            def tokens(q, par, j, src=X_ps):
                b, part = j // 2, j % 2
                act.wait_ge(s_x_ps, 16 * q + j + 1)
                need(act, s_v_ps, 16 * (q - 1))
                high(X[:, par, :, part, :, b * TOP:(b + 1) * TOP].rearrange("p e k c -> p k e c"),
                     src[:, :].rearrange("p (k e c) -> p k e c", k=K, e=QE)).then_inc(s_x_sb, 1)

            def places(unit):
                n, i = lin(unit), unit[2]
                act.wait_ge(s_place_ps_done, n + 1)
                need(act, s_sc_ps, 4 * (n - 1))
                for b in range(2):
                    for half in range(2):
                        high(place[rows(half), i % 2, :, b, :],
                             place16[rows(b), :, :]).then_inc(s_place_sb, 1)

            def u_high(unit, f):
                n, i = 4 * lin(unit) + f, unit[2]
                act.wait_ge(s_u_done, n + 1)
                need(act, s_y_ps, 4 * (lin(unit) - 1))
                high(U[:, i % 2, HI, f, :], u32[:, f % 2, :]).then_inc(s_u_hi, 1)

            def y_high(unit, t, src=Y_ps):
                n = 4 * lin(unit) + t
                act.wait_ge(s_y_ps, n + 1)
                need(act, s_sc_ps, n - 1)
                for b in range(2):
                    a = high(Y[rows(b), t % 2, b, :], src[rows(b), 0:D], Y_DOWN / W_UP)
                a.then_inc(s_y_hi, 1)

            def step(unit, more):
                q, par, i = unit
                last = before(unit)
                for f in range(FC):
                    n = 4 * lin(unit) + f
                    act.wait_ge(s_g_ps, n + 1)
                    need(act, s_u_done, n - 1)
                    act.activation(sg[:, f % 2, :], G_ps[f % 2][:, :], ACT.Silu,
                                   scale=1.0 / W_UP).then_inc(s_silu_done, 1)
                    if f:
                        u_high(unit, f - 1)
                    if f == 0 and last:
                        places(last)
                    if more and ends(i, f):
                        tokens(q + 1, 1 - par, QE * i + f)
                    if last:
                        y_high(last, f)
                    if more and not ends(i, f):
                        tokens(q + 1, 1 - par, QE * i + f)
                    if f == 0:
                        weights(2, unit)
                    if f in (1, 2) and (more or i < QE - 1):
                        weights(f - 1, (q, par, i + 1) if i < QE - 1 else (q + 1, 1 - par, 0))
                u_high(unit, FC - 1)

            def tail(unit):
                places(unit)
                for t in range(TILES):
                    y_high(unit, t, last_banks[t % 2])

            for j in range(16):
                tokens(0, 0, j, first_banks[j % 4])
                if j in (7, 11):
                    weights((j - 7) // 4, (0, 0, 0))
            units(act, step, tail)

        @block.vector
        def _(dve):
            def low(out, in_, hi, scale):
                return dve.scalar_tensor_tensor(out=out, in0=in_, scalar=scale, in1=hi,
                                                op0=ALU.mult, op1=ALU.subtract)

            def weights(m, unit):
                n, i = lin(unit), unit[2]
                dve.wait_ge(w_hi[m], n + 1)
                low(parts[m][:, i % 2, LO, :, :], raw[m][:, :, :], parts[m][:, i % 2, HI, :, :],
                    W_UP).then_inc(w_lo[m], 1)

            def picks(q, par, b2):
                need(dve, s_place_ps_done, 4 * (q - 1))
                pos = keep["POS"][:, group_of(q), q % (E // QE), 2 * b2:2 * b2 + 2, :]
                dve.tensor_tensor(
                    pick[:, par, b2, :, :, :],
                    pos.rearrange("p b i -> p i b").unsqueeze(3).broadcast_to([P, QE, 2, TOP]),
                    keep["iota"][:, :].unsqueeze(1).unsqueeze(1).broadcast_to([P, QE, 2, TOP]),
                    ALU.is_equal).then_inc(s_pick_set, 1)

            def y_low(unit, t, src=Y_ps):
                n = 4 * lin(unit) + t
                dve.wait_ge(s_y_hi, n + 1)
                for b in range(2):
                    a = low(Y[rows(1 - b), t % 2, b, :], src[rows(b), 0:D], Y[rows(b), t % 2, b, :],
                            Y_DOWN / W_UP)
                a.then_inc(s_y_lo, 1)

            def add(unit, t):
                q, par, i = unit
                n = 4 * lin(unit) + t
                g = group_of(q)
                dve.wait_ge(s_sc_ps, n + 1)
                dve.wait_ge(s_acc_in, 16 * (g + 1))
                need(dve, s_acc_done, n - 3)
                for b in range(2):
                    tile = acc[:, g % 2, 2 * t + b, :]
                    a = dve.scalar_tensor_tensor(
                        out=tile, in0=S_ps[:, D * b:D * (b + 1)],
                        scalar=keep["WT"][:, g, q % (E // QE), i, 2 * t + b:2 * t + b + 1], in1=tile,
                        op0=ALU.mult, op1=ALU.add)
                a.then_inc(s_acc_done, 1)

            def step(unit, more):
                q, par, i = unit
                last, last2 = before(unit), before(before(unit))
                for f in range(FC):
                    n = 4 * lin(unit) + f
                    if f == 0 and more:
                        picks(q + 1, 1 - par, i)
                    dve.wait_ge(s_v_ps, n + 1)
                    dve.wait_ge(s_silu_done, n + 1)
                    need(dve, s_u_hi, n - 1)
                    need(dve, s_u_lo, n - 1)
                    dve.scalar_tensor_tensor(out=u32[:, f % 2, :], in0=V_ps[f % 2][:, :],
                                             scalar=1.0 / W_UP, in1=sg[:, f % 2, :], op0=ALU.mult,
                                             op1=ALU.mult).then_inc(s_u_done, 1)
                    if last:
                        y_low(last, f)
                    if f and last:
                        add(last, f - 1)
                    if f == 0 and last2:
                        add(last2, TILES - 1)
                    if f == 0:
                        weights(2, unit)
                    if f in (1, 2) and (more or i < QE - 1):
                        weights(f - 1, (q, par, i + 1) if i < QE - 1 else (q + 1, 1 - par, 0))

            def tail(unit):
                for t in range(TILES):
                    y_low(unit, t, last_banks[t % 2])
                    if t:
                        add(unit, t - 1)
                    else:
                        add(before(unit), TILES - 1)
                add(unit, TILES - 1)

            for b2 in range(4):
                picks(0, 0, b2)
            weights(0, (0, 0, 0))
            weights(1, (0, 0, 0))
            units(dve, step, tail)

        @block.gpsimd
        def _(pool):
            def step(unit, more):
                q, par, i = unit
                for f in range(FC):
                    n = 4 * lin(unit) + f
                    pool.wait_ge(s_u_hi, n + 1)
                    pool.tensor_tensor(U[:, i % 2, LO, f, :], u32[:, f % 2, :], U[:, i % 2, HI, f, :],
                                       ALU.subtract).then_inc(s_u_lo, 1)

            units(pool, step, lambda unit: None)


def flamingo_kernel(nc, io):
    NB, S, D = io["x"].shape
    E, _, F = io["w1"].shape
    dims = dict(NB=NB, D=D, E=E, F=F, RH=io["rw1"].shape[1])
    assert S == P and D == HEADS * HD and dims["RH"] == P and E * GB == P and NB % GB == 0
    with ExitStack() as ctx:
        keep = dict(
            H=ctx.enter_context(nc.sbuf_tensor("H", [P, NB, 2, D], F16)),
            POS=ctx.enter_context(nc.sbuf_tensor("POS", [P, NB // GB, E // QE, GB, QE], F16)),
            WT=ctx.enter_context(nc.sbuf_tensor("WT", [P, NB // GB, E // QE, QE, GB], F32)),
            ident16=ctx.enter_context(nc.sbuf_tensor("ident16", [P, P], F16)),
            iota=ctx.enter_context(nc.sbuf_tensor("iota", [P, TOP], F32)),
        )
        attention_phase(nc, io, keep, dims)
        expert_phase(nc, io, keep, dims)


_INS = {
    'x': 'x', 'ctx_1024': 'ctx', 'g_xattn': 'g_xattn', 'g_ffn': 'g_ffn',
    'L0_xattn_Wq': 'Wq', 'L0_xattn_bq': 'bq', 'L0_xattn_Wk': 'Wk', 'L0_xattn_bk': 'bk',
    'L0_xattn_Wv': 'Wv', 'L0_xattn_bv': 'bv', 'L0_xattn_Wo': 'Wo', 'L0_xattn_bo': 'bo',
    'L0_ffn_router_w1': 'rw1', 'L0_ffn_router_w2': 'rw2',
    'L0_ffn_w1': 'w1', 'L0_ffn_w2': 'w2', 'L0_ffn_w3': 'w3',
}


def _constants():
    import numpy as np
    inv_freq = (1.0 / 10000.0 ** (np.arange(0, HD, 2, dtype=np.float32) / HD)).astype(np.float32)
    freqs = np.arange(P, dtype=np.float32)[:, None] * inv_freq[None, :]
    cos, sin = np.cos(freqs), np.sin(freqs)
    q_scale = np.float32(-HD ** -0.5)
    table = np.concatenate([np.concatenate([a * q_scale, a], axis=1) for a in (
        np.concatenate([cos, cos], axis=1), np.concatenate([-sin, sin], axis=1))], axis=1)
    return {
        'ident': np.eye(P, dtype=np.float32),
        'rope': table.astype(np.float32),
        'iota': np.tile(np.arange(1, TOP + 1, dtype=np.float32), (P, 1)),
    }


def kernel(**inputs):
    import numpy as _np
    import concourse.bacc as _bacc
    from concourse import mybir as _mybir
    from concourse.bass_utils import run_bass_kernel_spmd as _run

    nc = _bacc.Bacc("TRN2", target_bir_lowering=False, num_devices=1)
    arrays, aps = {}, {}
    for name, short in _INS.items():
        arrays[f"in_{short}_dram"] = _np.ascontiguousarray(inputs[name])
    for short, a in _constants().items():
        arrays[f"in_{short}_dram"] = a
    for key, a in arrays.items():
        aps[key[3:-5]] = nc.dram_tensor(key, a.shape, _mybir.dt.from_np(a.dtype), kind="ExternalInput").ap()
    shape = arrays["in_x_dram"].shape
    aps["out"] = nc.dram_tensor("out_0_dram", shape, _mybir.dt.float32, kind="ExternalOutput").ap()
    flamingo_kernel(nc, aps)
    r = _run(nc, [arrays], core_ids=[0])
    return r.results[0]["out_0_dram"]
```
